# Optimizing a Trainium2 kernel written in Bass

```python
import numpy as np
import jax
import jax.numpy as jnp

def _softmax(x, axis=-1):
    return jax.nn.softmax(x, axis=axis)

def _gelu(x):
    return jax.nn.gelu(x, approximate=True)

def _silu(x):
    return jax.nn.silu(x)

def _sigmoid(x):
    return jax.nn.sigmoid(x)

def _layernorm(x, axis=-1, eps=1e-05):
    m = jnp.mean(x, axis=axis, keepdims=True)
    v = jnp.var(x, axis=axis, keepdims=True)
    return (x - m) / jnp.sqrt(v + eps)

def _scatter_add(tgt, idx, src, axis=0):
    return tgt.at[idx].add(src)

def _segment_sum(src, seg, n):
    return jax.ops.segment_sum(src, seg, n)
kernel_name = 'mk_gnn_resnorm_d2_gnn_r64_35e775'

def setup_inputs(seed: int=0):
    np.random.seed(seed)
    _w = jnp.asarray

    def _rec_inputs():
        import jax
        import jax.numpy as jnp
        _gk = jax.random.key(seed)
        x = -0.0002117 + 1 * jax.random.normal(jax.random.fold_in(_gk, 1), (100000, 256), jnp.float32)
        src = jax.random.randint(jax.random.fold_in(_gk, 2), (25000,), 0, 100000, jnp.int32)
        dst = jax.random.randint(jax.random.fold_in(_gk, 3), (25000,), 0, 100000, jnp.int32)
        _o = jnp.argsort(dst, stable=True)
        src = src[_o]
        dst = dst[_o]
        return (x, src, dst)
    x, src, dst = _rec_inputs()

    def _L0_gnn_setup():
        import jax, jax.numpy as jnp
        import numpy as np
        N_NODES = 100000
        N_EDGES = 25000
        D_IN = 256
        D_OUT = 256
        key = jax.random.key(seed)
        k1, k2, k3, k4 = jax.random.split(key, 4)
        x = jax.random.normal(k1, (N_NODES, D_IN), dtype=jnp.float32)
        edge_index = jax.random.randint(k2, (2, N_EDGES), 0, N_NODES, dtype=jnp.int64)
        W = jax.random.normal(k3, (D_OUT, D_IN), dtype=jnp.float32) * (1.0 / np.sqrt(D_IN))
        b = jax.random.normal(k4, (D_OUT,), dtype=jnp.float32) * 0.01
        return {'x': x, 'edge_index': edge_index, 'W': W, 'b': b}
    _L0_gnn_all = _L0_gnn_setup()
    _L0_gnn_in = {k: v for k, v in _L0_gnn_all.items() if k in ('W', 'b')}
    del _L0_gnn_all

    def _L1_gnn_setup():
        import jax, jax.numpy as jnp
        import numpy as np
        N = 100000
        E = 50000
        FIN = 256
        FOUT = 256
        K = 4
        key = jax.random.key(seed)
        k1, k2, k3 = jax.random.split(key, 3)
        x = jax.random.normal(k1, (N, FIN), dtype=jnp.float32)
        edge_index = jax.random.randint(k2, (2, E), 0, N, dtype=jnp.int32)
        stdv = 1.0 / np.sqrt(FIN * K)
        weights = jax.random.uniform(k3, (K, FIN, FOUT), dtype=jnp.float32, minval=-stdv, maxval=stdv)
        return {'x': x, 'edge_index': edge_index, 'weights': weights}
    _L1_gnn_all = _L1_gnn_setup()
    _L1_gnn_in = {k: v for k, v in _L1_gnn_all.items() if k in ('weights',)}
    del _L1_gnn_all
    return {'x': x, 'src': src, 'dst': dst, 'L0_gnn_W': _L0_gnn_in['W'], 'L0_gnn_b': _L0_gnn_in['b'], 'L1_gnn_weights': _L1_gnn_in['weights']}

def reference(x, src, dst, L0_gnn_W, L0_gnn_b, L1_gnn_weights):
    import jax
    import jax.numpy as jnp

    def _L0_gnn_ref(x, edge_index, W, b):
        import jax, jax.numpy as jnp
        import numpy as np
        N_NODES = 100000
        N_EDGES = 25000
        D_IN = 256
        D_OUT = 256
        h = jnp.einsum('nd,od->no', x, W) + b
        row, col = (edge_index[0], edge_index[1])
        msgs = h[col]
        out = jax.ops.segment_sum(msgs, row, num_segments=h.shape[0])
        return out

    def _L1_gnn_ref(x, edge_index, weights):
        import jax, jax.numpy as jnp
        import numpy as np
        N = 100000
        E = 50000
        FIN = 256
        FOUT = 256
        K = 4
        src, dst = (edge_index[0], edge_index[1])

        def spmm(z):
            out = jnp.zeros_like(z).at[dst].add(z[src])
            return out.at[src].add(z[dst])
        zs = [x]
        for _ in range(1, weights.shape[0]):
            x = spmm(x)
            zs.append(x)
        return jnp.einsum('knf,kfo->no', jnp.stack(zs), weights)
    edge_index = jnp.stack([src, dst])
    x = _layernorm(x + _L0_gnn_ref(x, edge_index, L0_gnn_W, L0_gnn_b), axis=-1)
    x = _layernorm(x + _L1_gnn_ref(x, edge_index, L1_gnn_weights), axis=-1)
    return x

_drawn_inputs = setup_inputs


def setup_inputs(seed=0):
    import zlib

    import numpy as np

    out = dict(_drawn_inputs(seed))
    spreads = {}
    factors = {'L0_gnn_b': 8.0}
    for name, (base, spread) in spreads.items():
        noise = np.random.default_rng([zlib.crc32(name.encode()), seed]).standard_normal(out[name].shape)
        drawn = base * np.exp(spread * noise) if base else spread * noise
        out[name] = jnp.asarray(drawn.astype(out[name].dtype))
    for name, factor in factors.items():
        out[name] = (out[name] * factor).astype(out[name].dtype)
    return out
```

```python
from contextlib import ExitStack

import concourse.bass as bass
from concourse import mybir

ALU = mybir.AluOpType
ACT = mybir.ActivationFunctionType
F32 = mybir.dt.float32
I32 = mybir.dt.int32

P = 128
EPS = 1e-5


def gnn_kernel(nc, x, src, dst, w0, b0, w1, out):
    N, D = x.shape
    E = src.shape[0]
    K = w1.shape[0]
    C = D // P
    G = 8
    NT = -(-(2 * E) // (P * G)) * G
    NB = NT // G
    A = 4
    PT = NT // A
    FREE = A * P
    LOGF = FREE.bit_length() - 1
    NSORT = P * FREE
    LOGN = NSORT.bit_length() - 1
    FLAG = float(1 << 17)
    PAD = float((1 << 17) - 1)
    SKIP = float(1 << 18)
    EP = 125
    EF = E // EP
    DR = 4 * P
    ND = -(-N // DR)
    DU = 2
    assert D == 256 and K == 4 and EP * EF == E and NT % (A * 1) == 0 and PT <= P
    assert 2 * E <= NT * P <= NSORT and N < PAD and ND == 2 * NB * DU and 2 * EF <= FREE

    with ExitStack() as ctx:
        def sb(name, shape, dt=F32):
            return ctx.enter_context(nc.sbuf_tensor(name, shape, dt))

        def psum(name):
            return ctx.enter_context(nc.psum_tensor(name, [P, 512], F32))

        def sem(name):
            return ctx.enter_context(nc.semaphore(name))

        def dram(name, shape):
            return nc.dram_tensor(name, shape, F32, kind="Internal").ap()

        keys_dram = dram("keys_dram", [P + NSORT + P])
        first_dram = dram("first_dram", [A, PT])
        x1t_dram = dram("x1t_dram", [NB, P, G * D])
        rows_dram = {k: dram(f"r{k}_dram", [NT * P, D]) for k in (3, 2, 1)}
        edge_dram = dram("edge_dram", [NT, 2, D])
        start_dram = nc.dram_tensor("start_dram", [NSORT, 1], I32, kind="Internal").ap()

        ident = sb("ident", [P, P])
        ones = sb("ones", [P, 1])
        eps = sb("eps", [P, 1])
        bias_bc = sb("bias_bc", [P, D])
        w0_in = sb("w0_in", [P, C, D])
        w0t = sb("w0t", [P, C, D])
        wk = sb("wk", [P, K, C, D])

        edge_i = sb("edge_i", [P, 2, FREE], I32)
        sort_a = sb("sort_a", [P, 3, FREE])
        sort_b = sb("sort_b", [P, 3, FREE])
        place_i = sb("place_i", [P, FREE], I32)
        place = sb("place", [P, FREE])
        swap = sb("swap", [P, FREE // 2], I32)
        signs = sb("signs", [P, LOGN - LOGF])
        sign_row = sb("sign_row", [P, LOGN - LOGF, P])

        kbefore = sb("kbefore", [P, FREE])
        kprev = kbefore[:, 0:FREE:P]
        kafter = sb("kafter", [P, A])
        flag_x = sb("flag_x", [P, FREE])
        partner_x = sb("partner_x", [P, FREE])
        begin_x = sb("begin_x", [P, FREE])
        whole_x = sb("whole_x", [P, FREE])
        start_x = sb("start_x", [P, FREE])
        own_id_x = sb("own_id_x", [P, FREE])
        zeros = sb("zeros", [P, FREE])
        carry_a = sb("carry_a", [P, P])
        carry_b = sb("carry_b", [P, P + 1])
        dest_x = sb("dest_x", [P, FREE])
        kcol = sb("kcol", [P, NT])
        flagcol = sb("flagcol", [P, NT])
        wholecol = sb("wholecol", [P, NT])
        index = sb("index", [P, NT + G, 7], I32)
        index_now = sb("index_now", [P, 2, G, 3], I32)
        count = sb("count", [P, NT])
        first_bc = sb("first_bc", [P, A, PT])
        seam_eq = sb("seam_eq", [P, A, A, PT])
        seam_a = sb("seam_a", [P, A])
        seam_b = sb("seam_b", [P, A])
        seam_d = sb("seam_d", [P, A])
        seam_stat = sb("seam_stat", [P, A, 6])
        seam_mv = sb("seam_mv", [P, A, 2])
        seam_rstd = sb("seam_rstd", [P, A])
        start_now = sb("start_now", [P, 2, G], I32)
        seam_dest = sb("seam_dest", [P, 2, A], I32)
        seam_node = sb("seam_node", [P, A], I32)

        got = sb("got", [P, G, D])
        own = sb("own", [P, G, D])
        key_bc = sb("key_bc", [P, G, P])
        eq = sb("eq", [P, G, P])
        agg = sb("agg", [P, G, D])
        x1 = sb("x1", [P, G, D])
        x1t = sb("x1t", [P, G, D])
        res = sb("res", [P, G, D])
        stat = sb("stat", [P, G, 6])
        mv = sb("mv", [P, G, 2])
        rstd = sb("rstd", [P, G])
        firsts_t = sb("firsts_t", [P, C, NT])
        lasts_t = sb("lasts_t", [P, C, NT])
        seam_last = sb("seam_last", [P, A, D])
        seam_first = sb("seam_first", [P, A, D])
        seam_cnt = sb("seam_cnt", [P, 2, A])
        seam_cn = sb("seam_cn", [P, A])
        seam_agg = sb("seam_agg", [P, C, A, PT])
        seam_own = sb("seam_own", [P, A, D])
        seam_x1 = sb("seam_x1", [P, A, D])
        seam_x1t = sb("seam_x1t", [P, A, C, PT])
        seam_res = sb("seam_res", [P, A, D])
        dx = sb("dx", [P, DU, 4, D])
        dx1 = sb("dx1", [P, DU, 4, D])
        dx1t = sb("dx1t", [P, DU, 4, D])
        dy = sb("dy", [P, DU, 4, D])
        dstat = sb("dstat", [P, DU, 2, 4, 6])
        dmv = sb("dmv", [P, DU, 2, 4, 2])
        drstd = sb("drstd", [P, DU, 2, 4])

        bank = [psum(f"bank{n}") for n in range(8)]

        edges_in = sem("edges_in")
        weights_in = sem("weights_in")
        const_set = sem("const_set")
        guard_set = sem("guard_set")
        signs_set = sem("signs_set")
        cleared = sem("cleared")
        w0_turned = sem("w0_turned")
        w0_copied = sem("w0_copied")
        signs_turned = sem("signs_turned")
        signs_copied = sem("signs_copied")
        sort_v = sem("sort_v")
        sort_turned = sem("sort_turned")
        sort_copied = sem("sort_copied")
        keys_out = sem("keys_out")
        keys_back = sem("keys_back")
        first_out = sem("first_out")
        first_back = sem("first_back")
        facts_v = sem("facts_v")
        place_set = sem("place_set")
        table_set = sem("table_set")
        carry_v = sem("carry_v")
        carry_turned = sem("carry_turned")
        facts_done = sem("facts_done")
        facts_turned = sem("facts_turned")
        index_done = sem("index_done")
        seam_facts = sem("seam_facts")
        seam_mask = sem("seam_mask")
        starts_kept = sem("starts_kept")
        idx_ready = sem("idx_ready")
        got_in = [sem(f"got_in{j}") for j in range(G)]
        own_in = [sem(f"own_in{j}") for j in range(G)]
        x1t_in = [sem(f"x1t_in{q}") for q in range(G // 2)]
        r_out = [sem(f"r_out{q}") for q in range(G // 2)]
        table_out = [sem(f"table_out{b}") for b in range(2)]
        start_in = [sem(f"start_in{b}") for b in range(2)]
        x1t_out = [sem(f"x1t_out{q}") for q in range(G // 2)]
        scattered = [sem(f"scattered{j}") for j in range(G)]
        edge_out = sem("edge_out")
        key_in = sem("key_in")
        eq_done = sem("eq_done")
        got_used = sem("got_used")
        agg_copied = sem("agg_copied")
        h_done = sem("h_done")
        cnt_done = sem("cnt_done")
        cnt_copied = sem("cnt_copied")
        x1_done = sem("x1_done")
        turned = sem("turned")
        x1t_copied = sem("x1t_copied")
        r_done = sem("r_done")
        r_copied = sem("r_copied")
        var_done = sem("var_done")
        std_done = sem("std_done")
        y_done = sem("y_done")
        ln0_v = sem("ln0_v")
        ln3_v = sem("ln3_v")
        dense_v = sem("dense_v")
        dx_in = [sem(f"dx_in{u}") for u in range(DU)]
        dy_out = [sem(f"dy_out{u}") for u in range(DU)]
        dvar = sem("dvar")
        dstd = sem("dstd")
        dx1_done = sem("dx1_done")
        dturned = sem("dturned")
        dx1t_copied = sem("dx1t_copied")
        dmul = sem("dmul")
        dadded = sem("dadded")
        dy_done = sem("dy_done")
        sm_in = sem("sm_in")
        sm_own = sem("sm_own")
        sm_rows = sem("sm_rows")
        sm_rows_c = sem("sm_rows_c")
        sm_sum = sem("sm_sum")
        sm_agg = sem("sm_agg")
        sm_h = sem("sm_h")
        sm_var = sem("sm_var")
        sm_std = sem("sm_std")
        sm_x1 = sem("sm_x1")
        sm_turned = sem("sm_turned")
        sm_x1t = sem("sm_x1t")
        sm_r = sem("sm_r")
        sm_res = sem("sm_res")
        sm_v = sem("sm_v")
        passed_v = sem("passed_v")
        passed_g = sem("passed_g")
        sm_out = sem("sm_out")

        class Steps:

            def __init__(self, eng, s, base=0):
                self.eng, self.s, self.base, self.n = eng, s, base, 0

            def did(self, ins):
                ins.then_inc(self.s, 1)
                self.n += 1

            def settle(self):
                self.eng.wait_ge(self.s, self.base + self.n)

        def col(t, a, j):
            return t[:, bass.ds(a + j, 1)]

        block = ctx.enter_context(nc.Block())

        def network():
            for k in range(1, LOGN + 1):
                if k < LOGN:
                    yield "flip", k
                if k > LOGF:
                    yield "turn", 0
                    for j in range(k - 1, LOGF - 1, -1):
                        yield "step", 1 << (j - LOGF)
                    yield "turn", 0
                for j in range(min(k, LOGF) - 1, -1, -1):
                    yield "step", 1 << j
                if k < LOGN:
                    yield "flip", k

        STEP_V, FLIP_V = 7, 1
        moves = sum(kind != "flip" for kind, _ in network())
        sort_out = (sort_a, sort_b)[moves % 2]
        SORT_V = sum({"step": STEP_V, "flip": FLIP_V, "turn": 0}[kind] for kind, _ in network()) + 5
        SORT_V0 = 5

        def dense_base(s, i, u):
            g = (s * NB + i) * DU + u
            if isinstance(g, int):
                return max(N - (ND - g) * DR, 0)
            return g * DR + (N - ND * DR)

        def dense_rows(t, s, i, u):
            return t[bass.ds(dense_base(s, i, u), DR), :].rearrange("(p g) d -> p (g d)", g=4)

        @block.sync
        def _(sp):
            HP = G // 2
            for h, (node, part) in enumerate(((src, dst), (dst, src))):
                for c, v in enumerate((node, part)):
                    sp.dma_start(edge_i[0:EP, c, h * EF:(h + 1) * EF],
                                 v.rearrange("(p f) -> p f", f=EF)).then_inc(edges_in, 16)
            sp.dma_start(w0_in[:, :, :], w0.rearrange("(c p) d -> p c d", p=P)).then_inc(weights_in, 16)
            sp.dma_start(wk[:, :, :, :], w1.rearrange("k (c p) o -> p k c o", p=P)).then_inc(weights_in, 16)
            sp.dma_start(bias_bc[:, :], b0.partition_broadcast(P)).then_inc(weights_in, 16)
            sp.wait_ge(guard_set, 1)
            sp.dma_start(keys_dram[0:P].rearrange("(a f) -> a f", a=1), kbefore[0:1, 0:P]).then_inc(keys_out, 16)
            sp.dma_start(keys_dram[P + NSORT:].rearrange("(a f) -> a f", a=1), kbefore[0:1, 0:P]).then_inc(keys_out, 16)
            sp.wait_ge(place_set, 1)
            sp.dma_start(start_dram.rearrange("(p f) a -> p (f a)", p=P), place_i[:, :]).then_inc(table_set, 16)
            sp.wait_ge(sort_v, SORT_V)
            sp.dma_start(keys_dram[P:P + NSORT].rearrange("(p f) -> p f", f=FREE),
                         sort_out[:, 0, :]).then_inc(keys_out, 16)
            sp.dma_start(first_dram.rearrange("a p -> p a"), sort_out[0:PT, 0, 0:FREE:P],
                         allow_slow_non_contiguous=True).then_inc(first_out, 16)
            sp.wait_ge(keys_out, 48)
            sp.dma_start(kbefore[:, :], keys_dram[P - 1:P - 1 + NSORT].rearrange("(p f) -> p f", f=FREE)).then_inc(keys_back, 16)
            sp.dma_start(kafter[:, :], keys_dram[2 * P:2 * P + NSORT]
                         .rearrange("(p a f) -> p a f", a=A, f=P)[:, :, 0], allow_slow_non_contiguous=True).then_inc(keys_back, 16)
            sp.wait_ge(first_out, 16)
            sp.dma_start(first_bc[:, :, :], first_dram.partition_broadcast(P)).then_inc(first_back, 16)

            def keys(gb, i):
                if not (isinstance(gb, int) and gb == 0):
                    sp.wait_ge(eq_done, G * gb)
                sp.dma_start(key_bc[:, :, :],
                             keys_dram[bass.ds(P + i * (G * P), G * P)].partition_broadcast(P)
                             ).then_inc(key_in, 16)

            def pair_rows(t, i, q):
                return t[bass.ds(i * (G * P) + 2 * q * P, 2 * P), :].rearrange("(t s) d -> s t d", s=P)

            def pair_x1t(i, q):
                return x1t_dram[bass.ds(i, 1), :, 2 * q * D:(2 * q + 2) * D].rearrange("a p f -> (a p) f")

            def store_x1t(i, q):
                sp.wait_ge(x1t_copied, HP * i + q + 1)
                sp.dma_start(pair_x1t(i, q), x1t[:, 2 * q:2 * q + 2, :]).then_inc(x1t_out[q], 16)

            def load_x1t(s, i, q):
                gb = s * NB + i
                if isinstance(gb, int) and gb == NB:
                    sp.wait_ge(x1_done, HP * NB)
                else:
                    sp.wait_ge(got_used, G * (gb - 1) + 2 * q + 2)
                sp.dma_start(own[:, 2 * q:2 * q + 2, :], pair_x1t(i, q)).then_inc(x1t_in[q], 16)

            def store_rows(s, i, q):
                sp.wait_ge(r_copied, HP * (s * NB + i) + q + 1)
                sp.dma_start(pair_rows(rows_dram[3 - s], i, q), res[:, 2 * q:2 * q + 2, :]).then_inc(r_out[q], 16)

            def store_edges(i):
                sp.wait_ge(r_copied, HP * (3 * NB + i + 1))
                for h, p in enumerate((0, P - 1)):
                    sp.dma_start(edge_dram[bass.ds(G * i, G), h, :].rearrange("(a g) d -> a g d", a=1),
                                 res[p:p + 1, :, :]).then_inc(edge_out, 16)

            def load_dense(r, i):
                m = r * NB + i
                for u in range(DU):
                    if not (isinstance(m, int) and m == 0):
                        sp.wait_ge(dx1_done, DU * (m - 1) + u + 1)
                    sp.dma_start(dx[:, u, :, :].rearrange("p g d -> p (g d)"), dense_rows(x, r, i, u)).then_inc(dx_in[u], 16)

            def store_dense(r, i):
                m = r * NB + i
                for u in range(DU):
                    sp.wait_ge(dy_done, DU * m + u + 1)
                    if isinstance(m, int) and m == 0 and u == 1:
                        sp.wait_ge(dy_out[0], 16)
                    sp.dma_start(dense_rows(out, r, i, u), dy[:, u, :, :].rearrange("p g d -> p (g d)")
                                 ).then_inc(dy_out[u], 16)

            load_dense(0, 0)
            load_dense(0, 1)
            store_dense(0, 0)
            with sp.Fori(1, NB - 1) as i:
                load_dense(0, i + 1)
                store_dense(0, i)
            load_dense(1, 0)
            store_dense(0, NB - 1)

            def first_stage(i, last=False):
                if not last:
                    keys(i + 1, i + 1)
                    load_dense(1, i + 1)
                else:
                    keys(NB, 0)
                for q in range(HP):
                    store_x1t(i, q)
                for q in range(HP):
                    store_rows(0, i, q)
                store_dense(1, i)

            keys(0, 0)
            with sp.Fori(0, NB - 1) as i:
                first_stage(i)
            first_stage(NB - 1, last=True)
            for q in range(HP):
                sp.wait_ge(x1t_out[q], 16 * NB)
            for q in range(HP):
                load_x1t(1, 0, q)

            def later_stage(s, i, last=False):
                if not last:
                    keys(s * NB + i + 1, i + 1)
                elif s < 3:
                    keys((s + 1) * NB, 0)
                for q in range(HP):
                    if not last:
                        load_x1t(s, i + 1, q)
                    elif s < 3:
                        load_x1t(s + 1, 0, q)
                    if s < 3:
                        store_rows(s, i, q)
                if s == 3:
                    store_edges(i)

            for s in (1, 2, 3):
                with sp.Fori(0, NB - 1) as i:
                    later_stage(s, i)
                later_stage(s, NB - 1, last=True)
                if s < 3:
                    for q in range(HP):
                        sp.wait_ge(r_out[q], 16 * NB * (s + 1))
                    ev = rows_dram[3 - s].rearrange("(p a s) d -> p a s d", a=A, s=P)
                    last_rows, first_rows = ev[:, :, P - 1, :], ev[:, :, 0, :]
                else:
                    sp.wait_ge(edge_out, 32 * NB)
                    ev = edge_dram.rearrange("(p a) h d -> p a h d", a=A)
                    last_rows, first_rows = ev[:, :, 1, :], ev[:, :, 0, :]
                sp.wait_ge(sm_res, s)
                sp.dma_start(seam_last[0:PT, :, :], last_rows).then_inc(sm_in, 16)
                sp.dma_start(seam_first[0:PT, :, :], first_rows).then_inc(sm_in, 16)
            sp.wait_ge(dy_out[0], 32 * NB)
            sp.wait_ge(dy_out[1], 32 * NB)
            for j in range(G):
                sp.wait_ge(scattered[j], 16 * NB)
            sp.wait_ge(sm_out, 16 * A * 4)

        @block.gpsimd
        def _(gp):
            gp.memset(ident[:, :], 0.0).then_inc(const_set, 1)
            gp.memset(ones[:, :], 1.0).then_inc(const_set, 1)
            gp.memset(eps[:, :], EPS).then_inc(const_set, 1)
            gp.iota(place_i[:, :], pattern=[[1, FREE]], base=0, channel_multiplier=FREE).then_inc(place_set, 1)
            gp.wait_ge(const_set, 3)
            gp.affine_select(out=ident[:, :], in_=ident[:, :], compare_op=ALU.not_equal, fill=1.0,
                             base=0, pattern=[[-1, P]], channel_multiplier=1).then_inc(const_set, 1)
            gp.wait_ge(seam_facts, 1)
            for a in range(A):
                gp.affine_select(out=seam_eq[0:PT, a, :, :], in_=seam_eq[0:PT, a, :, :], compare_op=ALU.is_gt,
                                 fill=0.0, base=-a, pattern=[[1, A], [A, PT]],
                                 channel_multiplier=-A).then_inc(seam_mask, 1)
            gp.wait_ge(index_done, 1)

            HP = G // 2
            row_bound = {"x": gp.to_reg(N - 1), "slot": gp.to_reg(NT * P - 1), "place": gp.to_reg(NSORT - 1)}

            def take(i, b, fields, nth):
                lo, hi = fields
                gp.tensor_copy(index_now[:, b, :, 0:hi - lo], index[:, bass.ds(G * i, G), lo:hi]).then_inc(idx_ready, 1)
                gp.wait_ge(idx_ready, nth)
                gp.sem_inc(passed_g, 1)

            def gather(dst, table, b, j, f, bound, s):
                gp.indirect_dma_start(dst, None, table, bass.IndirectOffsetOnAxis(index_now[:, b, j, f:f + 1], 0),
                                      bounds_check=row_bound[bound], oob_is_err=False).then_inc(s, 16)

            def seam_scatter(s):
                gp.wait_ge(sm_res, s + 1)
                if s < 3:
                    for q in range(HP):
                        gp.wait_ge(r_out[q], 16 * NB * (s + 1))
                table, h, bound = (out, 1, "x") if s == 3 else (rows_dram[3 - s], 0, "slot")
                for a in range(A):
                    gp.indirect_dma_start(table[:, :], bass.IndirectOffsetOnAxis(seam_dest[0:PT, h, a:a + 1], 0),
                                          seam_res[0:PT, a, :], None, bounds_check=row_bound[bound], oob_is_err=False
                                          ).then_inc(sm_out, 16)
                gp.wait_ge(sm_out, 16 * A * (s + 1))

            def tabulate(i, b, fresh):
                if not fresh:
                    gp.wait_ge(table_out[b], (i - b) * (8 * G))
                take(i, b, (0, 2), i + 1)
                for j in range(G):
                    gp.indirect_dma_start(start_dram[:, :], bass.IndirectOffsetOnAxis(index_now[:, b, j, 0:1], 0),
                                          index_now[:, b, j, 1:2], None, bounds_check=row_bound["place"], oob_is_err=False
                                          ).then_inc(table_out[b], 16)

            gp.wait_ge(table_set, 16)
            tabulate(0, 0, True)
            tabulate(1, 1, True)
            with gp.Fori(2, NB - 1, 2) as i:
                tabulate(i, 0, False)
                tabulate(i + 1, 1, False)
            tabulate(NB - 1, 0, False)
            gp.wait_ge(cleared, 1)
            for a in range(A):
                gp.indirect_dma_start(seam_own[0:PT, a, :], None, x[:, :],
                                      bass.IndirectOffsetOnAxis(seam_node[0:PT, a:a + 1], 0),
                                      bounds_check=row_bound["x"], oob_is_err=False).then_inc(sm_own, 16)
            gp.wait_ge(table_out[0], 16 * G * (NB // 2 + 1))
            gp.wait_ge(table_out[1], 16 * G * (NB // 2))

            def keep_starts(i, b):
                gp.wait_ge(start_in[b], (i - b) * (8 * G) + 16 * G)
                gp.tensor_copy(index[:, bass.ds(G * i, G), 5], start_now[:, b, :]).then_inc(starts_kept, 1)

            def first_stage(i, b, fresh, first):
                if not fresh:
                    keep_starts(i - 2, b)
                    gp.wait_ge(got_used, G * (i - 1))
                    gp.wait_ge(x1_done, HP * (i - 1))
                    gp.wait_ge(starts_kept, i - 1)
                take(i, b, (2, 5), i + (NB + 1))
                for j in range(G):
                    if not first:
                        gp.wait_ge(got_used, G * (i - 1) + j + 1)
                        gp.sem_inc(passed_g, 1)
                    gather(got[:, j, :], x[:, :], b, j, 0, "x", got_in[j])
                    if not first:
                        gp.wait_ge(x1_done, HP * (i - 1) + j // 2 + 1)
                        gp.sem_inc(passed_g, 1)
                    gather(own[:, j, :], x[:, :], b, j, 1, "x", own_in[j])
                    gather(start_now[:, b, j:j + 1], start_dram[:, :], b, j, 2, "place", start_in[b])

            first_stage(0, 0, True, True)
            first_stage(1, 1, True, False)
            with gp.Fori(2, NB - 1, 2) as i:
                first_stage(i, 0, False, False)
                first_stage(i + 1, 1, False, False)
            first_stage(NB - 1, 0, False, False)
            keep_starts(NB - 2, 1)
            keep_starts(NB - 1, 0)
            gp.wait_ge(starts_kept, NB)
            seam_scatter(0)

            def later_stage(s, i, b, wait_half, last=False, do_gather=True, do_scatter=False):
                gb = s * NB + i
                nth = 2 * NB + (s - 1) * NB
                if wait_half:
                    gp.wait_ge(got_used, G * (gb - 1))
                    if do_scatter:
                        if not isinstance(i, int) or i > 2:
                            for j in range(G):
                                gp.wait_ge(scattered[j], 16 * (i - 2))
                take(i, b, (5, 7), i + (nth + 1))
                for j in range(G):
                    if do_gather:
                        gp.wait_ge(got_used, G * (gb - 1) + j + 1)
                        gp.sem_inc(passed_g, 1)
                        gather(got[:, j, :], rows_dram[4 - s][:, :], b, j, 0, "slot", got_in[j])
                    if do_scatter:
                        gp.wait_ge(y_done, HP * (i - 1) + j // 2 + 1)
                        gp.sem_inc(passed_g, 1)
                        gp.indirect_dma_start(out[:, :], bass.IndirectOffsetOnAxis(index_now[:, b, j, 1:2], 0),
                                              x1[:, j, :], None, bounds_check=row_bound["x"], oob_is_err=False
                                              ).then_inc(scattered[j], 16)

            for s in (1, 2, 3):
                if s == 3:
                    for u in range(DU):
                        gp.wait_ge(dy_out[u], 32 * NB)
                sc = s == 3
                later_stage(s, 0, 0, False)
                later_stage(s, 1, 1, False, do_scatter=sc)
                later_stage(s, 2, 0, True, do_scatter=sc)
                with gp.Fori(3, NB, 2) as i:
                    later_stage(s, i, 1, True, do_scatter=sc)
                    later_stage(s, i + 1, 0, True, do_scatter=sc)
                if sc:
                    later_stage(s, NB, 1, True, do_gather=False, do_scatter=True)
                seam_scatter(s)

        @block.tensor
        def _(pe):
            pe.wait_ge(const_set, 4)
            pe.wait_ge(weights_in, 48)
            for c in range(C):
                for o in range(C):
                    mm = pe.transpose(bank[0][:, (c * C + o) * P:(c * C + o + 1) * P],
                                      w0_in[:, o, c * P:(c + 1) * P], ident[:, :])
            mm.then_inc(w0_turned, 1)
            pe.wait_ge(signs_set, 1)
            for n in range(LOGN - LOGF):
                mm = pe.transpose(bank[1 + n // 4][:, (n % 4) * P:(n % 4 + 1) * P], sign_row[:, n, :], ident[:, :])
            mm.then_inc(signs_turned, 1)
            pe.wait_ge(w0_copied, 1)
            pe.wait_ge(signs_copied, 2)
            nv, buf, other = SORT_V0, sort_a, sort_b
            for kind, _ in network():
                if kind == "turn":
                    pe.wait_ge(sort_v, nv)
                    for h in range(3):
                        for a in range(A):
                            mm = pe.transpose(bank[h][:, a * P:(a + 1) * P], buf[:, h, a * P:(a + 1) * P], ident[:, :])
                    mm.then_inc(sort_turned, 1)
                nv += {"step": STEP_V, "flip": FLIP_V, "turn": 0}[kind]
                if kind != "flip":
                    buf, other = other, buf
            pe.wait_ge(carry_v, 1)
            pe.transpose(bank[0][:, 0:P], carry_a[:, :], ident[:, :]).then_inc(carry_turned, 1)
            pe.wait_ge(carry_v, 2)
            pe.transpose(bank[1][:, 0:P], carry_b[:, 0:P], ident[:, :]).then_inc(carry_turned, 1)
            pe.wait_ge(facts_done, 1)
            for n, t in enumerate((sort_out[:, 0, :], flag_x, whole_x, partner_x, dest_x, sort_out[:, 1, :], own_id_x, start_x)):
                for a in range(A):
                    mm = pe.transpose(bank[n][:, a * P:(a + 1) * P], t[:, a * P:(a + 1) * P], ident[:, :])
            mm.then_inc(facts_turned, 1)
            pe.wait_ge(index_done, 1)

            HP = G // 2

            DENSE_BANK = (5, 6, 7, 5)

            def dense_turn(m, n, first=False):
                u, v = n // 2, n % 2
                if v == 0:
                    pe.wait_ge(dx1_done, DU * m + u + 1)
                if n == 3:
                    pe.wait_ge(dadded, 4 * m + 1)
                elif not first:
                    pe.wait_ge(dadded, 4 * (m - 1) + (4 if n == 0 else n + 1))
                for g in (2 * v, 2 * v + 1):
                    for c in range(C):
                        mm = pe.transpose(bank[DENSE_BANK[n]][:, ((g % 2) * C + c) * P:((g % 2) * C + c + 1) * P],
                                          dx1[:, u, g, c * P:(c + 1) * P], ident[:, :])
                mm.then_inc(dturned, 1)

            def dense_mul(m, n):
                u, v = n // 2, n % 2
                pe.wait_ge(dx1t_copied, 4 * m + n + 1)
                for g in (2 * v, 2 * v + 1):
                    for c in range(C):
                        mm = pe.matmul(bank[DENSE_BANK[n]][:, (g % 2) * D:(g % 2 + 1) * D],
                                       dx1t[:, u, g, c * P:(c + 1) * P], wk[:, 0, c, :], start=(c == 0), stop=(c == C - 1))
                mm.then_inc(dmul, 1)

            def first_stage(i, first):
                for q in range(HP):
                    if not first:
                        pe.wait_ge(r_copied, HP * (i - 1) + q + 1)
                    for j in (2 * q, 2 * q + 1):
                        pe.wait_ge(eq_done, G * i + j + 1)
                        pe.wait_ge(got_in[j], 16 * i + 16)
                        for c in range(C):
                            mm = pe.matmul(bank[q][:, ((j % 2) * C + c) * P:((j % 2) * C + c + 1) * P],
                                           got[:, j, c * P:(c + 1) * P], eq[:, j, :], start=True, stop=True)
                        mm.then_inc(got_used, 1)
                if not first:
                    pe.wait_ge(cnt_copied, i)
                for j in range(G):
                    mm = pe.matmul(bank[4][:, j:j + 1], eq[:, j, :], ones[:, :], start=True, stop=True)
                mm.then_inc(cnt_done, 1)
                m = i + NB
                for n in range(3):
                    dense_turn(m, n)
                for q in range(HP):
                    pe.wait_ge(agg_copied, 3 * (HP * i + q + 1))
                    for j in (2 * q, 2 * q + 1):
                        for c in range(C):
                            mm = pe.matmul(bank[q][:, (j % 2) * D:(j % 2 + 1) * D],
                                           agg[:, j, c * P:(c + 1) * P], w0t[:, c, :], start=(c == 0), stop=(c == C - 1))
                    mm.then_inc(h_done, 1)
                for n in range(2):
                    dense_mul(m, n)
                for q in range(HP):
                    pe.wait_ge(x1_done, HP * i + q + 1)
                    for j in (2 * q, 2 * q + 1):
                        for c in range(C):
                            mm = pe.transpose(bank[q][:, ((j % 2) * C + c) * P:((j % 2) * C + c + 1) * P],
                                              x1[:, j, c * P:(c + 1) * P], ident[:, :])
                    mm.then_inc(turned, 1)
                for q in range(HP):
                    pe.wait_ge(x1t_copied, HP * i + q + 1)
                    for j in (2 * q, 2 * q + 1):
                        for c in range(C):
                            mm = pe.matmul(bank[q][:, (j % 2) * D:(j % 2 + 1) * D],
                                           x1t[:, j, c * P:(c + 1) * P], wk[:, 3, c, :], start=(c == 0), stop=(c == C - 1))
                    mm.then_inc(r_done, 1)
                dense_turn(m, 3)
                dense_mul(m, 2)
                dense_mul(m, 3)

            def dense_only(m, first=False):
                for n in range(3):
                    dense_turn(m, n, first)
                dense_mul(m, 0)
                dense_mul(m, 1)
                dense_turn(m, 3)
                dense_mul(m, 2)
                dense_mul(m, 3)

            def slots(s, i, q):
                gb = s * NB + i
                pe.wait_ge(r_copied, HP * (gb - 1) + q + 1)
                pe.wait_ge(x1t_in[q], 16 * (gb - NB) + 16)
                for j in (2 * q, 2 * q + 1):
                    o = bank[q][:, (j % 2) * D:(j % 2 + 1) * D]
                    for c in range(C):
                        pe.matmul(o, own[:, j, c * P:(c + 1) * P], wk[:, 3 - s, c, :], start=(c == 0), stop=False)
                    if s == 3:
                        for c in range(C):
                            pe.matmul(bank[q][:, (j % 2) * D + c * P:(j % 2) * D + (c + 1) * P],
                                      own[:, j, c * P:(c + 1) * P], ident[:, :], start=False, stop=False,
                                      skip_group_check=True)
                    pe.wait_ge(eq_done, G * gb + j + 1)
                    pe.wait_ge(got_in[j], 16 * gb + 16)
                    mm = pe.matmul(o, eq[:, j, :], got[:, j, :], start=False, stop=True)
                    mm.then_inc(got_used, 1)

            def seam_first_stage():
                pe.wait_ge(agg_copied, 3 * NB * HP)
                pe.wait_ge(cnt_copied, NB)
                pe.wait_ge(r_copied, HP * NB)
                pe.wait_ge(dadded, 4 * 2 * NB)
                pe.wait_ge(seam_mask, A)
                for c in range(C):
                    for a in range(A):
                        pe.transpose(bank[c][0:PT, a * P:(a + 1) * P], lasts_t[:, c, a:NT:A], ident[:, :])
                for a in range(A):
                    mm = pe.transpose(bank[5][0:PT, a * P:(a + 1) * P], count[:, a:NT:A], ident[:, :])
                mm.then_inc(sm_rows, 1)
                pe.wait_ge(sm_rows_c, 4)
                for c in range(C):
                    for a in range(A):
                        pe.matmul(bank[2 + c][:, 0:A * PT], seam_last[0:PT, a, c * P:(c + 1) * P],
                                  seam_eq[0:PT, a, :, :].rearrange("p a q -> p (a q)"),
                                  start=(a == 0), stop=(a == A - 1))
                for b in range(A):
                    for a in range(A):
                        mm = pe.matmul(bank[4][0:PT, b:b + 1], seam_eq[0:PT, a, b, :],
                                       seam_cnt[0:PT, 1, a:a + 1], start=(a == 0), stop=(a == A - 1))
                mm.then_inc(sm_sum, 1)
                pe.wait_ge(sm_agg, C + 1)
                for a in range(A):
                    for c in range(C):
                        mm = pe.matmul(bank[a // 2][0:PT, (a % 2) * D:(a % 2 + 1) * D], seam_agg[:, c, a, :],
                                       w0t[:, c, :], start=(c == 0), stop=(c == C - 1))
                mm.then_inc(sm_h, 1)
                pe.wait_ge(sm_x1, 1)
                for a in range(A):
                    for c in range(C):
                        mm = pe.transpose(bank[2 + a // 2][:, ((a % 2) * C + c) * PT:((a % 2) * C + c + 1) * PT],
                                          seam_x1[0:PT, a, c * P:(c + 1) * P], ident[0:PT, 0:PT])
                mm.then_inc(sm_turned, 1)
                pe.wait_ge(sm_x1t, 2)
                for a in range(A):
                    for c in range(C):
                        mm = pe.matmul(bank[a // 2][0:PT, (a % 2) * D:(a % 2 + 1) * D], seam_x1t[:, a, c, :],
                                       wk[:, 3, c, :], start=(c == 0), stop=(c == C - 1))
                mm.then_inc(sm_r, 1)

            def seam(s):
                pe.wait_ge(r_copied, HP * NB * (s + 1))
                pe.wait_ge(sm_in, 32 * s)
                for a in range(A):
                    o = bank[a // 2][0:PT, (a % 2) * D:(a % 2 + 1) * D]
                    for c in range(C):
                        pe.matmul(o, seam_x1t[:, a, c, :], wk[:, 3 - s, c, :], start=(c == 0), stop=False)
                    for b in range(A):
                        mm = pe.matmul(o, seam_eq[0:PT, b, a, :], seam_last[0:PT, b, :], start=False, stop=(b == A - 1))
                mm.then_inc(sm_r, 1)

            dense_only(0, True)
            with pe.Fori(1, NB) as i:
                dense_only(i)
            first_stage(0, True)
            with pe.Fori(1, NB) as i:
                first_stage(i, False)
            seam_first_stage()
            for s in (1, 2, 3):
                pe.wait_ge(sm_res, s)
                with pe.Fori(0, NB) as i:
                    for q in range(HP):
                        slots(s, i, q)
                seam(s)

        @block.scalar
        def _(act):
            HP = G // 2
            act.wait_ge(w0_turned, 1)
            act.copy(w0t[:, :, :].rearrange("p c d -> p (c d)"), bank[0][:, :]).then_inc(w0_copied, 1)
            act.wait_ge(signs_turned, 1)
            act.copy(signs[:, 0:4], bank[1][:, 0:4 * P:P]).then_inc(signs_copied, 1)
            act.copy(signs[:, 4:LOGN - LOGF], bank[2][:, 0:(LOGN - LOGF - 4) * P:P]).then_inc(signs_copied, 1)
            nv, nturn, ncopy, buf, other = SORT_V0, 0, 0, sort_a, sort_b
            for kind, _ in network():
                if kind == "turn":
                    nturn += 1
                    act.wait_ge(sort_turned, nturn)
                    for h in range(3):
                        act.copy(other[:, h, :], bank[h][:, :]).then_inc(sort_copied, 1)
                    ncopy += 3
                elif kind == "step":
                    act.wait_ge(sort_v, nv)
                    act.wait_ge(sort_copied, ncopy)
                    act.copy(other[:, 1:3, :], buf[:, 1:3, :]).then_inc(sort_copied, 1)
                    ncopy += 1
                nv += {"step": STEP_V, "flip": FLIP_V, "turn": 0}[kind]
                if kind != "flip":
                    buf, other = other, buf

            def copy_pair(dst, q, w):
                act.copy(dst[:, 2 * q:2 * q + 2, :].rearrange("p g d -> p (g d)"), bank[q][:, :]).then_inc(w, 1)

            def first_stage(i, first):
                for q in range(HP):
                    act.wait_ge(got_used, G * i + 2 * q + 2)
                    if not first:
                        act.wait_ge(h_done, HP * (i - 1) + q + 1)
                    copy_pair(agg, q, agg_copied)
                    v = bank[q][:, :].rearrange("p (g c f) -> p c g f", g=2, c=C)
                    act.copy(firsts_t[:, :, bass.ds(G * i + 2 * q, 2)], v[:, :, :, 0]).then_inc(agg_copied, 1)
                    act.copy(lasts_t[:, :, bass.ds(G * i + 2 * q, 2)], v[:, :, :, P - 1]).then_inc(agg_copied, 1)
                act.wait_ge(cnt_done, i + 1)
                act.copy(count[:, bass.ds(G * i, G)], bank[4][:, 0:G]).then_inc(cnt_copied, 1)
                m = i + NB
                for u in range(DU):
                    dense_root(m, u, 0)
                for n in range(3):
                    dense_copy(m, n)
                for q in range(HP):
                    act.wait_ge(var_done, HP * i + q + 1)
                    act.activation(rstd[:, 2 * q:2 * q + 2], mv[:, 2 * q:2 * q + 2, 1], ACT.Sqrt, bias=eps[:, :]).then_inc(std_done, 1)
                for q in range(HP):
                    act.wait_ge(turned, HP * i + q + 1)
                    if not first:
                        act.wait_ge(x1t_out[q], 16 * i)
                    copy_pair(x1t, q, x1t_copied)
                for q in range(HP):
                    act.wait_ge(r_done, HP * i + q + 1)
                    if not first:
                        act.wait_ge(r_out[q], 16 * i)
                    copy_pair(res, q, r_copied)
                dense_copy(m, 3)
                for u in range(DU):
                    dense_root(m, u, 1)

            def rows(s, i, q):
                gb = s * NB + i
                act.wait_ge(got_used, G * gb + 2 * q + 2)
                if s < 3 or (isinstance(i, int) and i == 0):
                    act.wait_ge(r_out[q], 16 * gb)
                else:
                    act.wait_ge(y_done, HP * (i - 1) + q + 1)
                    act.wait_ge(edge_out, 32 * i)
                copy_pair(res, q, r_copied)

            def root(q, i):
                act.wait_ge(var_done, HP * NB + HP * i + q + 1)
                act.activation(rstd[:, 2 * q:2 * q + 2], mv[:, 2 * q:2 * q + 2, 1], ACT.Sqrt, bias=eps[:, :]).then_inc(std_done, 1)

            def dense_root(m, u, h):
                act.wait_ge(dvar, 2 * DU * m + DU * h + u + 1)
                act.activation(drstd[:, u, h, :], dmv[:, u, h, :, 1], ACT.Sqrt, bias=eps[:, :]).then_inc(dstd, 1)

            def dense_copy(m, n):
                u, v = n // 2, n % 2
                act.wait_ge(dturned, 4 * m + n + 1)
                act.copy(dx1t[:, u, 2 * v:2 * v + 2, :].rearrange("p g d -> p (g d)"), bank[(5, 6, 7, 5)[n]][:, :]).then_inc(dx1t_copied, 1)

            def seam_first_stage():
                act.wait_ge(sm_rows, 1)
                for c in range(C):
                    act.copy(seam_last[0:PT, :, c * P:(c + 1) * P],
                             bank[c][0:PT, :].rearrange("p (a f) -> p a f", a=A)).then_inc(sm_rows_c, 1)
                v = bank[5][0:PT, :].rearrange("p (a f) -> p a f", a=A)
                act.copy(seam_cnt[0:PT, 0, :], v[:, :, 0]).then_inc(sm_rows_c, 1)
                act.copy(seam_cnt[0:PT, 1, :], v[:, :, P - 1]).then_inc(sm_rows_c, 1)
                seam_root(0)
                act.wait_ge(sm_turned, 1)
                for h in range(2):
                    act.copy(seam_x1t[:, 2 * h:2 * h + 2, :, :].rearrange("p a c f -> p (a c f)"),
                             bank[2 + h][:, 0:2 * C * PT]).then_inc(sm_x1t, 1)
                act.wait_ge(sm_r, 1)
                act.copy(seam_res[0:PT, 0:2, :].rearrange("p a d -> p (a d)"), bank[0][0:PT, :])
                act.copy(seam_res[0:PT, 2:4, :].rearrange("p a d -> p (a d)"), bank[1][0:PT, :]).then_inc(sm_res, 1)

            def seam_root(n):
                act.wait_ge(sm_var, n + 1)
                act.activation(seam_rstd[0:PT, :], seam_mv[0:PT, :, 1], ACT.Sqrt, bias=eps[0:PT, :]).then_inc(sm_std, 1)

            def dense_only(m):
                for u in range(DU):
                    dense_root(m, u, 0)
                for n in range(4):
                    dense_copy(m, n)
                for u in range(DU):
                    dense_root(m, u, 1)

            with act.Fori(0, NB) as i:
                dense_only(i)
            first_stage(0, True)
            with act.Fori(1, NB) as i:
                first_stage(i, False)
            seam_first_stage()

            def later_stage(s, i):
                for q in range(HP):
                    rows(s, i, q)
                    if s == 3 and q > 0:
                        root(q - 1, i)
                if s == 3:
                    root(HP - 1, i)

            for s in (1, 2, 3):
                later_stage(s, 0)
                with act.Fori(1, NB) as i:
                    later_stage(s, i)
            seam_root(1)

        @block.vector
        def _(ve):
            HP = G // 2
            ve.memset(sign_row[:, :, :], 1.0).then_inc(facts_v, 1)
            ve.memset(sort_a[:, :, :], PAD).then_inc(facts_v, 1)
            ve.memset(kbefore[0:1, 0:P], -1.0).then_inc(guard_set, 1)
            ve.wait_ge(facts_v, 2)
            for n in range(LOGN - LOGF):
                v = sign_row[:, n, :].rearrange("p (b h j) -> p b h j", h=2, j=1 << n)
                ins = ve.memset(v[:, :, 1, :], -1.0)
            ins.then_inc(signs_set, 1)
            ve.memset(got[:, :, :], 0.0)
            ve.memset(own[:, :, :], 0.0)
            ve.memset(start_now[:, :, :], 0)
            ve.memset(seam_own[:, :, :], 0.0).then_inc(cleared, 1)
            ve.memset(index[:, :, :], int(SKIP)).then_inc(facts_v, 1)
            ve.memset(zeros[:, :], 0.0)
            ve.memset(carry_b[:, 0:1], 0.0)
            ve.wait_ge(edges_in, 64)
            sv = Steps(ve, sort_v)
            sv.did(ve.tensor_copy(sort_a[0:EP, 0, 0:2 * EF], edge_i[0:EP, 0, 0:2 * EF]))
            sv.did(ve.tensor_scalar(sort_a[0:EP, 2, 0:EF], edge_i[0:EP, 1, 0:EF], FLAG, None, ALU.add))
            sv.did(ve.tensor_copy(sort_a[0:EP, 2, EF:2 * EF], edge_i[0:EP, 1, EF:2 * EF]))
            ve.wait_ge(place_set, 1)
            sv.did(ve.tensor_scalar(sort_a[0:EP, 1, 0:EF], place_i[0:EP, 0:EF], float(EF), None, ALU.add))
            sv.did(ve.tensor_scalar(sort_a[0:EP, 1, EF:2 * EF], place_i[0:EP, EF:2 * EF], float(-EF), None, ALU.add))
            ve.wait_ge(signs_copied, 2)
            ncopy, buf, other = 0, sort_a, sort_b
            for kind, arg in network():
                sv.settle()
                if kind == "turn":
                    ncopy += 3
                elif kind == "flip":
                    ve.wait_ge(sort_copied, ncopy)
                    if arg < LOGF:
                        v = buf[:, 0, :].rearrange("p (b h j) -> p b h j", h=2, j=1 << arg)[:, :, 1, :]
                        sv.did(ve.tensor_scalar(v, v, -1.0, None, ALU.mult))
                    else:
                        sv.did(ve.tensor_scalar(buf[:, 0, :], buf[:, 0, :], signs[:, arg - LOGF:arg - LOGF + 1], None, ALU.mult))
                else:
                    ve.wait_ge(sort_copied, ncopy)
                    lo, hi = (buf[:, :, :].rearrange("p w (b h j) -> p w b h j", h=2, j=arg)[:, :, :, h, :] for h in range(2))
                    olo, ohi = (other[:, :, :].rearrange("p w (b h j) -> p w b h j", h=2, j=arg)[:, :, :, h, :] for h in range(2))
                    m = swap[:, :].rearrange("p (b j) -> p b j", j=arg)
                    sv.did(ve.tensor_tensor(m, lo[:, 0], hi[:, 0], ALU.is_gt))
                    sv.did(ve.tensor_tensor(olo[:, 0], lo[:, 0], hi[:, 0], ALU.min))
                    sv.did(ve.tensor_tensor(ohi[:, 0], lo[:, 0], hi[:, 0], ALU.max))
                    ncopy += 1
                    ve.wait_ge(sort_copied, ncopy)
                    sv.settle()
                    for w in (1, 2):
                        sv.did(ve.copy_predicated(olo[:, w], m, hi[:, w]))
                        sv.did(ve.copy_predicated(ohi[:, w], m, lo[:, w]))
                if kind != "flip":
                    buf, other = other, buf
            assert sv.n == SORT_V and buf is sort_out

            fv = Steps(ve, facts_v, 3)
            key, partner_id, pay = (sort_out[:, w, :] for w in range(3))
            sv.settle()
            fv.did(ve.tensor_scalar(flag_x[:, :], pay, FLAG, None, ALU.is_ge))
            fv.did(ve.tensor_scalar(own_id_x[:, :], partner_id, float(EF), None, ALU.add))
            fv.did(ve.tensor_copy(place[:, :], place_i[:, :]))
            fv.settle()
            fv.did(ve.scalar_tensor_tensor(partner_x[:, :], flag_x[:, :], -FLAG, pay, ALU.mult, ALU.add))
            fv.did(ve.scalar_tensor_tensor(own_id_x[:, :], flag_x[:, :], float(-2 * EF), own_id_x[:, :], ALU.mult, ALU.add))
            ve.wait_ge(keys_back, 32)
            fv.did(ve.tensor_tensor(begin_x[:, :], key, kbefore[:, :], ALU.not_equal))
            for a in range(A):
                sl = slice(a * P, (a + 1) * P)
                fv.did(ve.tensor_scalar(whole_x[:, sl], key[:, sl], kafter[:, a:a + 1], None, ALU.not_equal))
            fv.settle()
            fv.did(ve.tensor_tensor(whole_x[:, :], whole_x[:, :], begin_x[:, :], ALU.mult))
            fv.did(ve.tensor_tensor(start_x[:, :], begin_x[:, :], place[:, :], ALU.mult))
            fv.settle()
            fv.did(ve.tensor_tensor_scan(begin_x[:, :], zeros[:, :], start_x[:, :], 0.0, ALU.add, ALU.max))
            fv.settle()
            ve.tensor_scalar(carry_a[:, :], zeros[:, 0:P], begin_x[:, FREE - 1:FREE], None, ALU.add).then_inc(carry_v, 1)
            ve.wait_ge(carry_turned, 1)
            ve.tensor_tensor_scan(carry_b[:, 1:P + 1], zeros[:, 0:P], bank[0][:, 0:P], 0.0, ALU.add, ALU.max).then_inc(carry_v, 1)
            ve.wait_ge(carry_turned, 2)
            fv.did(ve.tensor_copy(carry_a[:, 0:1], bank[1][:, 0:1]))
            fv.settle()
            fv.did(ve.tensor_scalar(start_x[:, :], begin_x[:, :], carry_a[:, 0:1], None, ALU.max))
            fv.did(ve.tensor_scalar(dest_x[:, :], key, SKIP, None, ALU.add))
            fv.settle()
            ve.scalar_tensor_tensor(dest_x[:, :], whole_x[:, :], -SKIP, dest_x[:, :], ALU.mult, ALU.add
                                    ).then_inc(facts_done, 1)
            kf, kl = key[:, 0:FREE:P], key[:, P - 1:FREE:P]
            fv.did(ve.tensor_tensor(seam_a[:, :], kf, kprev, ALU.is_equal))
            fv.did(ve.tensor_tensor(seam_b[:, :], kf, kl, ALU.is_equal))
            fv.did(ve.tensor_tensor(seam_d[:, :], kf, kafter[:, :], ALU.is_equal))
            fv.settle()
            fv.did(ve.tensor_tensor(seam_b[:, :], seam_b[:, :], seam_d[:, :], ALU.mult))
            fv.settle()
            fv.did(ve.tensor_scalar(seam_b[:, :], seam_b[:, :], -1.0, 1.0, ALU.mult, ALU.add))
            fv.settle()
            fv.did(ve.tensor_tensor(seam_a[:, :], seam_a[:, :], seam_b[:, :], ALU.mult))
            fv.did(ve.tensor_scalar(seam_d[:, :], kf, SKIP, None, ALU.add))
            fv.settle()
            fv.did(ve.scalar_tensor_tensor(seam_dest[:, 1, :], seam_a[:, :], -SKIP, seam_d[:, :], ALU.mult, ALU.add))
            fv.settle()
            fv.did(ve.tensor_scalar(seam_d[:, :], start_x[:, 0:FREE:P], SKIP, None, ALU.add))
            fv.settle()
            fv.did(ve.scalar_tensor_tensor(seam_dest[:, 0, :], seam_a[:, :], -SKIP, seam_d[:, :], ALU.mult, ALU.add))
            fv.did(ve.tensor_copy(seam_node[:, :], kf))
            ve.wait_ge(first_back, 16)
            for a in range(A):
                ins = ve.tensor_scalar(seam_eq[0:PT, a, :, :], first_bc[0:PT, :, :], key[0:PT, a * P + P - 1:a * P + P], None, ALU.is_equal)
            ins.then_inc(seam_facts, 1)
            ve.wait_ge(facts_turned, 1)

            def by_tile(n):
                return bank[n][:, :].rearrange("s (a p) -> s p a", a=A)[:, 0:PT, :]

            def tiles(t):
                return t.rearrange("s (p a) -> s p a", a=A)

            ve.tensor_copy(tiles(kcol[:, :]), by_tile(0))
            ve.tensor_copy(tiles(flagcol[:, :]), by_tile(1))
            ve.tensor_copy(tiles(wholecol[:, :]), by_tile(2))
            for field, n in ((0, 6), (1, 7), (2, 3), (3, 0), (4, 5)):
                ve.tensor_copy(tiles(index[:, 0:NT, field]), by_tile(n))
            ve.tensor_copy(tiles(index[:, G:NT + G, 6]), by_tile(4)).then_inc(index_done, 1)
            ve.wait_ge(index_done, 1)

            def equal(gb, i, flagged, js=range(G)):
                for j in js:
                    if j == js[0]:
                        ve.wait_ge(key_in, 16 * gb + 16)
                    if not (isinstance(gb, int) and gb == 0):
                        ve.wait_ge(got_used, G * (gb - 1) + j + 1)
                    if flagged:
                        ve.tensor_scalar(eq[:, j, :], key_bc[:, j, :], kcol[:, bass.ds(G * i + j, 1)],
                                         flagcol[:, bass.ds(G * i + j, 1)], ALU.is_equal, ALU.mult).then_inc(eq_done, 1)
                    else:
                        ve.tensor_scalar(eq[:, j, :], key_bc[:, j, :], kcol[:, bass.ds(G * i + j, 1)],
                                         None, ALU.is_equal).then_inc(eq_done, 1)

            def plain_wait():
                ve.sem_inc(passed_v, 1)

            DENSE_V = 2 * DU * (4 + 1)

            def dense_stats(dv, t, u, h, m):
                for g in range(4):
                    dv.did(ve.bn_stats(dstat[:, u, h, g, :], t[:, u, g, :]))
                dv.settle()
                plain_wait()
                for g in range(4):
                    ins = ve.bn_aggr(dmv[:, u, h, g, :], dstat[:, u, h, g, :])
                ins.then_inc(dvar, 1)

            def dense_norm(dv, t, t_out, u, h, m):
                ve.wait_ge(dstd, 2 * DU * m + DU * h + u + 1)
                dv.did(ve.reciprocal(drstd[:, u, h, :], drstd[:, u, h, :]))
                dv.settle()
                for g in range(4):
                    ins = ve.tensor_scalar(t_out[:, u, g, :], t[:, u, g, :], dmv[:, u, h, g, 0:1], drstd[:, u, h, g:g + 1],
                                           ALU.subtract, ALU.mult)
                return ins

            def dense_add(dv, m, u, first):
                if not first:
                    ve.wait_ge(dy_out[u], 16 * m)
                for v in range(2):
                    ve.wait_ge(dmul, 2 * DU * m + 2 * u + v + 1)
                    ve.tensor_tensor(dy[:, u, 2 * v:2 * v + 2, :].rearrange("p g d -> p (g d)"),
                                     dx1[:, u, 2 * v:2 * v + 2, :].rearrange("p g d -> p (g d)"),
                                     bank[(5, 6, 7, 5)[2 * u + v]][:, :], ALU.add).then_inc(dadded, 1)
                ve.wait_ge(dadded, 4 * m + 2 * u + 2)
                dense_stats(dv, dy, u, 1, m)

            def dense_begin(m, first=False):
                dv = Steps(ve, dense_v, DENSE_V * m)
                for u in range(DU):
                    ve.wait_ge(dx_in[u], 16 * m + 16)
                    dense_stats(dv, dx, u, 0, m)
                for u in range(DU):
                    if not first:
                        ve.wait_ge(dturned, 4 * (m - 1) + 2 * u + 2)
                    dense_norm(dv, dx, dx1, u, 0, m).then_inc(dx1_done, 1)
                return dv

            def dense_end(dv, m, first=False):
                for u in range(DU):
                    dense_add(dv, m, u, first)
                for u in range(DU):
                    dense_norm(dv, dy, dy, u, 1, m).then_inc(dy_done, 1)
                assert dv.n == DENSE_V, dv.n

            dense_end(dense_begin(0, True), 0, True)
            with ve.Fori(1, NB) as i:
                dense_end(dense_begin(i), i)

            LN0 = G + HP * (1 + 2 + 1 + 1 + 1)

            def first_stage(i, first=False, last=False):
                st = Steps(ve, ln0_v, LN0 * i)
                ve.wait_ge(cnt_copied, i + 1)
                for j in range(G):
                    ve.wait_ge(own_in[j], 16 * i + 16)
                    st.did(ve.scalar_tensor_tensor(own[:, j, :], bias_bc[:, :], count[:, bass.ds(G * i + j, 1)],
                                                   own[:, j, :], ALU.mult, ALU.add))
                dv = dense_begin(i + NB)

                def stats(q):
                    st.settle()
                    ve.wait_ge(h_done, HP * i + q + 1)
                    if not first:
                        ve.wait_ge(turned, HP * (i - 1) + q + 1)
                    pair = slice(2 * q, 2 * q + 2)
                    st.did(ve.tensor_tensor(x1[:, pair, :].rearrange("p g d -> p (g d)"),
                                            own[:, pair, :].rearrange("p g d -> p (g d)"), bank[q][:, :], ALU.add))
                    st.settle()
                    for j in (2 * q, 2 * q + 1):
                        st.did(ve.bn_stats(stat[:, j, :], x1[:, j, :]))
                    st.settle()
                    plain_wait()
                    for j in (2 * q, 2 * q + 1):
                        ins = ve.bn_aggr(mv[:, j, :], stat[:, j, :])
                    ins.then_inc(var_done, 1)

                def norm(q):
                    ve.wait_ge(std_done, HP * i + q + 1)
                    pair = slice(2 * q, 2 * q + 2)
                    st.did(ve.reciprocal(rstd[:, pair], rstd[:, pair]))
                    st.settle()
                    st.did(ve.tensor_tensor(rstd[:, pair], rstd[:, pair], wholecol[:, bass.ds(G * i + 2 * q, 2)], ALU.mult))
                    st.settle()
                    for j in (2 * q, 2 * q + 1):
                        ins = ve.tensor_scalar(x1[:, j, :], x1[:, j, :], mv[:, j, 0:1], rstd[:, j:j + 1], ALU.subtract, ALU.mult)
                        if j % 2 == 0:
                            st.did(ins)
                    ins.then_inc(x1_done, 1)

                stats(0)
                for q in range(1, HP):
                    stats(q)
                    norm(q - 1)
                norm(HP - 1)
                ve.wait_ge(cnt_done, i + 1)
                if last:
                    equal(NB, 0, False)
                else:
                    equal(i + 1, i + 1, True)
                dense_end(dv, i + NB)
                return st

            equal(0, 0, True)
            st = first_stage(0, True)
            assert st.n == LN0, st.n
            with ve.Fori(1, NB - 1) as i:
                first_stage(i)
            first_stage(NB - 1, last=True)

            sm = Steps(ve, sm_v)

            def seam_norm(t_out, n):
                sm.settle()
                for a in range(A):
                    sm.did(ve.bn_stats(seam_stat[0:PT, a, :], t_out[0:PT, a, :]))
                sm.settle()
                for a in range(A):
                    ins = ve.bn_aggr(seam_mv[0:PT, a, :], seam_stat[0:PT, a, :])
                ins.then_inc(sm_var, 1)
                ve.wait_ge(sm_std, n + 1)
                sm.did(ve.reciprocal(seam_rstd[0:PT, :], seam_rstd[0:PT, :]))
                sm.settle()
                for a in range(A):
                    ins = ve.tensor_scalar(t_out[0:PT, a, :], t_out[0:PT, a, :], seam_mv[0:PT, a, 0:1],
                                           seam_rstd[0:PT, a:a + 1], ALU.subtract, ALU.mult)
                return ins

            ve.wait_ge(sm_sum, 1)
            for c in range(C):
                ve.tensor_tensor(seam_agg[:, c, :, :], bank[2 + c][:, 0:A * PT].rearrange("p (a q) -> p a q", a=A),
                                 firsts_t[:, c, :].rearrange("p (q a) -> p a q", a=A), ALU.add).then_inc(sm_agg, 1)
            ve.tensor_tensor(seam_cn[0:PT, :], bank[4][0:PT, 0:A], seam_cnt[0:PT, 0, :], ALU.add).then_inc(sm_agg, 1)
            ve.wait_ge(sm_agg, C + 1)
            ve.wait_ge(sm_own, 16 * A)
            for a in range(A):
                sm.did(ve.scalar_tensor_tensor(seam_own[0:PT, a, :], bias_bc[0:PT, :], seam_cn[0:PT, a:a + 1],
                                               seam_own[0:PT, a, :], ALU.mult, ALU.add))
            sm.settle()
            ve.wait_ge(sm_h, 1)
            for h in range(2):
                sm.did(ve.tensor_tensor(seam_x1[0:PT, 2 * h:2 * h + 2, :].rearrange("p a d -> p (a d)"),
                                        seam_own[0:PT, 2 * h:2 * h + 2, :].rearrange("p a d -> p (a d)"), bank[h][0:PT, :], ALU.add))
            seam_norm(seam_x1, 0).then_inc(sm_x1, 1)

            def seam(s):
                ve.wait_ge(sm_r, s + 1)
                ve.wait_ge(sm_in, 32 * s)
                ve.wait_ge(sm_out, 16 * A * s)
                for h in range(2):
                    ins = ve.tensor_tensor(seam_res[0:PT, 2 * h:2 * h + 2, :].rearrange("p a d -> p (a d)"),
                                           seam_first[0:PT, 2 * h:2 * h + 2, :].rearrange("p a d -> p (a d)"), bank[h][0:PT, :], ALU.add)
                    if s == 3:
                        sm.did(ins)
                if s == 3:
                    sm.settle()
                    for h in range(2):
                        sm.did(ve.tensor_tensor(seam_res[0:PT, 2 * h:2 * h + 2, :], seam_res[0:PT, 2 * h:2 * h + 2, :],
                                                seam_x1[0:PT, 2 * h:2 * h + 2, :], ALU.add))
                    ins = seam_norm(seam_res, 1)
                ins.then_inc(sm_res, 1)

            for s in (1, 2):
                with ve.Fori(0, NB - 1) as i:
                    equal(s * NB + 1 + i, i + 1, False)
                equal((s + 1) * NB, 0, False)
                seam(s)

            LN3 = G + HP
            def last_stage(i, last=False):
                st = Steps(ve, ln3_v, LN3 * i)

                def stats(q):
                    ve.wait_ge(r_copied, HP * (3 * NB + i) + q + 1)
                    for j in (2 * q, 2 * q + 1):
                        st.did(ve.bn_stats(stat[:, j, :], res[:, j, :]))
                    st.settle()
                    plain_wait()
                    for j in (2 * q, 2 * q + 1):
                        ins = ve.bn_aggr(mv[:, j, :], stat[:, j, :])
                    ins.then_inc(var_done, 1)

                def norm(q):
                    ve.wait_ge(std_done, HP * (NB + i) + q + 1)
                    pair = slice(2 * q, 2 * q + 2)
                    st.did(ve.reciprocal(rstd[:, pair], rstd[:, pair]))
                    st.settle()
                    for j in (2 * q, 2 * q + 1):
                        if not (isinstance(i, int) and i == 0):
                            ve.wait_ge(scattered[j], 16 * i)
                        ins = ve.tensor_scalar(x1[:, j, :], res[:, j, :], mv[:, j, 0:1], rstd[:, j:j + 1], ALU.subtract, ALU.mult)
                    ins.then_inc(y_done, 1)

                def eq_pair(q):
                    if not last:
                        equal(3 * NB + i + 1, i + 1, False, range(2 * q, 2 * q + 2))

                stats(0)
                for q in range(1, HP):
                    eq_pair(q - 1)
                    stats(q)
                    norm(q - 1)
                eq_pair(HP - 1)
                norm(HP - 1)
                assert st.n == LN3

            last_stage(0)
            with ve.Fori(1, NB - 1) as i:
                last_stage(i)
            last_stage(NB - 1, last=True)
            seam(3)


_INS = ["x", "src", "dst", "L0_gnn_W", "L0_gnn_b", "L1_gnn_weights"]
_OUTS = [((100000, 256), "float32")]


def kernel(**inputs):
    import numpy as _np
    import concourse.bacc as _bacc
    from concourse import mybir as _mybir
    from concourse.bass_utils import run_bass_kernel_spmd as _run

    nc = _bacc.Bacc("TRN2", target_bir_lowering=False, num_devices=1)
    arrays, args = {}, []
    for name in _INS:
        a = _np.ascontiguousarray(inputs[name])
        arrays[f"in_{name}_dram"] = a
        args.append(nc.dram_tensor(f"in_{name}_dram", a.shape, _mybir.dt.from_np(a.dtype), kind="ExternalInput").ap())
    for i, (shape, dtype) in enumerate(_OUTS):
        dt = _mybir.dt.from_np(_np.dtype(dtype))
        args.append(nc.dram_tensor(f"out_{i}_dram", shape, dt, kind="ExternalOutput").ap())
    gnn_kernel(nc, *args)
    r = _run(nc, [arrays], core_ids=[0])
    return r.results[0]["out_0_dram"]
```

```python
from contextlib import ExitStack

import concourse.bass as bass
from concourse import mybir

ALU = mybir.AluOpType
ACT = mybir.ActivationFunctionType
F32 = mybir.dt.float32
I32 = mybir.dt.int32

P = 128
EPS = 1e-5


def gnn_kernel(nc, x, src, dst, w0, b0, w1, out):
    N, D = x.shape
    E = src.shape[0]
    K = w1.shape[0]
    C = D // P
    G = 8
    NT = -(-(2 * E) // (P * G)) * G
    NB = NT // G
    A = 4
    PT = NT // A
    FREE = A * P
    LOGF = FREE.bit_length() - 1
    NSORT = P * FREE
    LOGN = NSORT.bit_length() - 1
    FLAG = float(1 << 17)
    PAD = float((1 << 17) - 1)
    SKIP = float(1 << 18)
    EP = 125
    EF = E // EP
    DR = 4 * P
    ND = -(-N // DR)
    DU = 2
    assert D == 256 and K == 4 and EP * EF == E and NT % (A * 1) == 0 and PT <= P
    assert 2 * E <= NT * P <= NSORT and N < PAD and ND == 2 * NB * DU and 2 * EF <= FREE

    with ExitStack() as ctx:
        def sb(name, shape, dt=F32):
            return ctx.enter_context(nc.sbuf_tensor(name, shape, dt))

        def psum(name):
            return ctx.enter_context(nc.psum_tensor(name, [P, 512], F32))

        def sem(name):
            return ctx.enter_context(nc.semaphore(name))

        def dram(name, shape):
            return nc.dram_tensor(name, shape, F32, kind="Internal").ap()

        keys_dram = dram("keys_dram", [P + NSORT + P])
        first_dram = dram("first_dram", [A, PT])
        x1t_dram = dram("x1t_dram", [NB, P, G * D])
        rows_dram = {k: dram(f"r{k}_dram", [NT * P, D]) for k in (3, 2, 1)}
        edge_dram = dram("edge_dram", [NT, 2, D])
        start_dram = nc.dram_tensor("start_dram", [NSORT, 1], I32, kind="Internal").ap()

        ident = sb("ident", [P, P])
        ones = sb("ones", [P, 1])
        eps = sb("eps", [P, 1])
        bias_bc = sb("bias_bc", [P, D])
        w0_in = sb("w0_in", [P, C, D])
        w0t = sb("w0t", [P, C, D])
        wk = sb("wk", [P, K, C, D])

        edge_i = sb("edge_i", [P, 2, FREE], I32)
        sort_a = sb("sort_a", [P, 3, FREE])
        sort_b = sb("sort_b", [P, 3, FREE])
        place_i = sb("place_i", [P, FREE], I32)
        place = sb("place", [P, FREE])
        swap = sb("swap", [P, FREE // 2], I32)
        signs = sb("signs", [P, LOGN - LOGF])
        sign_row = sb("sign_row", [P, LOGN - LOGF, P])

        kbefore = sb("kbefore", [P, FREE])
        kprev = kbefore[:, 0:FREE:P]
        kafter = sb("kafter", [P, A])
        flag_x = sb("flag_x", [P, FREE])
        partner_x = sb("partner_x", [P, FREE])
        begin_x = sb("begin_x", [P, FREE])
        whole_x = sb("whole_x", [P, FREE])
        start_x = sb("start_x", [P, FREE])
        own_id_x = sb("own_id_x", [P, FREE])
        zeros = sb("zeros", [P, FREE])
        carry_a = sb("carry_a", [P, P])
        carry_b = sb("carry_b", [P, P + 1])
        dest_x = sb("dest_x", [P, FREE])
        kcol = sb("kcol", [P, NT])
        flagcol = sb("flagcol", [P, NT])
        wholecol = sb("wholecol", [P, NT])
        index = sb("index", [P, NT + G, 7], I32)
        index_now = sb("index_now", [P, 2, G, 3], I32)
        count = sb("count", [P, NT])
        first_bc = sb("first_bc", [P, A, PT])
        seam_eq = sb("seam_eq", [P, A, A, PT])
        seam_a = sb("seam_a", [P, A])
        seam_b = sb("seam_b", [P, A])
        seam_d = sb("seam_d", [P, A])
        seam_stat = sb("seam_stat", [P, A, 6])
        seam_mv = sb("seam_mv", [P, A, 2])
        seam_rstd = sb("seam_rstd", [P, A])
        start_now = sb("start_now", [P, 2, G], I32)
        seam_dest = sb("seam_dest", [P, 2, A], I32)
        seam_node = sb("seam_node", [P, A], I32)

        got = sb("got", [P, G, D])
        own = sb("own", [P, G, D])
        key_bc = sb("key_bc", [P, G, P])
        eq = sb("eq", [P, G, P])
        agg = sb("agg", [P, G, D])
        x1 = sb("x1", [P, G, D])
        x1t = sb("x1t", [P, G, D])
        res = sb("res", [P, G, D])
        stat = sb("stat", [P, G, 6])
        mv = sb("mv", [P, G, 2])
        rstd = sb("rstd", [P, G])
        firsts_t = sb("firsts_t", [P, C, NT])
        lasts_t = sb("lasts_t", [P, C, NT])
        seam_last = sb("seam_last", [P, A, D])
        seam_first = sb("seam_first", [P, A, D])
        seam_cnt = sb("seam_cnt", [P, 2, A])
        seam_cn = sb("seam_cn", [P, A])
        seam_agg = sb("seam_agg", [P, C, A, PT])
        seam_own = sb("seam_own", [P, A, D])
        seam_x1 = sb("seam_x1", [P, A, D])
        seam_x1t = sb("seam_x1t", [P, A, C, PT])
        seam_res = sb("seam_res", [P, A, D])
        dx = sb("dx", [P, DU, 4, D])
        dx1 = sb("dx1", [P, DU, 4, D])
        dx1t = sb("dx1t", [P, DU, 4, D])
        dy = sb("dy", [P, DU, 4, D])
        dstat = sb("dstat", [P, DU, 2, 4, 6])
        dmv = sb("dmv", [P, DU, 2, 4, 2])
        drstd = sb("drstd", [P, DU, 2, 4])
        dshift = sb("dshift", [P, DU, 2, 4])

        bank = [psum(f"bank{n}") for n in range(8)]

        edges_in = sem("edges_in")
        weights_in = sem("weights_in")
        const_set = sem("const_set")
        guard_set = sem("guard_set")
        signs_set = sem("signs_set")
        cleared = sem("cleared")
        w0_turned = sem("w0_turned")
        w0_copied = sem("w0_copied")
        signs_turned = sem("signs_turned")
        signs_copied = sem("signs_copied")
        sort_v = sem("sort_v")
        sort_turned = sem("sort_turned")
        sort_copied = sem("sort_copied")
        keys_out = sem("keys_out")
        keys_back = sem("keys_back")
        first_out = sem("first_out")
        first_back = sem("first_back")
        facts_v = sem("facts_v")
        place_set = sem("place_set")
        table_set = sem("table_set")
        carry_v = sem("carry_v")
        carry_turned = sem("carry_turned")
        facts_done = sem("facts_done")
        facts_turned = sem("facts_turned")
        index_done = sem("index_done")
        seam_facts = sem("seam_facts")
        seam_mask = sem("seam_mask")
        starts_kept = sem("starts_kept")
        idx_ready = sem("idx_ready")
        got_in = [sem(f"got_in{j}") for j in range(G)]
        own_in = [sem(f"own_in{j}") for j in range(G)]
        x1t_in = [sem(f"x1t_in{q}") for q in range(G // 2)]
        r_out = [sem(f"r_out{q}") for q in range(G // 2)]
        table_out = [sem(f"table_out{b}") for b in range(2)]
        start_in = [sem(f"start_in{b}") for b in range(2)]
        x1t_out = [sem(f"x1t_out{q}") for q in range(G // 2)]
        scattered = [sem(f"scattered{j}") for j in range(G)]
        edge_out = sem("edge_out")
        key_in = sem("key_in")
        eq_done = sem("eq_done")
        got_used = sem("got_used")
        agg_copied = sem("agg_copied")
        h_done = sem("h_done")
        cnt_done = sem("cnt_done")
        cnt_copied = sem("cnt_copied")
        x1_done = sem("x1_done")
        turned = sem("turned")
        x1t_copied = sem("x1t_copied")
        r_done = sem("r_done")
        r_copied = sem("r_copied")
        var_done = sem("var_done")
        std_done = sem("std_done")
        y_done = sem("y_done")
        ln0_v = sem("ln0_v")
        ln3_v = sem("ln3_v")
        dense_v = [[sem(f"dense_v{h}{u}") for u in range(DU)] for h in range(2)]
        dx_in = [sem(f"dx_in{u}") for u in range(DU)]
        dy_out = [sem(f"dy_out{u}") for u in range(DU)]
        dvar = [sem(f"dvar{h}") for h in range(2)]
        dstd = [sem(f"dstd{h}") for h in range(2)]
        dscale = [sem(f"dscale{h}") for h in range(2)]
        dx1_done = sem("dx1_done")
        dturned = sem("dturned")
        dx1t_copied = sem("dx1t_copied")
        dmul = sem("dmul")
        dadded = sem("dadded")
        dy_done = sem("dy_done")
        sm_in = sem("sm_in")
        sm_own = sem("sm_own")
        sm_rows = sem("sm_rows")
        sm_rows_c = sem("sm_rows_c")
        sm_sum = sem("sm_sum")
        sm_agg = sem("sm_agg")
        sm_h = sem("sm_h")
        sm_var = sem("sm_var")
        sm_std = sem("sm_std")
        sm_x1 = sem("sm_x1")
        sm_turned = sem("sm_turned")
        sm_x1t = sem("sm_x1t")
        sm_r = sem("sm_r")
        sm_res = sem("sm_res")
        sm_v = sem("sm_v")
        passed_v = sem("passed_v")
        passed_g = sem("passed_g")
        sm_out = sem("sm_out")

        class Steps:

            def __init__(self, eng, s, base=0):
                self.eng, self.s, self.base, self.n = eng, s, base, 0

            def did(self, ins):
                ins.then_inc(self.s, 1)
                self.n += 1

            def settle(self):
                self.eng.wait_ge(self.s, self.base + self.n)

        def col(t, a, j):
            return t[:, bass.ds(a + j, 1)]

        block = ctx.enter_context(nc.Block())

        def network():
            for k in range(1, LOGN + 1):
                if k < LOGN:
                    yield "flip", k
                if k > LOGF:
                    yield "turn", 0
                    for j in range(k - 1, LOGF - 1, -1):
                        yield "step", 1 << (j - LOGF)
                    yield "turn", 0
                for j in range(min(k, LOGF) - 1, -1, -1):
                    yield "step", 1 << j
                if k < LOGN:
                    yield "flip", k

        STEP_V, FLIP_V = 7, 1
        moves = sum(kind != "flip" for kind, _ in network())
        sort_out = (sort_a, sort_b)[moves % 2]
        SORT_V = sum({"step": STEP_V, "flip": FLIP_V, "turn": 0}[kind] for kind, _ in network()) + 5
        SORT_V0 = 5

        def dense_base(m, u):
            g = m * DU + u
            if isinstance(g, int):
                return max(N - (ND - g) * DR, 0)
            return g * DR + (N - ND * DR)

        def dense_rows(t, m, u):
            return t[bass.ds(dense_base(m, u), DR), :].rearrange("(p g) d -> p (g d)", g=4)

        @block.sync
        def _(sp):
            HP = G // 2
            for h, (node, part) in enumerate(((src, dst), (dst, src))):
                for c, v in enumerate((node, part)):
                    sp.dma_start(edge_i[0:EP, c, h * EF:(h + 1) * EF],
                                 v.rearrange("(p f) -> p f", f=EF)).then_inc(edges_in, 16)
            sp.dma_start(w0_in[:, :, :], w0.rearrange("(c p) d -> p c d", p=P)).then_inc(weights_in, 16)
            sp.dma_start(wk[:, :, :, :], w1.rearrange("k (c p) o -> p k c o", p=P)).then_inc(weights_in, 16)
            sp.dma_start(bias_bc[:, :], b0.partition_broadcast(P)).then_inc(weights_in, 16)
            sp.wait_ge(guard_set, 1)
            sp.dma_start(keys_dram[0:P].rearrange("(a f) -> a f", a=1), kbefore[0:1, 0:P]).then_inc(keys_out, 16)
            sp.dma_start(keys_dram[P + NSORT:].rearrange("(a f) -> a f", a=1), kbefore[0:1, 0:P]).then_inc(keys_out, 16)
            sp.wait_ge(place_set, 1)
            sp.dma_start(start_dram.rearrange("(p f) a -> p (f a)", p=P), place_i[:, :]).then_inc(table_set, 16)
            sp.wait_ge(sort_v, SORT_V)
            sp.dma_start(keys_dram[P:P + NSORT].rearrange("(p f) -> p f", f=FREE),
                         sort_out[:, 0, :]).then_inc(keys_out, 16)
            sp.dma_start(first_dram.rearrange("a p -> p a"), sort_out[0:PT, 0, 0:FREE:P],
                         allow_slow_non_contiguous=True).then_inc(first_out, 16)
            sp.wait_ge(keys_out, 48)
            sp.dma_start(kbefore[:, :], keys_dram[P - 1:P - 1 + NSORT].rearrange("(p f) -> p f", f=FREE)).then_inc(keys_back, 16)
            sp.dma_start(kafter[:, :], keys_dram[2 * P:2 * P + NSORT]
                         .rearrange("(p a f) -> p a f", a=A, f=P)[:, :, 0], allow_slow_non_contiguous=True).then_inc(keys_back, 16)
            sp.wait_ge(first_out, 16)
            sp.dma_start(first_bc[:, :, :], first_dram.partition_broadcast(P)).then_inc(first_back, 16)

            def keys(gb, i):
                if not (isinstance(gb, int) and gb == 0):
                    sp.wait_ge(eq_done, G * gb)
                sp.dma_start(key_bc[:, :, :],
                             keys_dram[bass.ds(P + i * (G * P), G * P)].partition_broadcast(P)
                             ).then_inc(key_in, 16)

            def pair_rows(t, i, q):
                return t[bass.ds(i * (G * P) + 2 * q * P, 2 * P), :].rearrange("(t s) d -> s t d", s=P)

            def pair_x1t(i, q):
                return x1t_dram[bass.ds(i, 1), :, 2 * q * D:(2 * q + 2) * D].rearrange("a p f -> (a p) f")

            def store_x1t(i, q):
                sp.wait_ge(x1t_copied, HP * i + q + 1)
                sp.dma_start(pair_x1t(i, q), x1t[:, 2 * q:2 * q + 2, :]).then_inc(x1t_out[q], 16)

            def load_x1t(s, i, q):
                gb = s * NB + i
                if isinstance(gb, int) and gb == NB:
                    sp.wait_ge(x1_done, HP * NB)
                else:
                    sp.wait_ge(got_used, G * (gb - 1) + 2 * q + 2)
                sp.dma_start(own[:, 2 * q:2 * q + 2, :], pair_x1t(i, q)).then_inc(x1t_in[q], 16)

            def store_rows(s, i, q):
                sp.wait_ge(r_copied, HP * (s * NB + i) + q + 1)
                sp.dma_start(pair_rows(rows_dram[3 - s], i, q), res[:, 2 * q:2 * q + 2, :]).then_inc(r_out[q], 16)

            def store_edges(i):
                sp.wait_ge(r_copied, HP * (3 * NB + i + 1))
                for h, p in enumerate((0, P - 1)):
                    sp.dma_start(edge_dram[bass.ds(G * i, G), h, :].rearrange("(a g) d -> a g d", a=1),
                                 res[p:p + 1, :, :]).then_inc(edge_out, 16)

            def load_dense(m, u):
                if not (isinstance(m, int) and m == 0):
                    sp.wait_ge(dx1_done, DU * (m - 1) + u + 1)
                sp.dma_start(dx[:, u, :, :].rearrange("p g d -> p (g d)"), dense_rows(x, m, u)).then_inc(dx_in[u], 16)

            def store_dense(m, u):
                sp.wait_ge(dy_done, DU * m + u + 1)
                if isinstance(m, int) and m == 0 and u == 1:
                    sp.wait_ge(dy_out[0], 16)
                sp.dma_start(dense_rows(out, m, u), dy[:, u, :, :].rearrange("p g d -> p (g d)")
                             ).then_inc(dy_out[u], 16)

            for m in range(2):
                for u in range(DU):
                    load_dense(m, u)
            for u in range(DU):
                store_dense(0, u)
                load_dense(2, u)
            with sp.Fori(1, NB - 1) as i:
                for u in range(DU):
                    store_dense(i, u)
                    load_dense(i + 2, u)
            store_dense(NB - 1, 0)
            load_dense(NB + 1, 0)

            def first_stage(i, left):
                m = i + NB
                keys(i + 1, 0 if left == 0 else i + 1)
                store_dense(m - 1, 1)
                if left > 0:
                    load_dense(m + 1, 1)
                for q in range(HP):
                    store_x1t(i, q)
                store_rows(0, i, 0)
                store_rows(0, i, 1)
                store_dense(m, 0)
                store_rows(0, i, 2)
                if left > 1:
                    load_dense(m + 2, 0)
                store_rows(0, i, 3)

            keys(0, 0)
            with sp.Fori(0, NB - 2) as i:
                first_stage(i, 2)
            first_stage(NB - 2, 1)
            first_stage(NB - 1, 0)
            store_dense(2 * NB - 1, 1)
            for q in range(HP):
                sp.wait_ge(x1t_out[q], 16 * NB)
            for q in range(HP):
                load_x1t(1, 0, q)

            def later_stage(s, i, last=False):
                if not last:
                    keys(s * NB + i + 1, i + 1)
                elif s < 3:
                    keys((s + 1) * NB, 0)
                for q in range(HP):
                    if not last:
                        load_x1t(s, i + 1, q)
                    elif s < 3:
                        load_x1t(s + 1, 0, q)
                    if s < 3:
                        store_rows(s, i, q)
                if s == 3:
                    store_edges(i)

            for s in (1, 2, 3):
                with sp.Fori(0, NB - 1) as i:
                    later_stage(s, i)
                later_stage(s, NB - 1, last=True)
                if s < 3:
                    for q in range(HP):
                        sp.wait_ge(r_out[q], 16 * NB * (s + 1))
                    ev = rows_dram[3 - s].rearrange("(p a s) d -> p a s d", a=A, s=P)
                    last_rows, first_rows = ev[:, :, P - 1, :], ev[:, :, 0, :]
                else:
                    sp.wait_ge(edge_out, 32 * NB)
                    ev = edge_dram.rearrange("(p a) h d -> p a h d", a=A)
                    last_rows, first_rows = ev[:, :, 1, :], ev[:, :, 0, :]
                sp.wait_ge(sm_res, s)
                sp.dma_start(seam_last[0:PT, :, :], last_rows).then_inc(sm_in, 16)
                sp.dma_start(seam_first[0:PT, :, :], first_rows).then_inc(sm_in, 16)
            sp.wait_ge(dy_out[0], 32 * NB)
            sp.wait_ge(dy_out[1], 32 * NB)
            for j in range(G):
                sp.wait_ge(scattered[j], 16 * NB)
            sp.wait_ge(sm_out, 16 * A * 4)

        @block.gpsimd
        def _(gp):
            gp.memset(ident[:, :], 0.0).then_inc(const_set, 1)
            gp.memset(ones[:, :], 1.0).then_inc(const_set, 1)
            gp.memset(eps[:, :], EPS).then_inc(const_set, 1)
            gp.iota(place_i[:, :], pattern=[[1, FREE]], base=0, channel_multiplier=FREE).then_inc(place_set, 1)
            gp.wait_ge(const_set, 3)
            gp.affine_select(out=ident[:, :], in_=ident[:, :], compare_op=ALU.not_equal, fill=1.0,
                             base=0, pattern=[[-1, P]], channel_multiplier=1).then_inc(const_set, 1)
            gp.wait_ge(seam_facts, 1)
            for a in range(A):
                gp.affine_select(out=seam_eq[0:PT, a, :, :], in_=seam_eq[0:PT, a, :, :], compare_op=ALU.is_gt,
                                 fill=0.0, base=-a, pattern=[[1, A], [A, PT]],
                                 channel_multiplier=-A).then_inc(seam_mask, 1)
            gp.wait_ge(index_done, 1)

            HP = G // 2
            row_bound = {"x": gp.to_reg(N - 1), "slot": gp.to_reg(NT * P - 1), "place": gp.to_reg(NSORT - 1)}

            def take(i, b, fields, nth):
                lo, hi = fields
                gp.tensor_copy(index_now[:, b, :, 0:hi - lo], index[:, bass.ds(G * i, G), lo:hi]).then_inc(idx_ready, 1)
                gp.wait_ge(idx_ready, nth)
                gp.sem_inc(passed_g, 1)

            def gather(dst, table, b, j, f, bound, s):
                gp.indirect_dma_start(dst, None, table, bass.IndirectOffsetOnAxis(index_now[:, b, j, f:f + 1], 0),
                                      bounds_check=row_bound[bound], oob_is_err=False).then_inc(s, 16)

            def seam_scatter(s):
                gp.wait_ge(sm_res, s + 1)
                if s < 3:
                    for q in range(HP):
                        gp.wait_ge(r_out[q], 16 * NB * (s + 1))
                table, h, bound = (out, 1, "x") if s == 3 else (rows_dram[3 - s], 0, "slot")
                for a in range(A):
                    gp.indirect_dma_start(table[:, :], bass.IndirectOffsetOnAxis(seam_dest[0:PT, h, a:a + 1], 0),
                                          seam_res[0:PT, a, :], None, bounds_check=row_bound[bound], oob_is_err=False
                                          ).then_inc(sm_out, 16)
                gp.wait_ge(sm_out, 16 * A * (s + 1))

            def tabulate(i, b, fresh):
                if not fresh:
                    gp.wait_ge(table_out[b], (i - b) * (8 * G))
                take(i, b, (0, 2), i + 1)
                for j in range(G):
                    gp.indirect_dma_start(start_dram[:, :], bass.IndirectOffsetOnAxis(index_now[:, b, j, 0:1], 0),
                                          index_now[:, b, j, 1:2], None, bounds_check=row_bound["place"], oob_is_err=False
                                          ).then_inc(table_out[b], 16)

            gp.wait_ge(table_set, 16)
            tabulate(0, 0, True)
            tabulate(1, 1, True)
            with gp.Fori(2, NB - 1, 2) as i:
                tabulate(i, 0, False)
                tabulate(i + 1, 1, False)
            tabulate(NB - 1, 0, False)
            gp.wait_ge(cleared, 1)
            for a in range(A):
                gp.indirect_dma_start(seam_own[0:PT, a, :], None, x[:, :],
                                      bass.IndirectOffsetOnAxis(seam_node[0:PT, a:a + 1], 0),
                                      bounds_check=row_bound["x"], oob_is_err=False).then_inc(sm_own, 16)
            gp.wait_ge(table_out[0], 16 * G * (NB // 2 + 1))
            gp.wait_ge(table_out[1], 16 * G * (NB // 2))

            def keep_starts(i, b):
                gp.wait_ge(start_in[b], (i - b) * (8 * G) + 16 * G)
                gp.tensor_copy(index[:, bass.ds(G * i, G), 5], start_now[:, b, :]).then_inc(starts_kept, 1)

            def first_stage(i, b, fresh, first):
                if not fresh:
                    keep_starts(i - 2, b)
                    gp.wait_ge(got_used, G * (i - 1))
                    gp.wait_ge(x1_done, HP * (i - 1))
                    gp.wait_ge(starts_kept, i - 1)
                take(i, b, (2, 5), i + (NB + 1))

                def starts(js):
                    for j in js:
                        gather(start_now[:, b, j:j + 1], start_dram[:, :], b, j, 2, "place", start_in[b])

                for j in range(G):
                    if not first:
                        gp.wait_ge(got_used, G * (i - 1) + j + 1)
                        gp.sem_inc(passed_g, 1)
                    gather(got[:, j, :], x[:, :], b, j, 0, "x", got_in[j])
                starts(range(0, G // 2))
                for j in range(G):
                    if not first and j % 2 == 0:
                        gp.wait_ge(x1_done, HP * (i - 1) + j // 2 + 1)
                        gp.sem_inc(passed_g, 1)
                    gather(own[:, j, :], x[:, :], b, j, 1, "x", own_in[j])
                starts(range(G // 2, G))

            first_stage(0, 0, True, True)
            first_stage(1, 1, True, False)
            with gp.Fori(2, NB - 1, 2) as i:
                first_stage(i, 0, False, False)
                first_stage(i + 1, 1, False, False)
            first_stage(NB - 1, 0, False, False)
            keep_starts(NB - 2, 1)
            keep_starts(NB - 1, 0)
            gp.wait_ge(starts_kept, NB)
            seam_scatter(0)

            def later_stage(s, i, b, wait_half, last=False, do_gather=True, do_scatter=False):
                gb = s * NB + i
                nth = 2 * NB + (s - 1) * NB
                if wait_half:
                    gp.wait_ge(got_used, G * (gb - 1))
                    if do_scatter:
                        if not isinstance(i, int) or i > 2:
                            for j in range(G):
                                gp.wait_ge(scattered[j], 16 * (i - 2))
                take(i, b, (5, 7), i + (nth + 1))
                for j in range(G):
                    if do_gather:
                        gp.wait_ge(got_used, G * (gb - 1) + j + 1)
                        gp.sem_inc(passed_g, 1)
                        gather(got[:, j, :], rows_dram[4 - s][:, :], b, j, 0, "slot", got_in[j])
                    if do_scatter:
                        gp.wait_ge(y_done, HP * (i - 1) + j // 2 + 1)
                        gp.sem_inc(passed_g, 1)
                        gp.indirect_dma_start(out[:, :], bass.IndirectOffsetOnAxis(index_now[:, b, j, 1:2], 0),
                                              x1[:, j, :], None, bounds_check=row_bound["x"], oob_is_err=False
                                              ).then_inc(scattered[j], 16)

            for s in (1, 2, 3):
                if s == 3:
                    for u in range(DU):
                        gp.wait_ge(dy_out[u], 32 * NB)
                sc = s == 3
                later_stage(s, 0, 0, False)
                later_stage(s, 1, 1, False, do_scatter=sc)
                later_stage(s, 2, 0, True, do_scatter=sc)
                with gp.Fori(3, NB, 2) as i:
                    later_stage(s, i, 1, True, do_scatter=sc)
                    later_stage(s, i + 1, 0, True, do_scatter=sc)
                if sc:
                    later_stage(s, NB, 1, True, do_gather=False, do_scatter=True)
                seam_scatter(s)

        @block.tensor
        def _(pe):
            pe.wait_ge(const_set, 4)
            pe.wait_ge(weights_in, 48)
            for c in range(C):
                for o in range(C):
                    mm = pe.transpose(bank[0][:, (c * C + o) * P:(c * C + o + 1) * P],
                                      w0_in[:, o, c * P:(c + 1) * P], ident[:, :])
            mm.then_inc(w0_turned, 1)
            pe.wait_ge(signs_set, 1)
            for n in range(LOGN - LOGF):
                mm = pe.transpose(bank[1 + n // 4][:, (n % 4) * P:(n % 4 + 1) * P], sign_row[:, n, :], ident[:, :])
            mm.then_inc(signs_turned, 1)
            pe.wait_ge(w0_copied, 1)
            pe.wait_ge(signs_copied, 2)
            nv, buf, other = SORT_V0, sort_a, sort_b
            for kind, _ in network():
                if kind == "turn":
                    pe.wait_ge(sort_v, nv)
                    for h in range(3):
                        for a in range(A):
                            mm = pe.transpose(bank[h][:, a * P:(a + 1) * P], buf[:, h, a * P:(a + 1) * P], ident[:, :])
                    mm.then_inc(sort_turned, 1)
                nv += {"step": STEP_V, "flip": FLIP_V, "turn": 0}[kind]
                if kind != "flip":
                    buf, other = other, buf
            pe.wait_ge(carry_v, 1)
            pe.transpose(bank[0][:, 0:P], carry_a[:, :], ident[:, :]).then_inc(carry_turned, 1)
            pe.wait_ge(carry_v, 2)
            pe.transpose(bank[1][:, 0:P], carry_b[:, 0:P], ident[:, :]).then_inc(carry_turned, 1)
            pe.wait_ge(facts_done, 1)
            for n, t in enumerate((sort_out[:, 0, :], flag_x, whole_x, partner_x, dest_x, sort_out[:, 1, :], own_id_x, start_x)):
                for a in range(A):
                    mm = pe.transpose(bank[n][:, a * P:(a + 1) * P], t[:, a * P:(a + 1) * P], ident[:, :])
            mm.then_inc(facts_turned, 1)
            pe.wait_ge(index_done, 1)

            HP = G // 2

            def dense_bank(alone, n):
                return bank[(5, 6, 7, 4 if alone else 5)[n]]

            def dense_turn(m, n, alone=False, first=False):
                u, v = n // 2, n % 2
                if v == 0:
                    pe.wait_ge(dx1_done, DU * m + u + 1)
                if n == 3 and not alone:
                    pe.wait_ge(dadded, 4 * m + 1)
                elif not first:
                    pe.wait_ge(dadded, 4 * (m - 1) + (4 if n == 0 and not alone else n + 1))
                for g in (2 * v, 2 * v + 1):
                    for c in range(C):
                        mm = pe.transpose(dense_bank(alone, n)[:, ((g % 2) * C + c) * P:((g % 2) * C + c + 1) * P],
                                          dx1[:, u, g, c * P:(c + 1) * P], ident[:, :])
                mm.then_inc(dturned, 1)

            def dense_mul(m, n, alone=False):
                u, v = n // 2, n % 2
                pe.wait_ge(dx1t_copied, 4 * m + n + 1)
                for g in (2 * v, 2 * v + 1):
                    for c in range(C):
                        mm = pe.matmul(dense_bank(alone, n)[:, (g % 2) * D:(g % 2 + 1) * D],
                                       dx1t[:, u, g, c * P:(c + 1) * P], wk[:, 0, c, :], start=(c == 0), stop=(c == C - 1))
                mm.then_inc(dmul, 1)

            def first_stage(i, first):
                for q in range(HP):
                    if not first:
                        pe.wait_ge(r_copied, HP * (i - 1) + q + 1)
                    for j in (2 * q, 2 * q + 1):
                        pe.wait_ge(eq_done, G * i + j + 1)
                        pe.wait_ge(got_in[j], 16 * i + 16)
                        for c in range(C):
                            mm = pe.matmul(bank[q][:, ((j % 2) * C + c) * P:((j % 2) * C + c + 1) * P],
                                           got[:, j, c * P:(c + 1) * P], eq[:, j, :], start=True, stop=True)
                        mm.then_inc(got_used, 1)
                if first:
                    pe.wait_ge(dadded, 4 * NB)
                else:
                    pe.wait_ge(cnt_copied, i)
                for j in range(G):
                    mm = pe.matmul(bank[4][:, j:j + 1], eq[:, j, :], ones[:, :], start=True, stop=True)
                mm.then_inc(cnt_done, 1)
                m = i + NB
                dense_turn(m, 0)
                dense_turn(m, 1)
                for q in range(HP):
                    pe.wait_ge(agg_copied, 3 * (HP * i + q + 1))
                    for j in (2 * q, 2 * q + 1):
                        for c in range(C):
                            mm = pe.matmul(bank[q][:, (j % 2) * D:(j % 2 + 1) * D],
                                           agg[:, j, c * P:(c + 1) * P], w0t[:, c, :], start=(c == 0), stop=(c == C - 1))
                    mm.then_inc(h_done, 1)
                dense_turn(m, 2)
                for n in range(3):
                    dense_mul(m, n)
                for q in range(HP):
                    pe.wait_ge(x1_done, HP * i + q + 1)
                    for j in (2 * q, 2 * q + 1):
                        for c in range(C):
                            mm = pe.transpose(bank[q][:, ((j % 2) * C + c) * P:((j % 2) * C + c + 1) * P],
                                              x1[:, j, c * P:(c + 1) * P], ident[:, :])
                    mm.then_inc(turned, 1)
                for q in range(HP):
                    pe.wait_ge(x1t_copied, HP * i + q + 1)
                    for j in (2 * q, 2 * q + 1):
                        for c in range(C):
                            mm = pe.matmul(bank[q][:, (j % 2) * D:(j % 2 + 1) * D],
                                           x1t[:, j, c * P:(c + 1) * P], wk[:, 3, c, :], start=(c == 0), stop=(c == C - 1))
                    mm.then_inc(r_done, 1)
                    if q == 0:
                        dense_turn(m, 3)
                    elif q == 1:
                        dense_mul(m, 3)

            def dense_only(m, first=False):
                for u in range(DU):
                    for n in (2 * u, 2 * u + 1):
                        dense_turn(m, n, True, first)
                    for n in (2 * u, 2 * u + 1):
                        dense_mul(m, n, True)

            def slots(s, i, q):
                gb = s * NB + i
                pe.wait_ge(r_copied, HP * (gb - 1) + q + 1)
                pe.wait_ge(x1t_in[q], 16 * (gb - NB) + 16)
                for j in (2 * q, 2 * q + 1):
                    o = bank[q][:, (j % 2) * D:(j % 2 + 1) * D]
                    for c in range(C):
                        pe.matmul(o, own[:, j, c * P:(c + 1) * P], wk[:, 3 - s, c, :], start=(c == 0), stop=False)
                    if s == 3:
                        for c in range(C):
                            pe.matmul(bank[q][:, (j % 2) * D + c * P:(j % 2) * D + (c + 1) * P],
                                      own[:, j, c * P:(c + 1) * P], ident[:, :], start=False, stop=False,
                                      skip_group_check=True)
                    pe.wait_ge(eq_done, G * gb + j + 1)
                    pe.wait_ge(got_in[j], 16 * gb + 16)
                    mm = pe.matmul(o, eq[:, j, :], got[:, j, :], start=False, stop=True)
                    mm.then_inc(got_used, 1)

            def seam_first_stage():
                pe.wait_ge(agg_copied, 3 * NB * HP)
                pe.wait_ge(cnt_copied, NB)
                pe.wait_ge(r_copied, HP * NB)
                pe.wait_ge(dadded, 4 * 2 * NB)
                pe.wait_ge(seam_mask, A)
                for c in range(C):
                    for a in range(A):
                        pe.transpose(bank[c][0:PT, a * P:(a + 1) * P], lasts_t[:, c, a:NT:A], ident[:, :])
                for a in range(A):
                    mm = pe.transpose(bank[5][0:PT, a * P:(a + 1) * P], count[:, a:NT:A], ident[:, :])
                mm.then_inc(sm_rows, 1)
                pe.wait_ge(sm_rows_c, 4)
                for c in range(C):
                    for a in range(A):
                        pe.matmul(bank[2 + c][:, 0:A * PT], seam_last[0:PT, a, c * P:(c + 1) * P],
                                  seam_eq[0:PT, a, :, :].rearrange("p a q -> p (a q)"),
                                  start=(a == 0), stop=(a == A - 1))
                for b in range(A):
                    for a in range(A):
                        mm = pe.matmul(bank[4][0:PT, b:b + 1], seam_eq[0:PT, a, b, :],
                                       seam_cnt[0:PT, 1, a:a + 1], start=(a == 0), stop=(a == A - 1))
                mm.then_inc(sm_sum, 1)
                pe.wait_ge(sm_agg, C + 1)
                for a in range(A):
                    for c in range(C):
                        mm = pe.matmul(bank[a // 2][0:PT, (a % 2) * D:(a % 2 + 1) * D], seam_agg[:, c, a, :],
                                       w0t[:, c, :], start=(c == 0), stop=(c == C - 1))
                mm.then_inc(sm_h, 1)
                pe.wait_ge(sm_x1, 1)
                for a in range(A):
                    for c in range(C):
                        mm = pe.transpose(bank[2 + a // 2][:, ((a % 2) * C + c) * PT:((a % 2) * C + c + 1) * PT],
                                          seam_x1[0:PT, a, c * P:(c + 1) * P], ident[0:PT, 0:PT])
                mm.then_inc(sm_turned, 1)
                pe.wait_ge(sm_x1t, 2)
                for a in range(A):
                    for c in range(C):
                        mm = pe.matmul(bank[a // 2][0:PT, (a % 2) * D:(a % 2 + 1) * D], seam_x1t[:, a, c, :],
                                       wk[:, 3, c, :], start=(c == 0), stop=(c == C - 1))
                mm.then_inc(sm_r, 1)

            def seam(s):
                pe.wait_ge(r_copied, HP * NB * (s + 1))
                pe.wait_ge(sm_in, 32 * s)
                for a in range(A):
                    o = bank[a // 2][0:PT, (a % 2) * D:(a % 2 + 1) * D]
                    for c in range(C):
                        pe.matmul(o, seam_x1t[:, a, c, :], wk[:, 3 - s, c, :], start=(c == 0), stop=False)
                    for b in range(A):
                        mm = pe.matmul(o, seam_eq[0:PT, b, a, :], seam_last[0:PT, b, :], start=False, stop=(b == A - 1))
                mm.then_inc(sm_r, 1)

            dense_only(0, True)
            with pe.Fori(1, NB) as i:
                dense_only(i)
            first_stage(0, True)
            with pe.Fori(1, NB) as i:
                first_stage(i, False)
            seam_first_stage()
            for s in (1, 2, 3):
                pe.wait_ge(sm_res, s)
                with pe.Fori(0, NB) as i:
                    for q in range(HP):
                        slots(s, i, q)
                seam(s)

        @block.scalar
        def _(act):
            HP = G // 2
            act.wait_ge(w0_turned, 1)
            act.copy(w0t[:, :, :].rearrange("p c d -> p (c d)"), bank[0][:, :]).then_inc(w0_copied, 1)
            act.wait_ge(signs_turned, 1)
            act.copy(signs[:, 0:4], bank[1][:, 0:4 * P:P]).then_inc(signs_copied, 1)
            act.copy(signs[:, 4:LOGN - LOGF], bank[2][:, 0:(LOGN - LOGF - 4) * P:P]).then_inc(signs_copied, 1)
            nv, nturn, ncopy, buf, other = SORT_V0, 0, 0, sort_a, sort_b
            for kind, _ in network():
                if kind == "turn":
                    nturn += 1
                    act.wait_ge(sort_turned, nturn)
                    for h in range(3):
                        act.copy(other[:, h, :], bank[h][:, :]).then_inc(sort_copied, 1)
                    ncopy += 3
                elif kind == "step":
                    act.wait_ge(sort_v, nv)
                    act.wait_ge(sort_copied, ncopy)
                    act.copy(other[:, 1:3, :], buf[:, 1:3, :]).then_inc(sort_copied, 1)
                    ncopy += 1
                nv += {"step": STEP_V, "flip": FLIP_V, "turn": 0}[kind]
                if kind != "flip":
                    buf, other = other, buf

            def copy_pair(dst, q, w):
                act.copy(dst[:, 2 * q:2 * q + 2, :].rearrange("p g d -> p (g d)"), bank[q][:, :]).then_inc(w, 1)

            def first_stage(i, first=False, last=False):
                for q in range(HP):
                    act.wait_ge(got_used, G * i + 2 * q + 2)
                    if not first:
                        act.wait_ge(h_done, HP * (i - 1) + q + 1)
                    copy_pair(agg, q, agg_copied)
                    v = bank[q][:, :].rearrange("p (g c f) -> p c g f", g=2, c=C)
                    act.copy(firsts_t[:, :, bass.ds(G * i + 2 * q, 2)], v[:, :, :, 0]).then_inc(agg_copied, 1)
                    act.copy(lasts_t[:, :, bass.ds(G * i + 2 * q, 2)], v[:, :, :, P - 1]).then_inc(agg_copied, 1)
                act.wait_ge(cnt_done, i + 1)
                act.copy(count[:, bass.ds(G * i, G)], bank[4][:, 0:G]).then_inc(cnt_copied, 1)
                m = i + NB
                dense_copy(m, 0)
                dense_copy(m, 1)
                for q in range(HP):
                    if q == 0:
                        dense_apply(m - 1, 1, 1)
                    elif q == 1:
                        dense_apply(m, 0, 1)
                    elif q == 2:
                        dense_copy(m, 2)
                    act.wait_ge(var_done, HP * i + q + 1)
                    act.activation(rstd[:, 2 * q:2 * q + 2], mv[:, 2 * q:2 * q + 2, 1], ACT.Sqrt, bias=eps[:, :]).then_inc(std_done, 1)
                for q in range(HP):
                    act.wait_ge(turned, HP * i + q + 1)
                    if not first:
                        act.wait_ge(x1t_out[q], 16 * i)
                    copy_pair(x1t, q, x1t_copied)
                dense_root(m, 1, 0)
                for q in range(HP):
                    act.wait_ge(r_done, HP * i + q + 1)
                    if not first:
                        act.wait_ge(r_out[q], 16 * i)
                    copy_pair(res, q, r_copied)
                    if q == 0:
                        dense_copy(m, 3)
                        if not last:
                            dense_root(m + 1, 0, 0)
                    elif q == 1:
                        dense_apply(m, 1, 0)
                    elif q == 2 and not last:
                        dense_apply(m + 1, 0, 0)
                dense_root(m, 1, 1)
                if not last:
                    dense_root(m + 1, 0, 1)

            def rows(s, i, q):
                gb = s * NB + i
                act.wait_ge(got_used, G * gb + 2 * q + 2)
                if s < 3 or (isinstance(i, int) and i == 0):
                    act.wait_ge(r_out[q], 16 * gb)
                else:
                    act.wait_ge(y_done, HP * (i - 1) + q + 1)
                    act.wait_ge(edge_out, 32 * i)
                copy_pair(res, q, r_copied)

            def root(q, i):
                act.wait_ge(var_done, HP * NB + HP * i + q + 1)
                act.activation(rstd[:, 2 * q:2 * q + 2], mv[:, 2 * q:2 * q + 2, 1], ACT.Sqrt, bias=eps[:, :]).then_inc(std_done, 1)

            def dense_root(m, h, u):
                act.wait_ge(dvar[h], DU * m + u + 1)
                act.activation(drstd[:, u, h, :], dmv[:, u, h, :, 1], ACT.Sqrt, bias=eps[:, :]).then_inc(dstd[h], 1)

            def dense_apply(m, h, u):
                act.wait_ge(dscale[h], DU * m + u + 1)
                if h == 0 and not (isinstance(m, int) and m == 0):
                    act.wait_ge(dadded, 4 * (m - 1) + 2 * u + 2)
                t, t_out, done = ((dx, dx1, dx1_done), (dy, dy, dy_done))[h]
                for g in range(4):
                    ins = act.activation(t_out[:, u, g, :], t[:, u, g, :], ACT.Identity,
                                         bias=dshift[:, u, h, g:g + 1], scale=drstd[:, u, h, g:g + 1])
                ins.then_inc(done, 1)

            def dense_copy(m, n, alone=False):
                u, v = n // 2, n % 2
                act.wait_ge(dturned, 4 * m + n + 1)
                act.copy(dx1t[:, u, 2 * v:2 * v + 2, :].rearrange("p g d -> p (g d)"), 
                         bank[(5, 6, 7, 4 if alone else 5)[n]][:, :]).then_inc(dx1t_copied, 1)

            def seam_first_stage():
                act.wait_ge(sm_rows, 1)
                for c in range(C):
                    act.copy(seam_last[0:PT, :, c * P:(c + 1) * P],
                             bank[c][0:PT, :].rearrange("p (a f) -> p a f", a=A)).then_inc(sm_rows_c, 1)
                v = bank[5][0:PT, :].rearrange("p (a f) -> p a f", a=A)
                act.copy(seam_cnt[0:PT, 0, :], v[:, :, 0]).then_inc(sm_rows_c, 1)
                act.copy(seam_cnt[0:PT, 1, :], v[:, :, P - 1]).then_inc(sm_rows_c, 1)
                seam_root(0)
                act.wait_ge(sm_turned, 1)
                for h in range(2):
                    act.copy(seam_x1t[:, 2 * h:2 * h + 2, :, :].rearrange("p a c f -> p (a c f)"),
                             bank[2 + h][:, 0:2 * C * PT]).then_inc(sm_x1t, 1)
                act.wait_ge(sm_r, 1)
                act.copy(seam_res[0:PT, 0:2, :].rearrange("p a d -> p (a d)"), bank[0][0:PT, :])
                act.copy(seam_res[0:PT, 2:4, :].rearrange("p a d -> p (a d)"), bank[1][0:PT, :]).then_inc(sm_res, 1)

            def seam_root(n):
                act.wait_ge(sm_var, n + 1)
                act.activation(seam_rstd[0:PT, :], seam_mv[0:PT, :, 1], ACT.Sqrt, bias=eps[0:PT, :]).then_inc(sm_std, 1)

            def dense_only(m, last=False):
                dense_copy(m, 2, True)
                dense_copy(m, 3, True)
                dense_root(m, 1, 0)
                dense_root(m + 1, 0, 0)
                dense_apply(m, 1, 0)
                dense_apply(m + 1, 0, 0)
                if not last:
                    dense_copy(m + 1, 0)
                    dense_copy(m + 1, 1)
                dense_root(m, 1, 1)
                dense_root(m + 1, 0, 1)
                if not last:
                    dense_apply(m, 1, 1)
                    dense_apply(m + 1, 0, 1)

            for u in range(DU):
                dense_root(0, 0, u)
            for u in range(DU):
                dense_apply(0, 0, u)
            dense_copy(0, 0)
            dense_copy(0, 1)
            with act.Fori(0, NB - 1) as i:
                dense_only(i)
            dense_only(NB - 1, last=True)
            first_stage(0, first=True)
            with act.Fori(1, NB - 1) as i:
                first_stage(i)
            first_stage(NB - 1, last=True)
            dense_apply(2 * NB - 1, 1, 1)
            seam_first_stage()

            def later_stage(s, i):
                for q in range(HP):
                    rows(s, i, q)
                    if s == 3 and q > 0:
                        root(q - 1, i)
                if s == 3:
                    root(HP - 1, i)

            for s in (1, 2, 3):
                later_stage(s, 0)
                with act.Fori(1, NB) as i:
                    later_stage(s, i)
            seam_root(1)

        @block.vector
        def _(ve):
            HP = G // 2
            ve.memset(sign_row[:, :, :], 1.0).then_inc(facts_v, 1)
            ve.memset(sort_a[:, :, :], PAD).then_inc(facts_v, 1)
            ve.memset(kbefore[0:1, 0:P], -1.0).then_inc(guard_set, 1)
            ve.wait_ge(facts_v, 2)
            for n in range(LOGN - LOGF):
                v = sign_row[:, n, :].rearrange("p (b h j) -> p b h j", h=2, j=1 << n)
                ins = ve.memset(v[:, :, 1, :], -1.0)
            ins.then_inc(signs_set, 1)
            ve.memset(got[:, :, :], 0.0)
            ve.memset(own[:, :, :], 0.0)
            ve.memset(start_now[:, :, :], 0)
            ve.memset(seam_own[:, :, :], 0.0).then_inc(cleared, 1)
            ve.memset(index[:, :, :], int(SKIP)).then_inc(facts_v, 1)
            ve.memset(zeros[:, :], 0.0)
            ve.memset(carry_b[:, 0:1], 0.0)
            ve.wait_ge(edges_in, 64)
            sv = Steps(ve, sort_v)
            sv.did(ve.tensor_copy(sort_a[0:EP, 0, 0:2 * EF], edge_i[0:EP, 0, 0:2 * EF]))
            sv.did(ve.tensor_scalar(sort_a[0:EP, 2, 0:EF], edge_i[0:EP, 1, 0:EF], FLAG, None, ALU.add))
            sv.did(ve.tensor_copy(sort_a[0:EP, 2, EF:2 * EF], edge_i[0:EP, 1, EF:2 * EF]))
            ve.wait_ge(place_set, 1)
            sv.did(ve.tensor_scalar(sort_a[0:EP, 1, 0:EF], place_i[0:EP, 0:EF], float(EF), None, ALU.add))
            sv.did(ve.tensor_scalar(sort_a[0:EP, 1, EF:2 * EF], place_i[0:EP, EF:2 * EF], float(-EF), None, ALU.add))
            ve.wait_ge(signs_copied, 2)
            ncopy, buf, other = 0, sort_a, sort_b
            for kind, arg in network():
                sv.settle()
                if kind == "turn":
                    ncopy += 3
                elif kind == "flip":
                    ve.wait_ge(sort_copied, ncopy)
                    if arg < LOGF:
                        v = buf[:, 0, :].rearrange("p (b h j) -> p b h j", h=2, j=1 << arg)[:, :, 1, :]
                        sv.did(ve.tensor_scalar(v, v, -1.0, None, ALU.mult))
                    else:
                        sv.did(ve.tensor_scalar(buf[:, 0, :], buf[:, 0, :], signs[:, arg - LOGF:arg - LOGF + 1], None, ALU.mult))
                else:
                    ve.wait_ge(sort_copied, ncopy)
                    lo, hi = (buf[:, :, :].rearrange("p w (b h j) -> p w b h j", h=2, j=arg)[:, :, :, h, :] for h in range(2))
                    olo, ohi = (other[:, :, :].rearrange("p w (b h j) -> p w b h j", h=2, j=arg)[:, :, :, h, :] for h in range(2))
                    m = swap[:, :].rearrange("p (b j) -> p b j", j=arg)
                    sv.did(ve.tensor_tensor(m, lo[:, 0], hi[:, 0], ALU.is_gt))
                    sv.did(ve.tensor_tensor(olo[:, 0], lo[:, 0], hi[:, 0], ALU.min))
                    sv.did(ve.tensor_tensor(ohi[:, 0], lo[:, 0], hi[:, 0], ALU.max))
                    ncopy += 1
                    ve.wait_ge(sort_copied, ncopy)
                    sv.settle()
                    for w in (1, 2):
                        sv.did(ve.copy_predicated(olo[:, w], m, hi[:, w]))
                        sv.did(ve.copy_predicated(ohi[:, w], m, lo[:, w]))
                if kind != "flip":
                    buf, other = other, buf
            assert sv.n == SORT_V and buf is sort_out

            fv = Steps(ve, facts_v, 3)
            key, partner_id, pay = (sort_out[:, w, :] for w in range(3))
            sv.settle()
            fv.did(ve.tensor_scalar(flag_x[:, :], pay, FLAG, None, ALU.is_ge))
            fv.did(ve.tensor_scalar(own_id_x[:, :], partner_id, float(EF), None, ALU.add))
            fv.did(ve.tensor_copy(place[:, :], place_i[:, :]))
            fv.settle()
            fv.did(ve.scalar_tensor_tensor(partner_x[:, :], flag_x[:, :], -FLAG, pay, ALU.mult, ALU.add))
            fv.did(ve.scalar_tensor_tensor(own_id_x[:, :], flag_x[:, :], float(-2 * EF), own_id_x[:, :], ALU.mult, ALU.add))
            ve.wait_ge(keys_back, 32)
            fv.did(ve.tensor_tensor(begin_x[:, :], key, kbefore[:, :], ALU.not_equal))
            for a in range(A):
                sl = slice(a * P, (a + 1) * P)
                fv.did(ve.tensor_scalar(whole_x[:, sl], key[:, sl], kafter[:, a:a + 1], None, ALU.not_equal))
            fv.settle()
            fv.did(ve.tensor_tensor(whole_x[:, :], whole_x[:, :], begin_x[:, :], ALU.mult))
            fv.did(ve.tensor_tensor(start_x[:, :], begin_x[:, :], place[:, :], ALU.mult))
            fv.settle()
            fv.did(ve.tensor_tensor_scan(begin_x[:, :], zeros[:, :], start_x[:, :], 0.0, ALU.add, ALU.max))
            fv.settle()
            ve.tensor_scalar(carry_a[:, :], zeros[:, 0:P], begin_x[:, FREE - 1:FREE], None, ALU.add).then_inc(carry_v, 1)
            ve.wait_ge(carry_turned, 1)
            ve.tensor_tensor_scan(carry_b[:, 1:P + 1], zeros[:, 0:P], bank[0][:, 0:P], 0.0, ALU.add, ALU.max).then_inc(carry_v, 1)
            ve.wait_ge(carry_turned, 2)
            fv.did(ve.tensor_copy(carry_a[:, 0:1], bank[1][:, 0:1]))
            fv.settle()
            fv.did(ve.tensor_scalar(start_x[:, :], begin_x[:, :], carry_a[:, 0:1], None, ALU.max))
            fv.did(ve.tensor_scalar(dest_x[:, :], key, SKIP, None, ALU.add))
            fv.settle()
            ve.scalar_tensor_tensor(dest_x[:, :], whole_x[:, :], -SKIP, dest_x[:, :], ALU.mult, ALU.add
                                    ).then_inc(facts_done, 1)
            kf, kl = key[:, 0:FREE:P], key[:, P - 1:FREE:P]
            fv.did(ve.tensor_tensor(seam_a[:, :], kf, kprev, ALU.is_equal))
            fv.did(ve.tensor_tensor(seam_b[:, :], kf, kl, ALU.is_equal))
            fv.did(ve.tensor_tensor(seam_d[:, :], kf, kafter[:, :], ALU.is_equal))
            fv.settle()
            fv.did(ve.tensor_tensor(seam_b[:, :], seam_b[:, :], seam_d[:, :], ALU.mult))
            fv.settle()
            fv.did(ve.tensor_scalar(seam_b[:, :], seam_b[:, :], -1.0, 1.0, ALU.mult, ALU.add))
            fv.settle()
            fv.did(ve.tensor_tensor(seam_a[:, :], seam_a[:, :], seam_b[:, :], ALU.mult))
            fv.did(ve.tensor_scalar(seam_d[:, :], kf, SKIP, None, ALU.add))
            fv.settle()
            fv.did(ve.scalar_tensor_tensor(seam_dest[:, 1, :], seam_a[:, :], -SKIP, seam_d[:, :], ALU.mult, ALU.add))
            fv.settle()
            fv.did(ve.tensor_scalar(seam_d[:, :], start_x[:, 0:FREE:P], SKIP, None, ALU.add))
            fv.settle()
            fv.did(ve.scalar_tensor_tensor(seam_dest[:, 0, :], seam_a[:, :], -SKIP, seam_d[:, :], ALU.mult, ALU.add))
            fv.did(ve.tensor_copy(seam_node[:, :], kf))
            ve.wait_ge(first_back, 16)
            for a in range(A):
                ins = ve.tensor_scalar(seam_eq[0:PT, a, :, :], first_bc[0:PT, :, :], key[0:PT, a * P + P - 1:a * P + P], None, ALU.is_equal)
            ins.then_inc(seam_facts, 1)
            ve.wait_ge(facts_turned, 1)

            def by_tile(n):
                return bank[n][:, :].rearrange("s (a p) -> s p a", a=A)[:, 0:PT, :]

            def tiles(t):
                return t.rearrange("s (p a) -> s p a", a=A)

            ve.tensor_copy(tiles(kcol[:, :]), by_tile(0))
            ve.tensor_copy(tiles(flagcol[:, :]), by_tile(1))
            ve.tensor_copy(tiles(wholecol[:, :]), by_tile(2))
            for field, n in ((0, 6), (1, 7), (2, 3), (3, 0), (4, 5)):
                ve.tensor_copy(tiles(index[:, 0:NT, field]), by_tile(n))
            ve.tensor_copy(tiles(index[:, G:NT + G, 6]), by_tile(4)).then_inc(index_done, 1)
            ve.wait_ge(index_done, 1)

            def equal(gb, i, flagged, js=range(G)):
                for j in js:
                    if j == js[0]:
                        ve.wait_ge(key_in, 16 * gb + 16)
                    if not (isinstance(gb, int) and gb == 0):
                        ve.wait_ge(got_used, G * (gb - 1) + j + 1)
                    if flagged:
                        ve.tensor_scalar(eq[:, j, :], key_bc[:, j, :], kcol[:, bass.ds(G * i + j, 1)],
                                         flagcol[:, bass.ds(G * i + j, 1)], ALU.is_equal, ALU.mult).then_inc(eq_done, 1)
                    else:
                        ve.tensor_scalar(eq[:, j, :], key_bc[:, j, :], kcol[:, bass.ds(G * i + j, 1)],
                                         None, ALU.is_equal).then_inc(eq_done, 1)

            def plain_wait():
                ve.sem_inc(passed_v, 1)

            def dense_stats(m, h, u, alone=False):
                if h == 0:
                    ve.wait_ge(dx_in[u], 16 * m + 16)
                else:
                    if not (isinstance(m, int) and m == 0):
                        ve.wait_ge(dy_out[u], 16 * m)
                    for v in range(2):
                        ve.wait_ge(dmul, 4 * m + 2 * u + v + 1)
                        n = 2 * u + v
                        ve.tensor_tensor(dy[:, u, 2 * v:2 * v + 2, :].rearrange("p g d -> p (g d)"),
                                         dx1[:, u, 2 * v:2 * v + 2, :].rearrange("p g d -> p (g d)"),
                                         bank[(5, 6, 7, 4 if alone else 5)[n]][:, :], ALU.add).then_inc(dadded, 1)
                    ve.wait_ge(dadded, 4 * m + 2 * u + 2)
                t = (dx, dy)[h]
                for g in range(4):
                    ins = ve.bn_stats(dstat[:, u, h, g, :], t[:, u, g, :])
                ins.then_inc(dense_v[h][u], 1)
                ve.wait_ge(dense_v[h][u], 2 * m + 1)
                plain_wait()
                for g in range(4):
                    ins = ve.bn_aggr(dmv[:, u, h, g, :], dstat[:, u, h, g, :])
                ins.then_inc(dvar[h], 1)

            def dense_scales(m, h, u):
                ve.wait_ge(dstd[h], DU * m + u + 1)
                ve.reciprocal(drstd[:, u, h, :], drstd[:, u, h, :]).then_inc(dense_v[h][u], 1)
                ve.wait_ge(dense_v[h][u], 2 * m + 2)
                ve.scalar_tensor_tensor(dshift[:, u, h, :], dmv[:, u, h, :, 0], -1.0, drstd[:, u, h, :],
                                        ALU.mult, ALU.mult).then_inc(dscale[h], 1)

            def dense_only(m):
                for u in range(DU):
                    dense_stats(m, 1, u, True)
                    dense_stats(m + 1, 0, u)
                    dense_scales(m, 1, u)
                    dense_scales(m + 1, 0, u)

            for u in range(DU):
                dense_stats(0, 0, u)
            for u in range(DU):
                dense_scales(0, 0, u)
            dense_only(0)
            with ve.Fori(1, NB) as i:
                dense_only(i)

            LN0 = G + HP * (1 + 2 + 1 + 1 + 1)

            def first_stage(i, first=False, last=False):
                st = Steps(ve, ln0_v, LN0 * i)
                ve.wait_ge(cnt_copied, i + 1)
                for j in range(G):
                    ve.wait_ge(own_in[j], 16 * i + 16)
                    st.did(ve.scalar_tensor_tensor(own[:, j, :], bias_bc[:, :], count[:, bass.ds(G * i + j, 1)],
                                                   own[:, j, :], ALU.mult, ALU.add))
                def stats(q):
                    st.settle()
                    ve.wait_ge(h_done, HP * i + q + 1)
                    if not first:
                        ve.wait_ge(turned, HP * (i - 1) + q + 1)
                    pair = slice(2 * q, 2 * q + 2)
                    st.did(ve.tensor_tensor(x1[:, pair, :].rearrange("p g d -> p (g d)"),
                                            own[:, pair, :].rearrange("p g d -> p (g d)"), bank[q][:, :], ALU.add))
                    st.settle()
                    for j in (2 * q, 2 * q + 1):
                        st.did(ve.bn_stats(stat[:, j, :], x1[:, j, :]))
                    st.settle()
                    plain_wait()
                    for j in (2 * q, 2 * q + 1):
                        ins = ve.bn_aggr(mv[:, j, :], stat[:, j, :])
                    ins.then_inc(var_done, 1)

                def norm(q):
                    ve.wait_ge(std_done, HP * i + q + 1)
                    pair = slice(2 * q, 2 * q + 2)
                    st.did(ve.reciprocal(rstd[:, pair], rstd[:, pair]))
                    st.settle()
                    st.did(ve.tensor_tensor(rstd[:, pair], rstd[:, pair], wholecol[:, bass.ds(G * i + 2 * q, 2)], ALU.mult))
                    st.settle()
                    for j in (2 * q, 2 * q + 1):
                        ins = ve.tensor_scalar(x1[:, j, :], x1[:, j, :], mv[:, j, 0:1], rstd[:, j:j + 1], ALU.subtract, ALU.mult)
                        if j % 2 == 0:
                            st.did(ins)
                    ins.then_inc(x1_done, 1)

                stats(0)
                for q in range(1, HP):
                    stats(q)
                    norm(q - 1)
                norm(HP - 1)
                ve.wait_ge(cnt_done, i + 1)
                m = i + NB
                for u in range(DU):
                    dense_stats(m, 1, u)
                    if u == 0:
                        if last:
                            equal(NB, 0, False)
                        else:
                            equal(i + 1, i + 1, True)
                    if not last:
                        dense_stats(m + 1, 0, u)
                    dense_scales(m, 1, u)
                    if not last:
                        dense_scales(m + 1, 0, u)
                return st

            equal(0, 0, True)
            st = first_stage(0, True)
            assert st.n == LN0, st.n
            with ve.Fori(1, NB - 1) as i:
                first_stage(i)
            first_stage(NB - 1, last=True)

            sm = Steps(ve, sm_v)

            def seam_norm(t_out, n):
                sm.settle()
                for a in range(A):
                    sm.did(ve.bn_stats(seam_stat[0:PT, a, :], t_out[0:PT, a, :]))
                sm.settle()
                for a in range(A):
                    ins = ve.bn_aggr(seam_mv[0:PT, a, :], seam_stat[0:PT, a, :])
                ins.then_inc(sm_var, 1)
                ve.wait_ge(sm_std, n + 1)
                sm.did(ve.reciprocal(seam_rstd[0:PT, :], seam_rstd[0:PT, :]))
                sm.settle()
                for a in range(A):
                    ins = ve.tensor_scalar(t_out[0:PT, a, :], t_out[0:PT, a, :], seam_mv[0:PT, a, 0:1],
                                           seam_rstd[0:PT, a:a + 1], ALU.subtract, ALU.mult)
                return ins

            ve.wait_ge(sm_sum, 1)
            for c in range(C):
                ve.tensor_tensor(seam_agg[:, c, :, :], bank[2 + c][:, 0:A * PT].rearrange("p (a q) -> p a q", a=A),
                                 firsts_t[:, c, :].rearrange("p (q a) -> p a q", a=A), ALU.add).then_inc(sm_agg, 1)
            ve.tensor_tensor(seam_cn[0:PT, :], bank[4][0:PT, 0:A], seam_cnt[0:PT, 0, :], ALU.add).then_inc(sm_agg, 1)
            ve.wait_ge(sm_agg, C + 1)
            ve.wait_ge(sm_own, 16 * A)
            for a in range(A):
                sm.did(ve.scalar_tensor_tensor(seam_own[0:PT, a, :], bias_bc[0:PT, :], seam_cn[0:PT, a:a + 1],
                                               seam_own[0:PT, a, :], ALU.mult, ALU.add))
            sm.settle()
            ve.wait_ge(sm_h, 1)
            for h in range(2):
                sm.did(ve.tensor_tensor(seam_x1[0:PT, 2 * h:2 * h + 2, :].rearrange("p a d -> p (a d)"),
                                        seam_own[0:PT, 2 * h:2 * h + 2, :].rearrange("p a d -> p (a d)"), bank[h][0:PT, :], ALU.add))
            seam_norm(seam_x1, 0).then_inc(sm_x1, 1)

            def seam(s):
                ve.wait_ge(sm_r, s + 1)
                ve.wait_ge(sm_in, 32 * s)
                ve.wait_ge(sm_out, 16 * A * s)
                for h in range(2):
                    ins = ve.tensor_tensor(seam_res[0:PT, 2 * h:2 * h + 2, :].rearrange("p a d -> p (a d)"),
                                           seam_first[0:PT, 2 * h:2 * h + 2, :].rearrange("p a d -> p (a d)"), bank[h][0:PT, :], ALU.add)
                    if s == 3:
                        sm.did(ins)
                if s == 3:
                    sm.settle()
                    for h in range(2):
                        sm.did(ve.tensor_tensor(seam_res[0:PT, 2 * h:2 * h + 2, :], seam_res[0:PT, 2 * h:2 * h + 2, :],
                                                seam_x1[0:PT, 2 * h:2 * h + 2, :], ALU.add))
                    ins = seam_norm(seam_res, 1)
                ins.then_inc(sm_res, 1)

            for s in (1, 2):
                with ve.Fori(0, NB - 1) as i:
                    equal(s * NB + 1 + i, i + 1, False)
                equal((s + 1) * NB, 0, False)
                seam(s)

            LN3 = G + HP
            def last_stage(i, last=False):
                st = Steps(ve, ln3_v, LN3 * i)

                def stats(q):
                    ve.wait_ge(r_copied, HP * (3 * NB + i) + q + 1)
                    for j in (2 * q, 2 * q + 1):
                        st.did(ve.bn_stats(stat[:, j, :], res[:, j, :]))
                    st.settle()
                    plain_wait()
                    for j in (2 * q, 2 * q + 1):
                        ins = ve.bn_aggr(mv[:, j, :], stat[:, j, :])
                    ins.then_inc(var_done, 1)

                def norm(q):
                    ve.wait_ge(std_done, HP * (NB + i) + q + 1)
                    pair = slice(2 * q, 2 * q + 2)
                    st.did(ve.reciprocal(rstd[:, pair], rstd[:, pair]))
                    st.settle()
                    for j in (2 * q, 2 * q + 1):
                        if not (isinstance(i, int) and i == 0):
                            ve.wait_ge(scattered[j], 16 * i)
                        ins = ve.tensor_scalar(x1[:, j, :], res[:, j, :], mv[:, j, 0:1], rstd[:, j:j + 1], ALU.subtract, ALU.mult)
                    ins.then_inc(y_done, 1)

                def eq_pair(q):
                    if not last:
                        equal(3 * NB + i + 1, i + 1, False, range(2 * q, 2 * q + 2))

                stats(0)
                for q in range(1, HP):
                    eq_pair(q - 1)
                    stats(q)
                    norm(q - 1)
                eq_pair(HP - 1)
                norm(HP - 1)
                assert st.n == LN3

            last_stage(0)
            with ve.Fori(1, NB - 1) as i:
                last_stage(i)
            last_stage(NB - 1, last=True)
            seam(3)


_INS = ["x", "src", "dst", "L0_gnn_W", "L0_gnn_b", "L1_gnn_weights"]
_OUTS = [((100000, 256), "float32")]


def kernel(**inputs):
    import numpy as _np
    import concourse.bacc as _bacc
    from concourse import mybir as _mybir
    from concourse.bass_utils import run_bass_kernel_spmd as _run

    nc = _bacc.Bacc("TRN2", target_bir_lowering=False, num_devices=1)
    arrays, args = {}, []
    for name in _INS:
        a = _np.ascontiguousarray(inputs[name])
        arrays[f"in_{name}_dram"] = a
        args.append(nc.dram_tensor(f"in_{name}_dram", a.shape, _mybir.dt.from_np(a.dtype), kind="ExternalInput").ap())
    for i, (shape, dtype) in enumerate(_OUTS):
        dt = _mybir.dt.from_np(_np.dtype(dtype))
        args.append(nc.dram_tensor(f"out_{i}_dram", shape, dt, kind="ExternalOutput").ap())
    gnn_kernel(nc, *args)
    r = _run(nc, [arrays], core_ids=[0])
    return r.results[0]["out_0_dram"]
```

```python
from contextlib import ExitStack

import concourse.bass as bass
from concourse import mybir

ALU = mybir.AluOpType
ACT = mybir.ActivationFunctionType
F32 = mybir.dt.float32
I32 = mybir.dt.int32

P = 128
EPS = 1e-5


def gnn_kernel(nc, x, src, dst, w0, b0, w1, out):
    N, D = x.shape
    E = src.shape[0]
    K = w1.shape[0]
    C = D // P
    G = 8
    NT = -(-(2 * E) // (P * G)) * G
    NB = NT // G
    A = 4
    PT = NT // A
    FREE = A * P
    LOGF = FREE.bit_length() - 1
    NSORT = P * FREE
    LOGN = NSORT.bit_length() - 1
    PH = (1 << 24) // (N + 1)
    PL = -(-(N + 1) // PH)
    OFF = float(1 << 24)
    WHOLE = 1024.0
    SKIP = float(1 << 18)
    EP = 125
    EF = E // EP
    DR = 4 * P
    ND = -(-N // DR)
    DU = 2
    assert D == 256 and K == 4 and EP * EF == E and NT % (A * 1) == 0 and PT <= P
    assert 2 * E <= NT * P <= NSORT and PL * 2 * E <= 1 << 25 and N < SKIP and ND == 2 * NB * DU and 2 * EF <= FREE

    with ExitStack() as ctx:
        def sb(name, shape, dt=F32):
            return ctx.enter_context(nc.sbuf_tensor(name, shape, dt))

        def psum(name):
            return ctx.enter_context(nc.psum_tensor(name, [P, 512], F32))

        def sem(name):
            return ctx.enter_context(nc.semaphore(name))

        def dram(name, shape):
            return nc.dram_tensor(name, shape, F32, kind="Internal").ap()

        keys_dram = dram("keys_dram", [P + NSORT + P])
        first_dram = dram("first_dram", [A, PT])
        x1t_dram = dram("x1t_dram", [NB, P, G * D])
        rows_dram = {k: dram(f"r{k}_dram", [NT * P, D]) for k in (3, 2, 1)}
        edge_dram = dram("edge_dram", [NT, 2, D])
        start_dram = nc.dram_tensor("start_dram", [NSORT, 1], I32, kind="Internal").ap()

        ident = sb("ident", [P, P])
        eps = sb("eps", [P, 1])
        bias_bc = sb("bias_bc", [P, D])
        w0_in = sb("w0_in", [P, C, D])
        w0t = sb("w0t", [P, C, D])
        wk = sb("wk", [P, K, C, D])

        edge_i = sb("edge_i", [P, 2, FREE], I32)
        edge_place = sb("edge_place", [P, 2 * EF], I32)
        sort_a = sb("sort_a", [P, 2, FREE])
        sort_b = sb("sort_b", [P, 2, FREE])
        quotient = sb("quotient", [P, FREE], I32)
        swap = quotient[:, :].rearrange("p (h j) -> p h j", h=2)
        remainder = sb("remainder", [P, FREE])
        above = sb("above", [P, FREE])
        place_i = sb("place_i", [P, FREE], I32)
        place = sb("place", [P, FREE])
        signs = sb("signs", [P, LOGN - LOGF])
        sign_row = sb("sign_row", [P, LOGN - LOGF, P])

        kbefore = sb("kbefore", [P, FREE])
        kprev = kbefore[:, 0:FREE:P]
        kafter = sb("kafter", [P, A])
        flag_x = sb("flag_x", [P, FREE])
        partner_x = sb("partner_x", [P, FREE])
        begin_x = sb("begin_x", [P, FREE])
        whole_x = sb("whole_x", [P, FREE])
        start_x = sb("start_x", [P, FREE])
        own_id_x = sb("own_id_x", [P, FREE])
        zeros = sb("zeros", [P, FREE])
        carry_a = sb("carry_a", [P, P])
        carry_b = sb("carry_b", [P, P + 1])
        dest_x = sb("dest_x", [P, FREE])
        kcol = sb("kcol", [P, NT])
        flagcol = sb("flagcol", [P, NT])
        wholecol = sb("wholecol", [P, NT])
        index = sb("index", [P, NT + G, 7], I32)
        index_now = sb("index_now", [P, 2, G, 3], I32)
        count = sb("count", [P, NT])
        first_bc = sb("first_bc", [P, A, PT])
        seam_eq = sb("seam_eq", [P, A, A, PT])
        seam_a = sb("seam_a", [P, A])
        seam_b = sb("seam_b", [P, A])
        seam_d = sb("seam_d", [P, A])
        seam_stat = sb("seam_stat", [P, A, 6])
        seam_mv = sb("seam_mv", [P, A, 2])
        seam_rstd = sb("seam_rstd", [P, A])
        start_now = sb("start_now", [P, 2, G], I32)
        seam_dest = sb("seam_dest", [P, 2, A], I32)
        seam_node = sb("seam_node", [P, A], I32)

        got = sb("got", [P, G, D])
        own = sb("own", [P, G, D])
        key_bc = sb("key_bc", [P, G, P])
        eq = sb("eq", [P, G, P])
        agg = sb("agg", [P, G, D])
        x1 = sb("x1", [P, G, D])
        x1t = sb("x1t", [P, G, D])
        res = sb("res", [P, G, D])
        stat = sb("stat", [P, G, 6])
        mv = sb("mv", [P, G, 2])
        rstd = sb("rstd", [P, G])
        firsts_t = sb("firsts_t", [P, C, NT])
        lasts_t = sb("lasts_t", [P, C, NT])
        seam_last = sb("seam_last", [P, A, D])
        seam_first = sb("seam_first", [P, A, D])
        seam_cnt = sb("seam_cnt", [P, 2, A])
        seam_cn = sb("seam_cn", [P, A])
        seam_agg = sb("seam_agg", [P, C, A, PT])
        seam_own = sb("seam_own", [P, A, D])
        seam_x1 = sb("seam_x1", [P, A, D])
        seam_x1t = sb("seam_x1t", [P, A, C, PT])
        seam_res = sb("seam_res", [P, A, D])
        dx = sb("dx", [P, DU, 4, D])
        dx1 = sb("dx1", [P, DU, 4, D])
        dx1t = sb("dx1t", [P, DU, 4, D])
        dy = sb("dy", [P, DU, 4, D])
        dstat = sb("dstat", [P, DU, 2, 4, 6])
        dmv = sb("dmv", [P, DU, 2, 4, 2])
        drstd = sb("drstd", [P, DU, 2, 4])
        dshift = sb("dshift", [P, DU, 2, 4])

        bank = [psum(f"bank{n}") for n in range(8)]

        edges_in = sem("edges_in")
        weights_in = sem("weights_in")
        const_set = sem("const_set")
        guard_set = sem("guard_set")
        signs_set = sem("signs_set")
        cleared = sem("cleared")
        w0_turned = sem("w0_turned")
        w0_copied = sem("w0_copied")
        signs_turned = sem("signs_turned")
        signs_copied = sem("signs_copied")
        sort_v = sem("sort_v")
        sort_turned = sem("sort_turned")
        sort_copied = sem("sort_copied")
        keys_out = sem("keys_out")
        keys_back = sem("keys_back")
        first_out = sem("first_out")
        first_back = sem("first_back")
        facts_v = sem("facts_v")
        place_set = sem("place_set")
        keys_done = sem("keys_done")
        table_set = sem("table_set")
        carry_v = sem("carry_v")
        carry_turned = sem("carry_turned")
        facts_done = sem("facts_done")
        facts_turned = sem("facts_turned")
        index_done = sem("index_done")
        seam_facts = sem("seam_facts")
        seam_mask = sem("seam_mask")
        starts_kept = sem("starts_kept")
        idx_ready = sem("idx_ready")
        got_in = [sem(f"got_in{j}") for j in range(G)]
        own_in = [sem(f"own_in{j}") for j in range(G)]
        x1t_in = [sem(f"x1t_in{q}") for q in range(G // 2)]
        r_out = [sem(f"r_out{q}") for q in range(G // 2)]
        table_out = [sem(f"table_out{b}") for b in range(2)]
        start_in = [sem(f"start_in{b}") for b in range(2)]
        x1t_out = [sem(f"x1t_out{q}") for q in range(G // 2)]
        scattered = [sem(f"scattered{j}") for j in range(G)]
        edge_out = sem("edge_out")
        key_in = sem("key_in")
        eq_done = sem("eq_done")
        got_used = sem("got_used")
        agg_copied = sem("agg_copied")
        h_done = sem("h_done")
        x1_done = sem("x1_done")
        turned = sem("turned")
        x1t_copied = sem("x1t_copied")
        r_done = sem("r_done")
        r_copied = sem("r_copied")
        var_done = sem("var_done")
        std_done = sem("std_done")
        y_done = sem("y_done")
        ln0_v = sem("ln0_v")
        ln3_v = sem("ln3_v")
        dense_v = [[sem(f"dense_v{h}{u}") for u in range(DU)] for h in range(2)]
        dx_in = [sem(f"dx_in{u}") for u in range(DU)]
        dy_out = [sem(f"dy_out{u}") for u in range(DU)]
        dvar = [sem(f"dvar{h}") for h in range(2)]
        dstd = [sem(f"dstd{h}") for h in range(2)]
        dscale = [sem(f"dscale{h}") for h in range(2)]
        dx1_done = sem("dx1_done")
        dturned = sem("dturned")
        dx1t_copied = sem("dx1t_copied")
        dmul = sem("dmul")
        dadded = sem("dadded")
        dy_done = sem("dy_done")
        sm_in = sem("sm_in")
        sm_own = sem("sm_own")
        sm_rows = sem("sm_rows")
        sm_rows_c = sem("sm_rows_c")
        sm_sum = sem("sm_sum")
        sm_agg = sem("sm_agg")
        sm_h = sem("sm_h")
        sm_var = sem("sm_var")
        sm_std = sem("sm_std")
        sm_x1 = sem("sm_x1")
        sm_turned = sem("sm_turned")
        sm_x1t = sem("sm_x1t")
        sm_r = sem("sm_r")
        sm_res = sem("sm_res")
        sm_v = sem("sm_v")
        passed_v = sem("passed_v")
        passed_g = sem("passed_g")
        sm_out = sem("sm_out")

        class Steps:

            def __init__(self, eng, s, base=0):
                self.eng, self.s, self.base, self.n = eng, s, base, 0

            def did(self, ins):
                ins.then_inc(self.s, 1)
                self.n += 1

            def settle(self):
                self.eng.wait_ge(self.s, self.base + self.n)

        def col(t, a, j):
            return t[:, bass.ds(a + j, 1)]

        block = ctx.enter_context(nc.Block())

        def network():
            for k in range(1, LOGN + 1):
                if k < LOGN:
                    yield "flip", k
                if k > LOGF:
                    yield "turn", 0
                    for j in range(k - 1, LOGF - 1, -1):
                        yield "step", 1 << (j - LOGF)
                    yield "turn", 0
                for j in range(min(k, LOGF) - 1, -1, -1):
                    yield "step", 1 << j
                if k < LOGN:
                    yield "flip", k

        STEP_V, FLIP_V = 5, 1
        moves = sum(kind != "flip" for kind, _ in network())
        sort_out, sort_spare = ((sort_a, sort_b), (sort_b, sort_a))[moves % 2]
        PACK_V = 9
        SORT_V = PACK_V + sum({"step": STEP_V, "flip": FLIP_V, "turn": 0}[kind] for kind, _ in network())

        def dense_base(m, u):
            g = m * DU + u
            if isinstance(g, int):
                return max(N - (ND - g) * DR, 0)
            return g * DR + (N - ND * DR)

        def normed(odd, alone=True):
            if not alone or odd == NB % 2:
                return dx1
            return x1.rearrange("p (u g) d -> p u g d", u=DU)

        def dense_rows(t, m, u):
            return t[bass.ds(dense_base(m, u), DR), :].rearrange("(p g) d -> p (g d)", g=4)

        @block.sync
        def _(sp):
            HP = G // 2
            for h, (node, part) in enumerate(((src, dst), (dst, src))):
                for c, v in enumerate((node, part)):
                    sp.dma_start(edge_i[0:EP, c, h * EF:(h + 1) * EF],
                                 v.rearrange("(p f) -> p f", f=EF)).then_inc(edges_in, 16)
            sp.dma_start(w0_in[:, :, :], w0.rearrange("(c p) d -> p c d", p=P)).then_inc(weights_in, 16)
            sp.dma_start(wk[:, :, :, :], w1.rearrange("k (c p) o -> p k c o", p=P)).then_inc(weights_in, 16)
            sp.dma_start(bias_bc[:, :], b0.partition_broadcast(P)).then_inc(weights_in, 16)
            sp.wait_ge(guard_set, 1)
            sp.dma_start(keys_dram[0:P].rearrange("(a f) -> a f", a=1), kbefore[0:1, 0:P]).then_inc(keys_out, 16)
            sp.dma_start(keys_dram[P + NSORT:].rearrange("(a f) -> a f", a=1), kbefore[0:1, 0:P]).then_inc(keys_out, 16)
            sp.wait_ge(place_set, 2)
            sp.dma_start(start_dram.rearrange("(p f) a -> p (f a)", p=P), place_i[:, :]).then_inc(table_set, 16)
            sp.wait_ge(keys_done, 1)
            sp.dma_start(keys_dram[P:P + NSORT].rearrange("(p f) -> p f", f=FREE),
                         sort_out[:, 0, :]).then_inc(keys_out, 16)
            sp.dma_start(first_dram.rearrange("a p -> p a"), sort_out[0:PT, 0, 0:FREE:P],
                         allow_slow_non_contiguous=True).then_inc(first_out, 16)
            sp.wait_ge(keys_out, 48)
            sp.dma_start(kbefore[:, :], keys_dram[P - 1:P - 1 + NSORT].rearrange("(p f) -> p f", f=FREE)).then_inc(keys_back, 16)
            sp.dma_start(kafter[:, :], keys_dram[2 * P:2 * P + NSORT]
                         .rearrange("(p a f) -> p a f", a=A, f=P)[:, :, 0], allow_slow_non_contiguous=True).then_inc(keys_back, 16)
            sp.wait_ge(first_out, 16)
            sp.dma_start(first_bc[:, :, :], first_dram.partition_broadcast(P)).then_inc(first_back, 16)

            def keys(gb, i):
                if not (isinstance(gb, int) and gb == 0):
                    sp.wait_ge(eq_done, G * gb)
                sp.dma_start(key_bc[:, :, :],
                             keys_dram[bass.ds(P + i * (G * P), G * P)].partition_broadcast(P)
                             ).then_inc(key_in, 16)

            def pair_rows(t, i, q):
                return t[bass.ds(i * (G * P) + 2 * q * P, 2 * P), :].rearrange("(t s) d -> s t d", s=P)

            def pair_x1t(i, q):
                return x1t_dram[bass.ds(i, 1), :, 2 * q * D:(2 * q + 2) * D].rearrange("a p f -> (a p) f")

            def store_x1t(i, q):
                sp.wait_ge(x1t_copied, HP * i + q + 1)
                sp.dma_start(pair_x1t(i, q), x1t[:, 2 * q:2 * q + 2, :]).then_inc(x1t_out[q], 16)

            def load_x1t(s, i, q):
                gb = s * NB + i
                if isinstance(gb, int) and gb == NB:
                    sp.wait_ge(x1_done, HP * NB)
                else:
                    sp.wait_ge(got_used, G * (gb - 1) + 2 * q + 2)
                sp.dma_start(own[:, 2 * q:2 * q + 2, :], pair_x1t(i, q)).then_inc(x1t_in[q], 16)

            def store_rows(s, i, q):
                sp.wait_ge(r_copied, HP * (s * NB + i) + q + 1)
                sp.dma_start(pair_rows(rows_dram[3 - s], i, q), res[:, 2 * q:2 * q + 2, :]).then_inc(r_out[q], 16)

            def store_edges(i):
                sp.wait_ge(r_copied, HP * (3 * NB + i + 1))
                for h, p in enumerate((0, P - 1)):
                    sp.dma_start(edge_dram[bass.ds(G * i, G), h, :].rearrange("(a g) d -> a g d", a=1),
                                 res[p:p + 1, :, :]).then_inc(edge_out, 16)

            def load_dense(m, u):
                if not (isinstance(m, int) and m == 0):
                    sp.wait_ge(dx1_done, 4 * (m - 1) + 2 * u + 2)
                sp.dma_start(dx[:, u, :, :].rearrange("p g d -> p (g d)"), dense_rows(x, m, u)).then_inc(dx_in[u], 16)

            def store_dense(m, u):
                sp.wait_ge(dy_done, DU * m + u + 1)
                if isinstance(m, int) and m == 0 and u == 1:
                    sp.wait_ge(dy_out[0], 16)
                sp.dma_start(dense_rows(out, m, u), dy[:, u, :, :].rearrange("p g d -> p (g d)")
                             ).then_inc(dy_out[u], 16)

            for m in range(2):
                for u in range(DU):
                    load_dense(m, u)
            for u in range(DU):
                load_dense(2, u)
            for u in range(DU):
                store_dense(0, u)
                load_dense(3, u)
            with sp.Fori(2, NB - 1) as i:
                for u in range(DU):
                    store_dense(i - 1, u)
                    load_dense(i + 2, u)
            store_dense(NB - 2, 0)
            load_dense(NB + 1, 0)
            store_dense(NB - 2, 1)
            store_dense(NB - 1, 0)

            def first_stage(i, left):
                m = i + NB
                keys(i + 1, 0 if left == 0 else i + 1)
                store_dense(m - 1, 1)
                if left > 0:
                    load_dense(m + 1, 1)
                for q in range(HP):
                    store_x1t(i, q)
                store_rows(0, i, 0)
                store_rows(0, i, 1)
                store_dense(m, 0)
                store_rows(0, i, 2)
                if left > 1:
                    load_dense(m + 2, 0)
                store_rows(0, i, 3)

            keys(0, 0)
            with sp.Fori(0, NB - 2) as i:
                first_stage(i, 2)
            first_stage(NB - 2, 1)
            first_stage(NB - 1, 0)
            store_dense(2 * NB - 1, 1)
            for q in range(HP):
                sp.wait_ge(x1t_out[q], 16 * NB)
            for q in range(HP):
                load_x1t(1, 0, q)

            def later_stage(s, i, last=False):
                if not last:
                    keys(s * NB + i + 1, i + 1)
                elif s < 3:
                    keys((s + 1) * NB, 0)
                for q in range(HP):
                    if not last:
                        load_x1t(s, i + 1, q)
                    elif s < 3:
                        load_x1t(s + 1, 0, q)
                    if s < 3:
                        store_rows(s, i, q)
                if s == 3:
                    store_edges(i)

            for s in (1, 2, 3):
                with sp.Fori(0, NB - 1) as i:
                    later_stage(s, i)
                later_stage(s, NB - 1, last=True)
                if s < 3:
                    for q in range(HP):
                        sp.wait_ge(r_out[q], 16 * NB * (s + 1))
                    ev = rows_dram[3 - s].rearrange("(p a s) d -> p a s d", a=A, s=P)
                    last_rows, first_rows = ev[:, :, P - 1, :], ev[:, :, 0, :]
                else:
                    sp.wait_ge(edge_out, 32 * NB)
                    ev = edge_dram.rearrange("(p a) h d -> p a h d", a=A)
                    last_rows, first_rows = ev[:, :, 1, :], ev[:, :, 0, :]
                sp.wait_ge(sm_res, s)
                sp.dma_start(seam_last[0:PT, :, :], last_rows).then_inc(sm_in, 16)
                sp.dma_start(seam_first[0:PT, :, :], first_rows).then_inc(sm_in, 16)
            sp.wait_ge(dy_out[0], 32 * NB)
            sp.wait_ge(dy_out[1], 32 * NB)
            for j in range(G):
                sp.wait_ge(scattered[j], 16 * NB)
            sp.wait_ge(sm_out, 16 * A * 4)

        @block.gpsimd
        def _(gp):
            gp.memset(ident[:, :], 0.0).then_inc(const_set, 1)
            gp.memset(eps[:, :], EPS).then_inc(const_set, 1)
            gp.iota(place_i[:, :], pattern=[[1, FREE]], base=0, channel_multiplier=FREE).then_inc(place_set, 1)
            gp.iota(edge_place[:, :], pattern=[[E, 2], [1, EF]], base=0, channel_multiplier=EF).then_inc(place_set, 1)
            gp.wait_ge(const_set, 2)
            gp.affine_select(out=ident[:, :], in_=ident[:, :], compare_op=ALU.not_equal, fill=1.0,
                             base=0, pattern=[[-1, P]], channel_multiplier=1).then_inc(const_set, 1)
            gp.wait_ge(seam_facts, 1)
            for a in range(A):
                gp.affine_select(out=seam_eq[0:PT, a, :, :], in_=seam_eq[0:PT, a, :, :], compare_op=ALU.is_gt,
                                 fill=0.0, base=-a, pattern=[[1, A], [A, PT]],
                                 channel_multiplier=-A).then_inc(seam_mask, 1)
            gp.wait_ge(index_done, 1)

            HP = G // 2
            row_bound = {"x": gp.to_reg(N - 1), "slot": gp.to_reg(NT * P - 1), "place": gp.to_reg(NSORT - 1)}

            def take(i, b, fields, nth):
                lo, hi = fields
                gp.tensor_copy(index_now[:, b, :, 0:hi - lo], index[:, bass.ds(G * i, G), lo:hi]).then_inc(idx_ready, 1)
                gp.wait_ge(idx_ready, nth)
                gp.sem_inc(passed_g, 1)

            def gather(dst, table, b, j, f, bound, s):
                gp.indirect_dma_start(dst, None, table, bass.IndirectOffsetOnAxis(index_now[:, b, j, f:f + 1], 0),
                                      bounds_check=row_bound[bound], oob_is_err=False).then_inc(s, 16)

            def seam_scatter(s):
                gp.wait_ge(sm_res, s + 1)
                if s < 3:
                    for q in range(HP):
                        gp.wait_ge(r_out[q], 16 * NB * (s + 1))
                table, h, bound = (out, 1, "x") if s == 3 else (rows_dram[3 - s], 0, "slot")
                for a in range(A):
                    gp.indirect_dma_start(table[:, :], bass.IndirectOffsetOnAxis(seam_dest[0:PT, h, a:a + 1], 0),
                                          seam_res[0:PT, a, :], None, bounds_check=row_bound[bound], oob_is_err=False
                                          ).then_inc(sm_out, 16)
                gp.wait_ge(sm_out, 16 * A * (s + 1))

            def tabulate(i, b, fresh):
                if not fresh:
                    gp.wait_ge(table_out[b], (i - b) * (8 * G))
                take(i, b, (0, 2), i + 1)
                for j in range(G):
                    gp.indirect_dma_start(start_dram[:, :], bass.IndirectOffsetOnAxis(index_now[:, b, j, 0:1], 0),
                                          index_now[:, b, j, 1:2], None, bounds_check=row_bound["place"], oob_is_err=False
                                          ).then_inc(table_out[b], 16)

            gp.wait_ge(table_set, 16)
            tabulate(0, 0, True)
            tabulate(1, 1, True)
            with gp.Fori(2, NB - 1, 2) as i:
                tabulate(i, 0, False)
                tabulate(i + 1, 1, False)
            tabulate(NB - 1, 0, False)
            gp.wait_ge(cleared, 1)
            for a in range(A):
                gp.indirect_dma_start(seam_own[0:PT, a, :], None, x[:, :],
                                      bass.IndirectOffsetOnAxis(seam_node[0:PT, a:a + 1], 0),
                                      bounds_check=row_bound["x"], oob_is_err=False).then_inc(sm_own, 16)
            gp.wait_ge(table_out[0], 16 * G * (NB // 2 + 1))
            gp.wait_ge(table_out[1], 16 * G * (NB // 2))

            def keep_starts(i, b):
                gp.wait_ge(start_in[b], (i - b) * (8 * G) + 16 * G)
                gp.tensor_copy(index[:, bass.ds(G * i, G), 5], start_now[:, b, :]).then_inc(starts_kept, 1)

            def first_stage(i, b, fresh, first):
                if not fresh:
                    keep_starts(i - 2, b)
                    gp.wait_ge(got_used, G * (i - 1))
                    gp.wait_ge(x1_done, HP * (i - 1))
                    gp.wait_ge(starts_kept, i - 1)
                take(i, b, (2, 5), i + (NB + 1))

                def starts(js):
                    for j in js:
                        gather(start_now[:, b, j:j + 1], start_dram[:, :], b, j, 2, "place", start_in[b])

                for j in range(G):
                    if not first:
                        gp.wait_ge(got_used, G * (i - 1) + j + 1)
                        gp.sem_inc(passed_g, 1)
                    gather(got[:, j, :], x[:, :], b, j, 0, "x", got_in[j])
                starts(range(0, G // 2))
                for j in range(G):
                    if not first and j % 2 == 0:
                        gp.wait_ge(x1_done, HP * (i - 1) + j // 2 + 1)
                        gp.sem_inc(passed_g, 1)
                    gather(own[:, j, :], x[:, :], b, j, 1, "x", own_in[j])
                starts(range(G // 2, G))

            first_stage(0, 0, True, True)
            first_stage(1, 1, True, False)
            with gp.Fori(2, NB - 1, 2) as i:
                first_stage(i, 0, False, False)
                first_stage(i + 1, 1, False, False)
            first_stage(NB - 1, 0, False, False)
            keep_starts(NB - 2, 1)
            keep_starts(NB - 1, 0)
            gp.wait_ge(starts_kept, NB)
            seam_scatter(0)

            def later_stage(s, i, b, wait_half, last=False, do_gather=True, do_scatter=False):
                gb = s * NB + i
                nth = 2 * NB + (s - 1) * NB
                if wait_half:
                    gp.wait_ge(got_used, G * (gb - 1))
                    if do_scatter:
                        if not isinstance(i, int) or i > 2:
                            for j in range(G):
                                gp.wait_ge(scattered[j], 16 * (i - 2))
                take(i, b, (5, 7), i + (nth + 1))
                for j in range(G):
                    if do_gather:
                        gp.wait_ge(got_used, G * (gb - 1) + j + 1)
                        gp.sem_inc(passed_g, 1)
                        gather(got[:, j, :], rows_dram[4 - s][:, :], b, j, 0, "slot", got_in[j])
                    if do_scatter:
                        gp.wait_ge(y_done, HP * (i - 1) + j // 2 + 1)
                        gp.sem_inc(passed_g, 1)
                        gp.indirect_dma_start(out[:, :], bass.IndirectOffsetOnAxis(index_now[:, b, j, 1:2], 0),
                                              x1[:, j, :], None, bounds_check=row_bound["x"], oob_is_err=False
                                              ).then_inc(scattered[j], 16)

            for s in (1, 2, 3):
                if s == 3:
                    for u in range(DU):
                        gp.wait_ge(dy_out[u], 32 * NB)
                sc = s == 3
                later_stage(s, 0, 0, False)
                later_stage(s, 1, 1, False, do_scatter=sc)
                later_stage(s, 2, 0, True, do_scatter=sc)
                with gp.Fori(3, NB, 2) as i:
                    later_stage(s, i, 1, True, do_scatter=sc)
                    later_stage(s, i + 1, 0, True, do_scatter=sc)
                if sc:
                    later_stage(s, NB, 1, True, do_gather=False, do_scatter=True)
                seam_scatter(s)

        @block.tensor
        def _(pe):
            pe.wait_ge(const_set, 3)
            pe.wait_ge(weights_in, 48)
            for c in range(C):
                for o in range(C):
                    mm = pe.transpose(bank[0][:, (c * C + o) * P:(c * C + o + 1) * P],
                                      w0_in[:, o, c * P:(c + 1) * P], ident[:, :])
            mm.then_inc(w0_turned, 1)
            pe.wait_ge(signs_set, 1)
            for n in range(LOGN - LOGF):
                mm = pe.transpose(bank[1 + n // 4][:, (n % 4) * P:(n % 4 + 1) * P], sign_row[:, n, :], ident[:, :])
            mm.then_inc(signs_turned, 1)
            pe.wait_ge(w0_copied, 1)
            pe.wait_ge(signs_copied, 2)
            nv, buf, other = PACK_V, sort_a, sort_b
            for kind, _ in network():
                if kind == "turn":
                    pe.wait_ge(sort_v, nv)
                    for h in range(2):
                        for a in range(A):
                            mm = pe.transpose(bank[h][:, a * P:(a + 1) * P], buf[:, h, a * P:(a + 1) * P], ident[:, :])
                    mm.then_inc(sort_turned, 1)
                nv += {"step": STEP_V, "flip": FLIP_V, "turn": 0}[kind]
                if kind != "flip":
                    buf, other = other, buf
            pe.wait_ge(carry_v, 1)
            pe.transpose(bank[0][:, 0:P], carry_a[:, :], ident[:, :]).then_inc(carry_turned, 1)
            pe.wait_ge(carry_v, 2)
            pe.transpose(bank[1][:, 0:P], carry_b[:, 0:P], ident[:, :]).then_inc(carry_turned, 1)
            pe.wait_ge(facts_done, 1)
            for n, t in enumerate((sort_out[:, 0, :], flag_x, sort_spare[:, 1, :], partner_x, dest_x, sort_out[:, 1, :], own_id_x, start_x)):
                for a in range(A):
                    mm = pe.transpose(bank[n][:, a * P:(a + 1) * P], t[:, a * P:(a + 1) * P], ident[:, :])
            mm.then_inc(facts_turned, 1)
            pe.wait_ge(index_done, 1)

            HP = G // 2

            DENSE_BANK = (5, 6, 7, 4)

            def turn_pair(t, n, b):
                u, v = n // 2, n % 2
                for g in (2 * v, 2 * v + 1):
                    for c in range(C):
                        mm = pe.transpose(bank[b][:, ((g % 2) * C + c) * P:((g % 2) * C + c + 1) * P],
                                          t[:, u, g, c * P:(c + 1) * P], ident[:, :])
                mm.then_inc(dturned, 1)

            def mul_pair(n, b):
                u, v = n // 2, n % 2
                for g in (2 * v, 2 * v + 1):
                    for c in range(C):
                        mm = pe.matmul(bank[b][:, (g % 2) * D:(g % 2 + 1) * D],
                                       dx1t[:, u, g, c * P:(c + 1) * P], wk[:, 0, c, :], start=(c == 0), stop=(c == C - 1))
                mm.then_inc(dmul, 1)

            def dense_turn(m, n):
                pe.wait_ge(dx1_done, 4 * m + n + 1)
                pe.wait_ge(dadded, 4 * (m - 1) + n + 1)
                turn_pair(dx1, n, DENSE_BANK[n])

            def dense_mul(m, n):
                pe.wait_ge(dx1t_copied, 4 * m + n + 1)
                mul_pair(n, DENSE_BANK[n])

            def turn_alone(m, n, odd, first=False):
                pe.wait_ge(dx1_done, 4 * m + n + 1)
                if not first:
                    pe.wait_ge(dx1t_copied, 4 * (m - 1) + n + 1)
                turn_pair(normed(odd), n, n)

            def mul_alone(m, n, first=False):
                pe.wait_ge(dx1t_copied, 4 * m + n + 1)
                if not first:
                    pe.wait_ge(dadded, 4 * (m - 1) + n + 1)
                mul_pair(n, DENSE_BANK[n])

            def first_stage(i, first):
                for q in range(HP):
                    if not first:
                        pe.wait_ge(r_copied, HP * (i - 1) + q + 1)
                    for j in (2 * q, 2 * q + 1):
                        pe.wait_ge(eq_done, G * i + j + 1)
                        pe.wait_ge(got_in[j], 16 * i + 16)
                        for c in range(C):
                            mm = pe.matmul(bank[q][:, ((j % 2) * C + c) * P:((j % 2) * C + c + 1) * P],
                                           got[:, j, c * P:(c + 1) * P], eq[:, j, :], start=True, stop=True)
                        mm.then_inc(got_used, 1)
                m = i + NB
                dense_turn(m, 0)
                dense_turn(m, 1)
                for q in range(HP):
                    pe.wait_ge(agg_copied, 3 * (HP * i + q + 1))
                    for j in (2 * q, 2 * q + 1):
                        for c in range(C):
                            mm = pe.matmul(bank[q][:, (j % 2) * D:(j % 2 + 1) * D],
                                           agg[:, j, c * P:(c + 1) * P], w0t[:, c, :], start=(c == 0), stop=(c == C - 1))
                    mm.then_inc(h_done, 1)
                dense_turn(m, 2)
                dense_turn(m, 3)
                for n in range(3):
                    dense_mul(m, n)
                for q in range(HP):
                    if q == HP - 1:
                        dense_mul(m, 3)
                    pe.wait_ge(x1_done, HP * i + q + 1)
                    for j in (2 * q, 2 * q + 1):
                        for c in range(C):
                            mm = pe.transpose(bank[q][:, ((j % 2) * C + c) * P:((j % 2) * C + c + 1) * P],
                                              x1[:, j, c * P:(c + 1) * P], ident[:, :])
                    mm.then_inc(turned, 1)
                for q in range(HP):
                    pe.wait_ge(x1t_copied, HP * i + q + 1)
                    for j in (2 * q, 2 * q + 1):
                        for c in range(C):
                            mm = pe.matmul(bank[q][:, (j % 2) * D:(j % 2 + 1) * D],
                                           x1t[:, j, c * P:(c + 1) * P], wk[:, 3, c, :], start=(c == 0), stop=(c == C - 1))
                    mm.then_inc(r_done, 1)

            def dense_only(m, odd, first=False, last=False):
                for u in range(DU):
                    for n in (2 * u, 2 * u + 1):
                        mul_alone(m, n, first)
                    if not last:
                        for n in (2 * u, 2 * u + 1):
                            turn_alone(m + 1, n, not odd)

            def slots(s, i, q):
                gb = s * NB + i
                pe.wait_ge(r_copied, HP * (gb - 1) + q + 1)
                pe.wait_ge(x1t_in[q], 16 * (gb - NB) + 16)
                for j in (2 * q, 2 * q + 1):
                    o = bank[q][:, (j % 2) * D:(j % 2 + 1) * D]
                    for c in range(C):
                        pe.matmul(o, own[:, j, c * P:(c + 1) * P], wk[:, 3 - s, c, :], start=(c == 0), stop=False)
                    if s == 3:
                        for c in range(C):
                            pe.matmul(bank[q][:, (j % 2) * D + c * P:(j % 2) * D + (c + 1) * P],
                                      own[:, j, c * P:(c + 1) * P], ident[:, :], start=False, stop=False,
                                      skip_group_check=True)
                    pe.wait_ge(eq_done, G * gb + j + 1)
                    pe.wait_ge(got_in[j], 16 * gb + 16)
                    mm = pe.matmul(o, eq[:, j, :], got[:, j, :], start=False, stop=True)
                    mm.then_inc(got_used, 1)

            def seam_first_stage():
                pe.wait_ge(agg_copied, 3 * NB * HP)
                pe.wait_ge(r_copied, HP * NB)
                pe.wait_ge(dadded, 4 * 2 * NB)
                pe.wait_ge(seam_mask, A)
                for c in range(C):
                    for a in range(A):
                        pe.transpose(bank[c][0:PT, a * P:(a + 1) * P], lasts_t[:, c, a:NT:A], ident[:, :])
                for a in range(A):
                    mm = pe.transpose(bank[5][0:PT, a * P:(a + 1) * P], count[:, a:NT:A], ident[:, :])
                mm.then_inc(sm_rows, 1)
                pe.wait_ge(sm_rows_c, 4)
                for c in range(C):
                    for a in range(A):
                        pe.matmul(bank[2 + c][:, 0:A * PT], seam_last[0:PT, a, c * P:(c + 1) * P],
                                  seam_eq[0:PT, a, :, :].rearrange("p a q -> p (a q)"),
                                  start=(a == 0), stop=(a == A - 1))
                for b in range(A):
                    for a in range(A):
                        mm = pe.matmul(bank[4][0:PT, b:b + 1], seam_eq[0:PT, a, b, :],
                                       seam_cnt[0:PT, 1, a:a + 1], start=(a == 0), stop=(a == A - 1))
                mm.then_inc(sm_sum, 1)
                pe.wait_ge(sm_agg, C + 1)
                for a in range(A):
                    for c in range(C):
                        mm = pe.matmul(bank[a // 2][0:PT, (a % 2) * D:(a % 2 + 1) * D], seam_agg[:, c, a, :],
                                       w0t[:, c, :], start=(c == 0), stop=(c == C - 1))
                mm.then_inc(sm_h, 1)
                pe.wait_ge(sm_x1, 1)
                for a in range(A):
                    for c in range(C):
                        mm = pe.transpose(bank[2 + a // 2][:, ((a % 2) * C + c) * PT:((a % 2) * C + c + 1) * PT],
                                          seam_x1[0:PT, a, c * P:(c + 1) * P], ident[0:PT, 0:PT])
                mm.then_inc(sm_turned, 1)
                pe.wait_ge(sm_x1t, 2)
                for a in range(A):
                    for c in range(C):
                        mm = pe.matmul(bank[a // 2][0:PT, (a % 2) * D:(a % 2 + 1) * D], seam_x1t[:, a, c, :],
                                       wk[:, 3, c, :], start=(c == 0), stop=(c == C - 1))
                mm.then_inc(sm_r, 1)

            def seam(s):
                pe.wait_ge(r_copied, HP * NB * (s + 1))
                pe.wait_ge(sm_in, 32 * s)
                for a in range(A):
                    o = bank[a // 2][0:PT, (a % 2) * D:(a % 2 + 1) * D]
                    for c in range(C):
                        pe.matmul(o, seam_x1t[:, a, c, :], wk[:, 3 - s, c, :], start=(c == 0), stop=False)
                    for b in range(A):
                        mm = pe.matmul(o, seam_eq[0:PT, b, a, :], seam_last[0:PT, b, :], start=False, stop=(b == A - 1))
                mm.then_inc(sm_r, 1)

            for n in range(4):
                turn_alone(0, n, False, first=True)
            dense_only(0, False, first=True)
            dense_only(1, True)
            with pe.Fori(2, NB - 1, 2) as i:
                dense_only(i, False)
                dense_only(i + 1, True)
            dense_only(NB - 1, False, last=True)
            first_stage(0, True)
            with pe.Fori(1, NB) as i:
                first_stage(i, False)
            seam_first_stage()
            for s in (1, 2, 3):
                pe.wait_ge(sm_res, s)
                with pe.Fori(0, NB) as i:
                    for q in range(HP):
                        slots(s, i, q)
                seam(s)

        @block.scalar
        def _(act):
            HP = G // 2
            act.wait_ge(w0_turned, 1)
            act.copy(w0t[:, :, :].rearrange("p c d -> p (c d)"), bank[0][:, :]).then_inc(w0_copied, 1)
            act.wait_ge(signs_turned, 1)
            act.copy(signs[:, 0:4], bank[1][:, 0:4 * P:P]).then_inc(signs_copied, 1)
            act.copy(signs[:, 4:LOGN - LOGF], bank[2][:, 0:(LOGN - LOGF - 4) * P:P]).then_inc(signs_copied, 1)
            nv, nturn, ncopy, buf, other = PACK_V, 0, 0, sort_a, sort_b
            for kind, _ in network():
                if kind == "turn":
                    nturn += 1
                    act.wait_ge(sort_turned, nturn)
                    for h in range(2):
                        act.copy(other[:, h, :], bank[h][:, :]).then_inc(sort_copied, 1)
                    ncopy += 2
                elif kind == "step":
                    act.wait_ge(sort_v, nv)
                    act.wait_ge(sort_copied, ncopy)
                    act.copy(other[:, 1, :], buf[:, 1, :]).then_inc(sort_copied, 1)
                    ncopy += 1
                nv += {"step": STEP_V, "flip": FLIP_V, "turn": 0}[kind]
                if kind != "flip":
                    buf, other = other, buf

            def copy_pair(dst, q, w):
                act.copy(dst[:, 2 * q:2 * q + 2, :].rearrange("p g d -> p (g d)"), bank[q][:, :]).then_inc(w, 1)

            def first_stage(i, first=False, last=False):
                for q in range(HP):
                    act.wait_ge(got_used, G * i + 2 * q + 2)
                    if not first:
                        act.wait_ge(h_done, HP * (i - 1) + q + 1)
                    copy_pair(agg, q, agg_copied)
                    v = bank[q][:, :].rearrange("p (g c f) -> p c g f", g=2, c=C)
                    act.copy(firsts_t[:, :, bass.ds(G * i + 2 * q, 2)], v[:, :, :, 0]).then_inc(agg_copied, 1)
                    act.copy(lasts_t[:, :, bass.ds(G * i + 2 * q, 2)], v[:, :, :, P - 1]).then_inc(agg_copied, 1)
                m = i + NB
                dense_copy(m, 0)
                dense_copy(m, 1)
                for q in range(HP):
                    if q == 0:
                        dense_apply(m - 1, 1, 1)
                    elif q == 1:
                        dense_apply(m, 0, 1)
                    elif q == 2:
                        dense_copy(m, 2)
                        dense_copy(m, 3)
                    act.wait_ge(var_done, HP * i + q + 1)
                    act.activation(rstd[:, 2 * q:2 * q + 2], mv[:, 2 * q:2 * q + 2, 1], ACT.Sqrt, bias=eps[:, :]).then_inc(std_done, 1)
                for q in range(HP):
                    act.wait_ge(turned, HP * i + q + 1)
                    if not first:
                        act.wait_ge(x1t_out[q], 16 * i)
                    copy_pair(x1t, q, x1t_copied)
                dense_root(m, 1, 0)
                for q in range(HP):
                    act.wait_ge(r_done, HP * i + q + 1)
                    if not first:
                        act.wait_ge(r_out[q], 16 * i)
                    copy_pair(res, q, r_copied)
                    if q == 0 and not last:
                        dense_root(m + 1, 0, 0)
                    elif q == 1:
                        dense_apply(m, 1, 0)
                if not last:
                    dense_apply(m + 1, 0, 0)
                dense_root(m, 1, 1)
                if not last:
                    dense_root(m + 1, 0, 1)

            def rows(s, i, q):
                gb = s * NB + i
                act.wait_ge(got_used, G * gb + 2 * q + 2)
                if s < 3 or (isinstance(i, int) and i == 0):
                    act.wait_ge(r_out[q], 16 * gb)
                else:
                    act.wait_ge(y_done, HP * (i - 1) + q + 1)
                    act.wait_ge(edge_out, 32 * i)
                copy_pair(res, q, r_copied)

            def root(q, i):
                act.wait_ge(var_done, HP * NB + HP * i + q + 1)
                act.activation(rstd[:, 2 * q:2 * q + 2], mv[:, 2 * q:2 * q + 2, 1], ACT.Sqrt, bias=eps[:, :]).then_inc(std_done, 1)

            def dense_root(m, h, u):
                act.wait_ge(dvar[h], DU * m + u + 1)
                act.activation(drstd[:, u, h, :], dmv[:, u, h, :, 1], ACT.Sqrt, bias=eps[:, :]).then_inc(dstd[h], 1)

            def dense_apply(m, h, u, odd=False, alone=False):
                act.wait_ge(dscale[h], DU * m + u + 1)
                before = 2 if alone else 1
                if h == 0 and not (isinstance(m, int) and m < before):
                    act.wait_ge(dadded, 4 * (m - before) + 2 * u + 2)
                t, t_out, done = ((dx, normed(odd, alone), dx1_done), (dy, dy, dy_done))[h]
                for g in range(4):
                    ins = act.activation(t_out[:, u, g, :], t[:, u, g, :], ACT.Identity,
                                         bias=dshift[:, u, h, g:g + 1], scale=drstd[:, u, h, g:g + 1])
                    if g == 3 or (h == 0 and g == 1):
                        ins.then_inc(done, 1)

            def dense_copy(m, n, alone=False):
                u, v = n // 2, n % 2
                act.wait_ge(dturned, 4 * m + n + 1)
                act.copy(dx1t[:, u, 2 * v:2 * v + 2, :].rearrange("p g d -> p (g d)"), 
                         bank[n if alone else (5, 6, 7, 4)[n]][:, :]).then_inc(dx1t_copied, 1)

            def seam_first_stage():
                act.wait_ge(sm_rows, 1)
                for c in range(C):
                    act.copy(seam_last[0:PT, :, c * P:(c + 1) * P],
                             bank[c][0:PT, :].rearrange("p (a f) -> p a f", a=A)).then_inc(sm_rows_c, 1)
                v = bank[5][0:PT, :].rearrange("p (a f) -> p a f", a=A)
                act.copy(seam_cnt[0:PT, 0, :], v[:, :, 0]).then_inc(sm_rows_c, 1)
                act.copy(seam_cnt[0:PT, 1, :], v[:, :, P - 1]).then_inc(sm_rows_c, 1)
                seam_root(0)
                act.wait_ge(sm_turned, 1)
                for h in range(2):
                    act.copy(seam_x1t[:, 2 * h:2 * h + 2, :, :].rearrange("p a c f -> p (a c f)"),
                             bank[2 + h][:, 0:2 * C * PT]).then_inc(sm_x1t, 1)
                act.wait_ge(sm_r, 1)
                act.copy(seam_res[0:PT, 0:2, :].rearrange("p a d -> p (a d)"), bank[0][0:PT, :])
                act.copy(seam_res[0:PT, 2:4, :].rearrange("p a d -> p (a d)"), bank[1][0:PT, :]).then_inc(sm_res, 1)

            def seam_root(n):
                act.wait_ge(sm_var, n + 1)
                act.activation(seam_rstd[0:PT, :], seam_mv[0:PT, :, 1], ACT.Sqrt, bias=eps[0:PT, :]).then_inc(sm_std, 1)

            def dense_only(k, odd, first=False, last=False):
                for u in range(DU):
                    if not first:
                        dense_root(k - 1, 1, u)
                    dense_root(k + 1, 0, u)
                    if not first:
                        dense_apply(k - 1, 1, u)
                    if not (last and u == 1):
                        dense_apply(k + 1, 0, u, not odd, alone=True)
                    if not last:
                        for n in (2 * u, 2 * u + 1):
                            dense_copy(k + 1, n, alone=True)

            for u in range(DU):
                dense_root(0, 0, u)
                dense_apply(0, 0, u, False, alone=True)
            for n in range(4):
                dense_copy(0, n, alone=True)
            dense_only(0, False, first=True)
            dense_only(1, True)
            with act.Fori(2, NB - 1, 2) as i:
                dense_only(i, False)
                dense_only(i + 1, True)
            dense_only(NB - 1, False, last=True)
            dense_root(NB - 1, 1, 0)
            dense_apply(NB - 1, 1, 0)
            dense_root(NB - 1, 1, 1)
            first_stage(0, first=True)
            with act.Fori(1, NB - 1) as i:
                first_stage(i)
            first_stage(NB - 1, last=True)
            dense_apply(2 * NB - 1, 1, 1)
            seam_first_stage()

            def later_stage(s, i):
                for q in range(HP):
                    rows(s, i, q)
                    if s == 3 and q > 0:
                        root(q - 1, i)
                if s == 3:
                    root(HP - 1, i)

            for s in (1, 2, 3):
                later_stage(s, 0)
                with act.Fori(1, NB) as i:
                    later_stage(s, i)
            seam_root(1)

        @block.vector
        def _(ve):
            HP = G // 2
            ve.memset(sign_row[:, :, :], 1.0).then_inc(facts_v, 1)
            ve.memset(sort_a[:, 0, :], float((N + 1) * PH - 1))
            ve.memset(sort_a[:, 1, :], float(PL * 2 * E - 1) - OFF).then_inc(facts_v, 1)
            ve.memset(kbefore[0:1, 0:P], -1.0).then_inc(guard_set, 1)
            ve.wait_ge(facts_v, 2)
            for n in range(LOGN - LOGF):
                v = sign_row[:, n, :].rearrange("p (b h j) -> p b h j", h=2, j=1 << n)
                ins = ve.memset(v[:, :, 1, :], -1.0)
            ins.then_inc(signs_set, 1)
            ve.memset(got[:, :, :], 0.0)
            ve.memset(own[:, :, :], 0.0)
            ve.memset(start_now[:, :, :], 0)
            ve.memset(seam_own[:, :, :], 0.0).then_inc(cleared, 1)
            ve.memset(index[:, :, :], int(SKIP)).then_inc(facts_v, 1)
            ve.memset(zeros[:, :], 0.0)
            ve.memset(carry_b[:, 0:1], 0.0)
            ve.wait_ge(edges_in, 64)
            sv = Steps(ve, sort_v)
            node, partner = edge_i[0:EP, 0, 0:2 * EF], edge_i[0:EP, 1, 0:2 * EF]
            q, r, up = (t[0:EP, 0:2 * EF] for t in (quotient, remainder, above))
            sv.did(ve.tensor_scalar(q, partner, 0.5, 1.0 / PL, ALU.add, ALU.mult))
            sv.settle()
            sv.did(ve.scalar_tensor_tensor(r, q, float(-PL), partner, ALU.mult, ALU.add))
            sv.settle()
            sv.did(ve.tensor_scalar(up, r, 0.0, None, ALU.is_lt))
            sv.settle()
            sv.did(ve.scalar_tensor_tensor(r, up, float(PL), r, ALU.mult, ALU.add))
            sv.settle()
            sv.did(ve.tensor_tensor(up, q, up, ALU.subtract))
            sv.settle()
            sv.did(ve.scalar_tensor_tensor(sort_a[0:EP, 0, 0:2 * EF], node, float(PH), up, ALU.mult, ALU.add))
            ve.wait_ge(place_set, 2)
            sv.settle()
            sv.did(ve.tensor_scalar(up, edge_place[0:EP, :], -OFF, None, ALU.add))
            sv.settle()
            sv.did(ve.scalar_tensor_tensor(sort_a[0:EP, 1, 0:2 * EF], r, float(2 * E), up, ALU.mult, ALU.add))
            sv.did(ve.tensor_copy(place[:, :], place_i[:, :]))
            ve.wait_ge(signs_copied, 2)
            ncopy, nstep, buf, other = 0, 0, sort_a, sort_b
            keys_at = sv.n
            for kind, arg in network():
                if kind != "turn":
                    ve.wait_ge(sort_v, keys_at)
                if kind == "turn":
                    ncopy += 2
                elif kind == "flip":
                    ve.wait_ge(sort_copied, ncopy)
                    if arg < LOGF:
                        v = buf[:, 0, :].rearrange("p (b h j) -> p b h j", h=2, j=1 << arg)[:, :, 1, :]
                        sv.did(ve.tensor_scalar(v, v, -1.0, None, ALU.mult))
                    else:
                        sv.did(ve.tensor_scalar(buf[:, 0, :], buf[:, 0, :], signs[:, arg - LOGF:arg - LOGF + 1], None, ALU.mult))
                    keys_at = sv.n
                else:
                    ve.wait_ge(sort_copied, ncopy)
                    lo, hi = (buf[:, :, :].rearrange("p w (b h j) -> p w b h j", h=2, j=arg)[:, :, :, h, :] for h in range(2))
                    olo, ohi = (other[:, :, :].rearrange("p w (b h j) -> p w b h j", h=2, j=arg)[:, :, :, h, :] for h in range(2))
                    m = swap[:, nstep % 2, :].rearrange("p (b j) -> p b j", j=arg)
                    nstep += 1
                    sv.did(ve.tensor_tensor(m, lo[:, 0], hi[:, 0], ALU.is_gt))
                    sv.did(ve.tensor_tensor(olo[:, 0], lo[:, 0], hi[:, 0], ALU.min))
                    sv.did(ve.tensor_tensor(ohi[:, 0], lo[:, 0], hi[:, 0], ALU.max))
                    keys_at = sv.n
                    ncopy += 1
                    ve.wait_ge(sort_copied, ncopy)
                    ve.wait_ge(sort_v, sv.n - 2)
                    sv.did(ve.copy_predicated(olo[:, 1], m, hi[:, 1]))
                    sv.did(ve.copy_predicated(ohi[:, 1], m, lo[:, 1]))
                if kind != "flip":
                    buf, other = other, buf
            assert sv.n == SORT_V and buf is sort_out

            fv = Steps(ve, facts_v, 3)
            key, pay = (sort_out[:, w, :] for w in range(2))
            sv.settle()

            def divide(value, guess, unit, start, digit):
                fv.did(ve.tensor_scalar(quotient[:, :], value, guess, 1.0 / unit, ALU.add, ALU.mult))
                fv.settle()
                if start:
                    fv.did(ve.tensor_scalar(remainder[:, :], quotient[:, :], -unit, start, ALU.mult, ALU.add))
                    fv.settle()
                    fv.did(ve.tensor_tensor(value, remainder[:, :], value, ALU.add))
                else:
                    fv.did(ve.scalar_tensor_tensor(value, quotient[:, :], -unit, value, ALU.mult, ALU.add))
                fv.settle()
                fv.did(ve.tensor_scalar(above[:, :], value, 0.0, None, ALU.is_lt))
                fv.settle()
                fv.did(ve.scalar_tensor_tensor(above[:, :], value, unit, above[:, :], ALU.is_ge, ALU.subtract))
                fv.settle()
                fv.did(ve.scalar_tensor_tensor(value, above[:, :], -unit, value, ALU.mult, ALU.add))
                return ve.tensor_tensor(digit, quotient[:, :], above[:, :], ALU.add)

            fv.did(ve.tensor_copy(partner_x[:, :], key))
            fv.settle()
            divide(partner_x[:, :], 0.0, float(PH), 0.0, key).then_inc(keys_done, 1)
            ve.wait_ge(keys_done, 1)
            fv.did(divide(pay, OFF, float(2 * E), OFF, own_id_x[:, :]))
            fv.settle()
            fv.did(ve.scalar_tensor_tensor(partner_x[:, :], partner_x[:, :], float(PL), own_id_x[:, :], ALU.mult, ALU.add))
            fv.did(ve.tensor_scalar(flag_x[:, :], pay, float(E), None, ALU.is_lt))
            fv.did(ve.tensor_scalar(above[:, :], key, float(N), None, ALU.is_ge))
            fv.settle()
            fv.did(ve.scalar_tensor_tensor(own_id_x[:, :], above[:, :], SKIP, pay, ALU.mult, ALU.add))
            fv.settle()
            fv.did(ve.scalar_tensor_tensor(pay, flag_x[:, :], float(2 * E), own_id_x[:, :], ALU.mult, ALU.add))
            fv.settle()
            fv.did(ve.tensor_scalar(pay, pay, float(-E), None, ALU.add))
            ve.wait_ge(keys_back, 32)
            fv.did(ve.tensor_tensor(begin_x[:, :], key, kbefore[:, :], ALU.not_equal))
            for a in range(A):
                sl = slice(a * P, (a + 1) * P)
                fv.did(ve.tensor_scalar(whole_x[:, sl], key[:, sl], kafter[:, a:a + 1], None, ALU.not_equal))
            fv.settle()
            fv.did(ve.tensor_tensor(whole_x[:, :], whole_x[:, :], begin_x[:, :], ALU.mult))
            fv.did(ve.tensor_copy(above[:, :], begin_x[:, :]))
            fv.did(ve.tensor_tensor(start_x[:, :], begin_x[:, :], place[:, :], ALU.mult))
            fv.settle()
            fv.did(ve.tensor_tensor_scan(begin_x[:, :], zeros[:, :], start_x[:, :], 0.0, ALU.add, ALU.max))
            fv.settle()
            ve.tensor_scalar(carry_a[:, :], zeros[:, 0:P], begin_x[:, FREE - 1:FREE], None, ALU.add).then_inc(carry_v, 1)
            first_x, upto = above, remainder
            ends, before = sort_spare[:, 0, :], sort_spare[:, 1, :]
            fv.did(ve.memset(first_x[:, 0:FREE:P], 1.0))
            fv.did(ve.tensor_tensor_scan(upto[:, :], zeros[:, :], flag_x[:, :], 0.0, ALU.add, ALU.add))
            fv.settle()
            fv.did(ve.tensor_tensor(ends, upto[:, :], flag_x[:, :], ALU.subtract))
            fv.settle()
            fv.did(ve.tensor_tensor(ends, ends, first_x[:, :], ALU.mult))
            fv.settle()
            fv.did(ve.tensor_tensor_scan(before, zeros[:, :], ends, 0.0, ALU.add, ALU.max))
            fv.settle()
            fv.did(ve.scalar_tensor_tensor(ends[:, 0:FREE - 1], first_x[:, 1:FREE], -SKIP, upto[:, 0:FREE - 1], ALU.mult, ALU.add))
            fv.did(ve.tensor_scalar(ends[:, FREE - 1:FREE], upto[:, FREE - 1:FREE], -SKIP, None, ALU.add))
            in_tiles = ends.rearrange("p (a s) -> p a s", s=P)
            for n in range(P.bit_length() - 1):
                d = 1 << n
                fv.settle()
                fv.did(ve.tensor_tensor(in_tiles[:, :, 0:P - d], in_tiles[:, :, 0:P - d], in_tiles[:, :, d:P], ALU.min))
            fv.settle()
            fv.did(ve.scalar_tensor_tensor(before, ends, SKIP, before, ALU.add, ALU.subtract))
            fv.settle()
            fv.did(ve.scalar_tensor_tensor(before, whole_x[:, :], WHOLE, before, ALU.mult, ALU.add))
            fv.settle()
            ve.wait_ge(carry_turned, 1)
            ve.tensor_tensor_scan(carry_b[:, 1:P + 1], zeros[:, 0:P], bank[0][:, 0:P], 0.0, ALU.add, ALU.max).then_inc(carry_v, 1)
            ve.wait_ge(carry_turned, 2)
            fv.did(ve.tensor_copy(carry_a[:, 0:1], bank[1][:, 0:1]))
            fv.settle()
            fv.did(ve.tensor_scalar(start_x[:, :], begin_x[:, :], carry_a[:, 0:1], None, ALU.max))
            fv.did(ve.tensor_scalar(dest_x[:, :], key, SKIP, None, ALU.add))
            fv.settle()
            ve.scalar_tensor_tensor(dest_x[:, :], whole_x[:, :], -SKIP, dest_x[:, :], ALU.mult, ALU.add
                                    ).then_inc(facts_done, 1)
            kf, kl = key[:, 0:FREE:P], key[:, P - 1:FREE:P]
            fv.did(ve.tensor_tensor(seam_a[:, :], kf, kprev, ALU.is_equal))
            fv.did(ve.tensor_tensor(seam_b[:, :], kf, kl, ALU.is_equal))
            fv.did(ve.tensor_tensor(seam_d[:, :], kf, kafter[:, :], ALU.is_equal))
            fv.settle()
            fv.did(ve.tensor_tensor(seam_b[:, :], seam_b[:, :], seam_d[:, :], ALU.mult))
            fv.settle()
            fv.did(ve.tensor_scalar(seam_b[:, :], seam_b[:, :], -1.0, 1.0, ALU.mult, ALU.add))
            fv.settle()
            fv.did(ve.tensor_tensor(seam_a[:, :], seam_a[:, :], seam_b[:, :], ALU.mult))
            fv.did(ve.tensor_scalar(seam_d[:, :], kf, SKIP, None, ALU.add))
            fv.settle()
            fv.did(ve.scalar_tensor_tensor(seam_dest[:, 1, :], seam_a[:, :], -SKIP, seam_d[:, :], ALU.mult, ALU.add))
            fv.settle()
            fv.did(ve.tensor_scalar(seam_d[:, :], start_x[:, 0:FREE:P], SKIP, None, ALU.add))
            fv.settle()
            fv.did(ve.scalar_tensor_tensor(seam_dest[:, 0, :], seam_a[:, :], -SKIP, seam_d[:, :], ALU.mult, ALU.add))
            fv.did(ve.tensor_copy(seam_node[:, :], kf))
            ve.wait_ge(first_back, 16)
            for a in range(A):
                ins = ve.tensor_scalar(seam_eq[0:PT, a, :, :], first_bc[0:PT, :, :], key[0:PT, a * P + P - 1:a * P + P], None, ALU.is_equal)
            ins.then_inc(seam_facts, 1)
            ve.wait_ge(facts_turned, 1)

            def by_tile(n):
                return bank[n][:, :].rearrange("s (a p) -> s p a", a=A)[:, 0:PT, :]

            def tiles(t):
                return t.rearrange("s (p a) -> s p a", a=A)

            ve.tensor_copy(tiles(kcol[:, :]), by_tile(0))
            ve.tensor_copy(tiles(flagcol[:, :]), by_tile(1))
            fv.did(ve.tensor_scalar(tiles(wholecol[:, :]), by_tile(2), WHOLE, None, ALU.is_ge))
            fv.settle()
            ve.scalar_tensor_tensor(tiles(count[:, :]), tiles(wholecol[:, :]), -WHOLE, by_tile(2), ALU.mult, ALU.add)
            for field, n in ((0, 6), (1, 7), (2, 3), (3, 0), (4, 5)):
                ve.tensor_copy(tiles(index[:, 0:NT, field]), by_tile(n))
            ve.tensor_copy(tiles(index[:, G:NT + G, 6]), by_tile(4)).then_inc(index_done, 1)
            ve.wait_ge(index_done, 1)

            def equal(gb, i, flagged, js=range(G)):
                for j in js:
                    if j == js[0]:
                        ve.wait_ge(key_in, 16 * gb + 16)
                    if not (isinstance(gb, int) and gb == 0):
                        ve.wait_ge(got_used, G * (gb - 1) + j + 1)
                    if flagged:
                        ve.tensor_scalar(eq[:, j, :], key_bc[:, j, :], kcol[:, bass.ds(G * i + j, 1)],
                                         flagcol[:, bass.ds(G * i + j, 1)], ALU.is_equal, ALU.mult).then_inc(eq_done, 1)
                    else:
                        ve.tensor_scalar(eq[:, j, :], key_bc[:, j, :], kcol[:, bass.ds(G * i + j, 1)],
                                         None, ALU.is_equal).then_inc(eq_done, 1)

            def plain_wait():
                ve.sem_inc(passed_v, 1)

            def dense_stats(m, h, u, odd=False, alone=False):
                if h == 0:
                    ve.wait_ge(dx_in[u], 16 * m + 16)
                else:
                    if not (isinstance(m, int) and m == 0):
                        ve.wait_ge(dy_out[u], 16 * m)
                    for v in range(2):
                        ve.wait_ge(dmul, 4 * m + 2 * u + v + 1)
                        n = 2 * u + v
                        ve.tensor_tensor(dy[:, u, 2 * v:2 * v + 2, :].rearrange("p g d -> p (g d)"),
                                         normed(odd, alone)[:, u, 2 * v:2 * v + 2, :].rearrange("p g d -> p (g d)"),
                                         bank[(5, 6, 7, 4)[n]][:, :], ALU.add).then_inc(dadded, 1)
                    ve.wait_ge(dadded, 4 * m + 2 * u + 2)
                t = (dx, dy)[h]
                for g in range(4):
                    ins = ve.bn_stats(dstat[:, u, h, g, :], t[:, u, g, :])
                ins.then_inc(dense_v[h][u], 1)
                ve.wait_ge(dense_v[h][u], 2 * m + 1)
                plain_wait()
                for g in range(4):
                    ins = ve.bn_aggr(dmv[:, u, h, g, :], dstat[:, u, h, g, :])
                ins.then_inc(dvar[h], 1)

            def dense_scales(m, h, u):
                ve.wait_ge(dstd[h], DU * m + u + 1)
                ve.reciprocal(drstd[:, u, h, :], drstd[:, u, h, :]).then_inc(dense_v[h][u], 1)
                ve.wait_ge(dense_v[h][u], 2 * m + 2)
                ve.scalar_tensor_tensor(dshift[:, u, h, :], dmv[:, u, h, :, 0], -1.0, drstd[:, u, h, :],
                                        ALU.mult, ALU.mult).then_inc(dscale[h], 1)

            def dense_only(k, odd, first=False):
                for u in range(DU):
                    if not first:
                        dense_stats(k - 1, 1, u, not odd, alone=True)
                    dense_stats(k + 1, 0, u)
                    if not first:
                        dense_scales(k - 1, 1, u)
                    dense_scales(k + 1, 0, u)

            for u in range(DU):
                dense_stats(0, 0, u)
                dense_scales(0, 0, u)
            dense_only(0, False, first=True)
            dense_only(1, True)
            with ve.Fori(2, NB - 1, 2) as i:
                dense_only(i, False)
                dense_only(i + 1, True)
            dense_only(NB - 1, False)
            for u in range(DU):
                dense_stats(NB - 1, 1, u, NB % 2 == 0, alone=True)
                dense_scales(NB - 1, 1, u)

            LN0 = G + HP * (1 + 2 + 1 + 1 + 1)

            def first_stage(i, first=False, last=False):
                st = Steps(ve, ln0_v, LN0 * i)
                for j in range(G):
                    ve.wait_ge(own_in[j], 16 * i + 16)
                    st.did(ve.scalar_tensor_tensor(own[:, j, :], bias_bc[:, :], count[:, bass.ds(G * i + j, 1)],
                                                   own[:, j, :], ALU.mult, ALU.add))
                def stats(q):
                    st.settle()
                    ve.wait_ge(h_done, HP * i + q + 1)
                    if not first:
                        ve.wait_ge(turned, HP * (i - 1) + q + 1)
                    pair = slice(2 * q, 2 * q + 2)
                    st.did(ve.tensor_tensor(x1[:, pair, :].rearrange("p g d -> p (g d)"),
                                            own[:, pair, :].rearrange("p g d -> p (g d)"), bank[q][:, :], ALU.add))
                    st.settle()
                    for j in (2 * q, 2 * q + 1):
                        st.did(ve.bn_stats(stat[:, j, :], x1[:, j, :]))
                    st.settle()
                    plain_wait()
                    for j in (2 * q, 2 * q + 1):
                        ins = ve.bn_aggr(mv[:, j, :], stat[:, j, :])
                    ins.then_inc(var_done, 1)

                def norm(q):
                    ve.wait_ge(std_done, HP * i + q + 1)
                    pair = slice(2 * q, 2 * q + 2)
                    st.did(ve.reciprocal(rstd[:, pair], rstd[:, pair]))
                    st.settle()
                    st.did(ve.tensor_tensor(rstd[:, pair], rstd[:, pair], wholecol[:, bass.ds(G * i + 2 * q, 2)], ALU.mult))
                    st.settle()
                    for j in (2 * q, 2 * q + 1):
                        ins = ve.tensor_scalar(x1[:, j, :], x1[:, j, :], mv[:, j, 0:1], rstd[:, j:j + 1], ALU.subtract, ALU.mult)
                        if j % 2 == 0:
                            st.did(ins)
                    ins.then_inc(x1_done, 1)

                stats(0)
                for q in range(1, HP):
                    stats(q)
                    norm(q - 1)
                norm(HP - 1)
                m = i + NB
                for u in range(DU):
                    dense_stats(m, 1, u)
                    if u == 0:
                        if last:
                            equal(NB, 0, False)
                        else:
                            equal(i + 1, i + 1, True)
                    if not last:
                        dense_stats(m + 1, 0, u)
                    dense_scales(m, 1, u)
                    if not last:
                        dense_scales(m + 1, 0, u)
                return st

            equal(0, 0, True)
            st = first_stage(0, True)
            assert st.n == LN0, st.n
            with ve.Fori(1, NB - 1) as i:
                first_stage(i)
            first_stage(NB - 1, last=True)

            sm = Steps(ve, sm_v)

            def seam_norm(t_out, n):
                sm.settle()
                for a in range(A):
                    sm.did(ve.bn_stats(seam_stat[0:PT, a, :], t_out[0:PT, a, :]))
                sm.settle()
                for a in range(A):
                    ins = ve.bn_aggr(seam_mv[0:PT, a, :], seam_stat[0:PT, a, :])
                ins.then_inc(sm_var, 1)
                ve.wait_ge(sm_std, n + 1)
                sm.did(ve.reciprocal(seam_rstd[0:PT, :], seam_rstd[0:PT, :]))
                sm.settle()
                for a in range(A):
                    ins = ve.tensor_scalar(t_out[0:PT, a, :], t_out[0:PT, a, :], seam_mv[0:PT, a, 0:1],
                                           seam_rstd[0:PT, a:a + 1], ALU.subtract, ALU.mult)
                return ins

            ve.wait_ge(sm_sum, 1)
            for c in range(C):
                ve.tensor_tensor(seam_agg[:, c, :, :], bank[2 + c][:, 0:A * PT].rearrange("p (a q) -> p a q", a=A),
                                 firsts_t[:, c, :].rearrange("p (q a) -> p a q", a=A), ALU.add).then_inc(sm_agg, 1)
            ve.tensor_tensor(seam_cn[0:PT, :], bank[4][0:PT, 0:A], seam_cnt[0:PT, 0, :], ALU.add).then_inc(sm_agg, 1)
            ve.wait_ge(sm_agg, C + 1)
            ve.wait_ge(sm_own, 16 * A)
            for a in range(A):
                sm.did(ve.scalar_tensor_tensor(seam_own[0:PT, a, :], bias_bc[0:PT, :], seam_cn[0:PT, a:a + 1],
                                               seam_own[0:PT, a, :], ALU.mult, ALU.add))
            sm.settle()
            ve.wait_ge(sm_h, 1)
            for h in range(2):
                sm.did(ve.tensor_tensor(seam_x1[0:PT, 2 * h:2 * h + 2, :].rearrange("p a d -> p (a d)"),
                                        seam_own[0:PT, 2 * h:2 * h + 2, :].rearrange("p a d -> p (a d)"), bank[h][0:PT, :], ALU.add))
            seam_norm(seam_x1, 0).then_inc(sm_x1, 1)

            def seam(s):
                ve.wait_ge(sm_r, s + 1)
                ve.wait_ge(sm_in, 32 * s)
                ve.wait_ge(sm_out, 16 * A * s)
                for h in range(2):
                    ins = ve.tensor_tensor(seam_res[0:PT, 2 * h:2 * h + 2, :].rearrange("p a d -> p (a d)"),
                                           seam_first[0:PT, 2 * h:2 * h + 2, :].rearrange("p a d -> p (a d)"), bank[h][0:PT, :], ALU.add)
                    if s == 3:
                        sm.did(ins)
                if s == 3:
                    sm.settle()
                    for h in range(2):
                        sm.did(ve.tensor_tensor(seam_res[0:PT, 2 * h:2 * h + 2, :], seam_res[0:PT, 2 * h:2 * h + 2, :],
                                                seam_x1[0:PT, 2 * h:2 * h + 2, :], ALU.add))
                    ins = seam_norm(seam_res, 1)
                ins.then_inc(sm_res, 1)

            for s in (1, 2):
                with ve.Fori(0, NB - 1) as i:
                    equal(s * NB + 1 + i, i + 1, False)
                equal((s + 1) * NB, 0, False)
                seam(s)

            LN3 = G + HP
            def last_stage(i, last=False):
                st = Steps(ve, ln3_v, LN3 * i)

                def stats(q):
                    ve.wait_ge(r_copied, HP * (3 * NB + i) + q + 1)
                    for j in (2 * q, 2 * q + 1):
                        st.did(ve.bn_stats(stat[:, j, :], res[:, j, :]))
                    st.settle()
                    plain_wait()
                    for j in (2 * q, 2 * q + 1):
                        ins = ve.bn_aggr(mv[:, j, :], stat[:, j, :])
                    ins.then_inc(var_done, 1)

                def norm(q):
                    ve.wait_ge(std_done, HP * (NB + i) + q + 1)
                    pair = slice(2 * q, 2 * q + 2)
                    st.did(ve.reciprocal(rstd[:, pair], rstd[:, pair]))
                    st.settle()
                    for j in (2 * q, 2 * q + 1):
                        if not (isinstance(i, int) and i == 0):
                            ve.wait_ge(scattered[j], 16 * i)
                        ins = ve.tensor_scalar(x1[:, j, :], res[:, j, :], mv[:, j, 0:1], rstd[:, j:j + 1], ALU.subtract, ALU.mult)
                    ins.then_inc(y_done, 1)

                def eq_pair(q):
                    if not last:
                        equal(3 * NB + i + 1, i + 1, False, range(2 * q, 2 * q + 2))

                stats(0)
                for q in range(1, HP):
                    eq_pair(q - 1)
                    stats(q)
                    norm(q - 1)
                eq_pair(HP - 1)
                norm(HP - 1)
                assert st.n == LN3

            last_stage(0)
            with ve.Fori(1, NB - 1) as i:
                last_stage(i)
            last_stage(NB - 1, last=True)
            seam(3)


_INS = ["x", "src", "dst", "L0_gnn_W", "L0_gnn_b", "L1_gnn_weights"]
_OUTS = [((100000, 256), "float32")]


def kernel(**inputs):
    import numpy as _np
    import concourse.bacc as _bacc
    from concourse import mybir as _mybir
    from concourse.bass_utils import run_bass_kernel_spmd as _run

    nc = _bacc.Bacc("TRN2", target_bir_lowering=False, num_devices=1)
    arrays, args = {}, []
    for name in _INS:
        a = _np.ascontiguousarray(inputs[name])
        arrays[f"in_{name}_dram"] = a
        args.append(nc.dram_tensor(f"in_{name}_dram", a.shape, _mybir.dt.from_np(a.dtype), kind="ExternalInput").ap())
    for i, (shape, dtype) in enumerate(_OUTS):
        dt = _mybir.dt.from_np(_np.dtype(dtype))
        args.append(nc.dram_tensor(f"out_{i}_dram", shape, dt, kind="ExternalOutput").ap())
    gnn_kernel(nc, *args)
    r = _run(nc, [arrays], core_ids=[0])
    return r.results[0]["out_0_dram"]
```
